# Optimizing a Trainium2 kernel written in Bass

```python
import numpy as np
import jax
import jax.numpy as jnp

def _softmax(x, axis=-1):
    return jax.nn.softmax(x, axis=axis)

def _gelu(x):
    return jax.nn.gelu(x, approximate=True)

def _silu(x):
    return jax.nn.silu(x)

def _sigmoid(x):
    return jax.nn.sigmoid(x)

def _layernorm(x, axis=-1, eps=1e-05):
    m = jnp.mean(x, axis=axis, keepdims=True)
    v = jnp.var(x, axis=axis, keepdims=True)
    return (x - m) / jnp.sqrt(v + eps)

def _scatter_add(tgt, idx, src, axis=0):
    return tgt.at[idx].add(src)

def _segment_sum(src, seg, n):
    return jax.ops.segment_sum(src, seg, n)
kernel_name = 'mk_flamingo_gated_d1_seqx_r4_eae122'

def setup_inputs(seed: int=0):
    np.random.seed(seed)
    _w = jnp.asarray

    def _rec_inputs():
        import jax
        import jax.numpy as jnp
        _rk = jax.random.key(seed)
        x = -0.000125 + 0.9999 * jax.random.normal(jax.random.fold_in(_rk, 1), (16, 100, 512), jnp.float32)
        _lenS = 100 - jax.random.randint(jax.random.fold_in(_rk, 7), (16,), 0, max(1, 100 // 4) + 1, jnp.int32)
        _lenS2 = 361 - jax.random.randint(jax.random.fold_in(_rk, 8), (16,), 0, max(1, 361 // 4) + 1, jnp.int32)
        _ctx_2048P = jax.random.normal(jax.random.fold_in(_rk, 11), (16, 16, 512), jnp.float32)
        _ctx_2048c = jax.random.dirichlet(jax.random.fold_in(_rk, 511), 0.3 * jnp.ones((16,), jnp.float32), (16, 361))
        _ctx_2048t = jnp.einsum('bsk,bkd->bsd', _ctx_2048c, _ctx_2048P)
        _ctx_2048t = _ctx_2048t * jax.lax.rsqrt(jnp.mean(jnp.square(_ctx_2048t)) + 1e-12) * 0.953939
        ctx_2048 = -0.000514642 + 1.00011 * (_ctx_2048t + 0.3 * jax.random.normal(jax.random.fold_in(_rk, 611), (16, 361, 512), jnp.float32))
        _validS = jnp.arange(100)[None, :] < _lenS[:, None]
        _validS2 = jnp.arange(361)[None, :] < _lenS2[:, None]
        _causal = jnp.tril(jnp.ones((100, 100), dtype=bool))
        mask_BxS2_bk0 = jnp.logical_not(jnp.broadcast_to(_validS2[:, :], (16, 361)))
        _g = jax.random.normal(jax.random.fold_in(_rk, 9001), (2, 1), jnp.float32)
        _g = jnp.sign(_g) * jnp.maximum(jnp.abs(_g), 1.0) + (_g == 0) * 1.0
        g_xattn = _g[0]
        g_ffn = _g[1]
        return (x, ctx_2048, mask_BxS2_bk0, g_xattn, g_ffn)
    x, ctx_2048, mask_BxS2_bk0, g_xattn, g_ffn = _rec_inputs()

    def _L0_xattn_setup():
        import jax, jax.numpy as jnp
        import numpy as np
        H = 512
        NH = 16
        HD = H // NH
        EPS = 1e-06

        def rmsnorm(x, w, eps=EPS):
            var = jnp.mean(x * x, axis=-1, keepdims=True)
            return x * jax.lax.rsqrt(var + eps) * w
        key = jax.random.key(seed)
        ks = jax.random.split(key, 9)
        B, L, M = (4, 1024, 64)
        s = 1.0 / np.sqrt(H)
        return {'hidden_states': jax.random.normal(ks[0], (B, L, H), dtype=jnp.float32), 'memory_tokens': jax.random.normal(ks[1], (B, M, H), dtype=jnp.float32), 'memory_mask': jax.random.randint(ks[2], (B, M), 0, 2).astype(bool), 'norm_w': jnp.ones((H,), dtype=jnp.float32), 'wq': jax.random.normal(ks[3], (H, H), dtype=jnp.float32) * s, 'wk': jax.random.normal(ks[4], (H, H), dtype=jnp.float32) * s, 'wv': jax.random.normal(ks[5], (H, H), dtype=jnp.float32) * s, 'wo': jax.random.normal(ks[6], (H, H), dtype=jnp.float32) * s, 'wg': jax.random.normal(ks[7], (H, H), dtype=jnp.float32) * s}
    _L0_xattn_all = _L0_xattn_setup()
    _L0_xattn_in = {k: v for k, v in _L0_xattn_all.items() if k in ('norm_w', 'wq', 'wk', 'wv', 'wo', 'wg')}
    del _L0_xattn_all

    def _L0_ffn_setup():
        import jax, jax.numpy as jnp
        import numpy as np
        _FP4_LUT = jnp.array([0.0, 0.5, 1.0, 1.5, 2.0, 3.0, 4.0, 6.0, -0.0, -0.5, -1.0, -1.5, -2.0, -3.0, -4.0, -6.0], dtype=jnp.float32)
        GROUP_SIZE = 128
        EPS = 1e-06

        def _dequant_fp4(packed_i32, scales_f16, group_size):
            out_f, in_p = packed_i32.shape
            w = packed_i32.astype(jnp.uint32)
            shifts = jnp.arange(8, dtype=jnp.uint32) * 4
            nib = w[:, :, None] >> shifts & jnp.uint32(15)
            vals = _FP4_LUT[nib.astype(jnp.int32)].reshape(out_f, in_p * 8)
            s = scales_f16.astype(jnp.float32).T
            s_full = jnp.repeat(s, group_size, axis=1)
            return vals * s_full
        key = jax.random.key(seed)
        k1, k2, k3, k4, k5 = jax.random.split(key, 5)
        B, S, H, I = (4, 512, 512, 1408)
        x = jax.random.normal(k1, (B, S, H), dtype=jnp.float32)
        gate_up_packed = jax.random.randint(k2, (2 * I, H // 8), 0, 2147483647, dtype=jnp.int32)
        gate_up_scales = jax.random.uniform(k3, (H // GROUP_SIZE, 2 * I), dtype=jnp.float32).astype(jnp.float16)
        down_packed = jax.random.randint(k4, (H, I // 8), 0, 2147483647, dtype=jnp.int32)
        down_scales = jax.random.uniform(k5, (I // GROUP_SIZE, H), dtype=jnp.float32).astype(jnp.float16)
        return {'x': x, 'gate_up_packed': gate_up_packed, 'gate_up_scales': gate_up_scales, 'down_packed': down_packed, 'down_scales': down_scales}
    _L0_ffn_all = _L0_ffn_setup()
    _L0_ffn_in = {k: v for k, v in _L0_ffn_all.items() if k in ('gate_up_packed', 'gate_up_scales', 'down_packed', 'down_scales')}
    del _L0_ffn_all
    return {'x': x, 'ctx_2048': ctx_2048, 'mask_BxS2_bk0': mask_BxS2_bk0, 'g_xattn': g_xattn, 'g_ffn': g_ffn, 'L0_xattn_norm_w': _L0_xattn_in['norm_w'], 'L0_xattn_wq': _L0_xattn_in['wq'], 'L0_xattn_wk': _L0_xattn_in['wk'], 'L0_xattn_wv': _L0_xattn_in['wv'], 'L0_xattn_wo': _L0_xattn_in['wo'], 'L0_xattn_wg': _L0_xattn_in['wg'], 'L0_ffn_gate_up_packed': _L0_ffn_in['gate_up_packed'], 'L0_ffn_gate_up_scales': _L0_ffn_in['gate_up_scales'], 'L0_ffn_down_packed': _L0_ffn_in['down_packed'], 'L0_ffn_down_scales': _L0_ffn_in['down_scales']}

def reference(x, ctx_2048, mask_BxS2_bk0, g_xattn, g_ffn, L0_xattn_norm_w, L0_xattn_wq, L0_xattn_wk, L0_xattn_wv, L0_xattn_wo, L0_xattn_wg, L0_ffn_gate_up_packed, L0_ffn_gate_up_scales, L0_ffn_down_packed, L0_ffn_down_scales):
    import jax
    import jax.numpy as jnp

    def _L0_xattn_ref(hidden_states, memory_tokens, memory_mask, norm_w, wq, wk, wv, wo, wg):
        import jax, jax.numpy as jnp
        import numpy as np
        H = 512
        NH = 16
        HD = H // NH
        EPS = 1e-06

        def rmsnorm(x, w, eps=EPS):
            var = jnp.mean(x * x, axis=-1, keepdims=True)
            return x * jax.lax.rsqrt(var + eps) * w
        B, L, C = hidden_states.shape
        M = memory_tokens.shape[1]
        scale = HD ** (-0.5)
        x = rmsnorm(hidden_states, norm_w)
        q = (x @ wq.T).reshape(B, L, NH, HD)
        k = (memory_tokens @ wk.T).reshape(B, M, NH, HD)
        v = (memory_tokens @ wv.T).reshape(B, M, NH, HD)
        attn = jnp.einsum('blhd,bmhd->bhlm', q, k) * scale
        attn = jnp.where(memory_mask[:, None, None, :], attn, -jnp.inf)
        attn = jax.nn.softmax(attn, axis=-1)
        attn = jnp.nan_to_num(attn, nan=0.0)
        out = jnp.einsum('bhlm,bmhd->blhd', attn, v).reshape(B, L, C)
        out = out @ wo.T
        gate = jax.nn.sigmoid(x @ wg.T)
        return gate * out

    def _L0_ffn_ref(x, gate_up_packed, gate_up_scales, down_packed, down_scales):
        import jax, jax.numpy as jnp
        import numpy as np
        _FP4_LUT = jnp.array([0.0, 0.5, 1.0, 1.5, 2.0, 3.0, 4.0, 6.0, -0.0, -0.5, -1.0, -1.5, -2.0, -3.0, -4.0, -6.0], dtype=jnp.float32)
        GROUP_SIZE = 128
        EPS = 1e-06

        def _dequant_fp4(packed_i32, scales_f16, group_size):
            out_f, in_p = packed_i32.shape
            w = packed_i32.astype(jnp.uint32)
            shifts = jnp.arange(8, dtype=jnp.uint32) * 4
            nib = w[:, :, None] >> shifts & jnp.uint32(15)
            vals = _FP4_LUT[nib.astype(jnp.int32)].reshape(out_f, in_p * 8)
            s = scales_f16.astype(jnp.float32).T
            s_full = jnp.repeat(s, group_size, axis=1)
            return vals * s_full
        I = gate_up_packed.shape[0] // 2
        w_gu = _dequant_fp4(gate_up_packed, gate_up_scales, GROUP_SIZE)
        w_down = _dequant_fp4(down_packed, down_scales, GROUP_SIZE)
        gate_up = jnp.einsum('bsh,oh->bso', x, w_gu)
        gate, up = (gate_up[..., :I], gate_up[..., I:])
        h = jax.nn.silu(gate) * up
        y = jnp.einsum('bsi,hi->bsh', h, w_down)
        rms = jnp.sqrt(jnp.mean(y * y, axis=-1, keepdims=True) + EPS)
        return y / rms
    x = x + jnp.tanh(g_xattn[0]) * _L0_xattn_ref(_layernorm(x, axis=-1), ctx_2048, mask_BxS2_bk0, L0_xattn_norm_w, L0_xattn_wq, L0_xattn_wk, L0_xattn_wv, L0_xattn_wo, L0_xattn_wg)
    x = x + jnp.tanh(g_ffn[0]) * _L0_ffn_ref(_layernorm(x, axis=-1), L0_ffn_gate_up_packed, L0_ffn_gate_up_scales, L0_ffn_down_packed, L0_ffn_down_scales)
    return x

_drawn_inputs = setup_inputs


def setup_inputs(seed=0):
    import zlib

    import numpy as np

    out = dict(_drawn_inputs(seed))
    spreads = {'L0_xattn_norm_w': (1.0, 0.2)}
    factors = {}
    for name, (base, spread) in spreads.items():
        noise = np.random.default_rng([zlib.crc32(name.encode()), seed]).standard_normal(out[name].shape)
        drawn = base * np.exp(spread * noise) if base else spread * noise
        out[name] = jnp.asarray(drawn.astype(out[name].dtype))
    for name, factor in factors.items():
        out[name] = (out[name] * factor).astype(out[name].dtype)
    return out
```

```python
from contextlib import ExitStack

import numpy as np

import concourse.bass as bass
from concourse import mybir

F32, F32R, BF16, F16 = mybir.dt.float32, mybir.dt.float32r, mybir.dt.bfloat16, mybir.dt.float16
I32, I16, U8 = mybir.dt.int32, mybir.dt.int16, mybir.dt.uint8
ALU = mybir.AluOpType
ACT = mybir.ActivationFunctionType
AXIS_X = mybir.AxisListType.X

B, L, D = 16, 100, 512
M = 361
HEADS, HD = 16, 32
KT = D // 128
NB = 4
GROUPS = B // NB
GT = NB * L
HG = 4
HPG = HEADS // HG
TAIL = 96
KC = NB * TAIL
CHUNK = 128
CHUNKS = KC // CHUNK
STEPS = HG * NB
CONSTS = 5
FF = 1408
FT = FF // 128
TOKENS = B * L
TG = 320
FGROUPS = TOKENS // TG
ROWS = (128, 128, 64)
FP4_UNIT = 16384.0
MASKED = 1e30
PIECES = FT + 6
LN_EPS, RMS_EPS = 1e-5, 1e-6


def build(nc, x, ctx_tail, ctx_full, mask, mask_tail, g_xattn, g_ffn, norm_w, wq, wk, wv, wo, wg,
          gu_packed, gu_scales, dn_packed, dn_scales, identity, shifts, x1_dram, out):
    es = ExitStack()
    with es:
        def sem(name):
            return es.enter_context(nc.semaphore(name))

        def sb(stack, name, shape, dt):
            return stack.enter_context(nc.sbuf_tensor(name, shape, dt))

        ident = sb(es, "ident", [128, 128], F32)
        shift = sb(es, "shift", [128, 5], I32)
        normw = sb(es, "normw", [128, KT], F32)
        gates = sb(es, "gates", [128, 2], F32)
        tanhs = sb(es, "tanhs", [128, 2], F32)
        halfpow = sb(es, "halfpow", [128, 4], F32)
        anykeep = sb(es, "anykeep", [128, B], F32)
        coef_a = sb(es, "coef_a", [128, B], F32)
        headkeep = sb(es, "headkeep", [1, 1], I32)
        headmax = sb(es, "headmax", [1, 1], F32)
        stats = sb(es, "stats", [128, 4, 6], F32)
        mv = sb(es, "mv", [128, 4, 2], F32)
        var = sb(es, "var", [128, 4], F32)
        rstd = sb(es, "rstd", [128, 4], F32)

        phase_a, phase_b, setup_a = ExitStack(), ExitStack(), ExitStack()
        W = {}
        for name in ("wq", "wk", "wv", "wg", "wo"):
            W[name] = [sb(phase_a, f"{name}_{half}", [128, KT, D], F32R) for half in ("hi", "lo")]
        xa = sb(phase_a, "xa", [L, NB, D], F32)
        xn = sb(phase_a, "xn", [L, 2, D], F32)
        xT = [sb(phase_a, f"xT_{half}", [128, KT, GT], F32R) for half in ("hi", "lo")]
        ctx_raw = sb(phase_a, "ctx_raw", [128, KT, KC], F32)
        ctxT = [sb(phase_a, f"ctxT_{half}", [128, KT, KC], F32R) for half in ("hi", "lo")]
        kblk = [[sb(phase_a, f"kblk{s}_{half}", [128, HPG, KC], F32R) for half in ("hi", "lo")] for s in range(2)]
        vv = [sb(phase_a, f"v_{half}", [128, NB, D], F32R) for half in ("hi", "lo")]
        qT = [[sb(phase_a, f"qT{s}_{half}", [128, GT], F32R) for half in ("hi", "lo")] for s in range(2)]
        mbias = sb(phase_a, "mbias", [128, B, TAIL], BF16)
        ones = sb(phase_a, "ones", [128, L], BF16)
        nmax = sb(phase_a, "nmax", [L, 4, HPG], F32)
        rsum = sb(phase_a, "rsum", [L, 4, HPG], F32)
        rinv = sb(phase_a, "rinv", [L, 4, HPG], F32)
        raw = [sb(setup_a, f"raw{s}", [128, KT, D], F32) for s in range(2)]
        maskall = sb(setup_a, "maskall", [L, B, M], U8)
        masktail = sb(setup_a, "masktail", [1, B, TAIL], U8)
        setup_a.close()
        probs = [sb(phase_a, f"probs{s}", [L, HPG, TAIL], F32) for s in range(3)]
        pT = [[sb(phase_a, f"pT{s}_{half}", [128, HPG, L], F32R) for half in ("hi", "lo")] for s in range(2)]
        oT = [sb(phase_a, f"oT_{half}", [128, HG, GT], F32R) for half in ("hi", "lo")]
        gate = [sb(phase_a, f"gate{s}", [L, D], F32) for s in range(2)]
        gated = sb(phase_a, "gated", [L, D], F32)
        maskrow = sb(phase_a, "maskrow", [1, KC], U8)
        nmax_c = sb(phase_a, "nmax_c", [L, CHUNKS, HPG], F32)
        rsum_c = sb(phase_a, "rsum_c", [L, CHUNKS, HPG], F32)
        probs_full = xa[:, 1:NB, :].rearrange("t b d -> t (b d)").rearrange("t (h k) -> t h k", h=HPG)
        mbias_full = mbias[:, 0:NB, :].rearrange("p b k -> p (b k)")
        phase_a.close()
        wgu = [sb(phase_b, f"wgu_{half}", [128, KT, 2 * FF], F32R) for half in ("hi", "lo")]
        wdn = [sb(phase_b, f"wdn_{half}", [128, FT, D], F32R) for half in ("hi", "lo")]
        words = [sb(phase_b, f"words{s}", [128, D], I32) for s in range(2)]
        scale = [sb(phase_b, f"scale{s}", [128, D], F16) for s in range(2)]
        scale_a = sb(phase_b, "scale_a", [128, D], F16)
        scale_b = sb(phase_b, "scale_b", [128, D], F32)
        shifted = sb(phase_b, "shifted", [128, D], I32)
        fp4 = [sb(phase_b, f"fp4_{s}", [128, D], I32) for s in range(2)]
        xb = [sb(phase_b, f"xb{s}", [128, 3, D], F32) for s in range(2)]
        mn = sb(phase_b, "mn", [128, D], F32)
        mT = [sb(phase_b, f"mT_{half}", [128, KT, TG], F32R) for half in ("hi", "lo")]
        hT = [sb(phase_b, f"hT_{half}", [128, FT, TG], F32R) for half in ("hi", "lo")]
        tgate = sb(phase_b, "tgate", [128, TG], F32)
        hidden = [sb(phase_b, f"hidden{s}", [128, TG], F32) for s in range(2)]
        yo = [sb(phase_b, f"yo{s}", [128, D], F32) for s in range(2)]
        ssq = sb(phase_b, "ssq", [128, 2], F32)
        ms = sb(phase_b, "ms", [128, 2], F32)
        rrms = sb(phase_b, "rrms", [128, 2], F32)
        coef_y = sb(phase_b, "coef_y", [128, 2], F32)
        phase_b.close()

        bank = [es.enter_context(nc.psum_tensor(f"bank{i}", [128, 512], F32)) for i in range(8)]
        PJ, SC, PT, PV = bank[0:2], bank[2:4], bank[4:6], bank[6:8]

        s_const = sem("consts_loaded")
        s_mask = sem("masks_loaded")
        s_w = [sem(f"weight_loaded{s}") for s in range(2)]
        s_x = [sem(f"x_loaded{b}") for b in range(NB)]
        s_x1st = [sem(f"x1_stored{b}") for b in range(NB)]
        s_ctx = sem("ctx_loaded")
        s_split = sem("weights_split_hi")
        s_splitlo = sem("weights_split_lo")
        s_zero = sem("kblk_zeroed")
        s_setup = sem("dve_setup")
        s_tanh = sem("gates_tanh")
        s_pconst = sem("pool_consts")
        s_ctxhi, s_ctxlo = sem("ctx_hi_done"), sem("ctx_lo_done")
        s_ln = sem("ln_chain")
        s_pow = sem("rstd_ready")
        s_xn = sem("xn_ready")
        s_pj = [sem(f"projected{i}") for i in range(2)]
        s_pjfree = [sem(f"projection_read{i}") for i in range(2)]
        s_pjhi = sem("projection_hi_done")
        s_sc, s_max, s_exp, s_inv, s_norm = (sem(n) for n in ("scores_ready", "max_ready", "exp_done", "inverse_ready", "probs_normed"))
        s_pt, s_pthi, s_ptlo = sem("probsT_ready"), sem("probsT_hi"), sem("probsT_lo")
        s_pv, s_ohi, s_olo = sem("attn_ready"), sem("attn_hi"), sem("attn_lo")
        s_gate, s_gated, s_x1 = sem("gate_ready"), sem("gated_ready"), sem("x1_ready")
        f_load, f_ctxhi, f_ctx, f_bias = sem("full_loaded"), sem("full_ctx_hi"), sem("full_ctx_split"), sem("full_bias")
        f_ln, f_pow, f_xn = sem("full_ln_chain"), sem("full_rstd"), sem("full_xn_ready")
        f_pj, f_pjhi, f_pjlo = sem("full_projected"), sem("full_projection_hi"), sem("full_projection_lo")
        f_sc, f_maxc, f_max, f_exp, f_sum, f_inv, f_norm = (sem(f"full_{n}") for n in (
            "scores_ready", "max_chain", "max_ready", "exp_done", "sum_chain", "inverse_ready", "probs_normed"))
        f_pt, f_pthi, f_ptlo = sem("full_probsT_ready"), sem("full_probsT_hi"), sem("full_probsT_lo")
        f_pv, f_ohi, f_olo = sem("full_attn_ready"), sem("full_attn_hi"), sem("full_attn_lo")
        f_g, f_o, f_gate, f_gated, f_x1, f_st = (sem(f"full_{n}") for n in (
            "gate_projected", "out_projected", "gate_ready", "gated_ready", "x1_ready", "x1_stored"))
        s_apart = sem("waits_apart")
        s_pa = sem("phase_a_done")
        s_words = [sem(f"words_loaded{s}") for s in range(2)]
        s_dq = sem("dequant_chain")
        s_dec = sem("piece_decoded")
        s_whi, s_wlo = sem("ffn_weight_hi"), sem("ffn_weight_lo")
        s_xb = [sem(f"x1_loaded{s}") for s in range(2)]
        s_bln, s_bpow, s_mn = sem("ffn_ln_chain"), sem("ffn_rstd"), sem("mn_ready")
        s_mt, s_mthi, s_mtlo = sem("mT_ready"), sem("mT_hi"), sem("mT_lo")
        s_gu, s_tg, s_sg, s_h, s_hhi, s_hlo = (sem(n) for n in ("gate_up_ready", "tanh_gate", "silu_gate", "hidden_ready", "hidden_hi", "hidden_lo"))
        s_y, s_sq, s_ms, s_rr, s_cy, s_yo = (sem(n) for n in ("y_ready", "y_squared", "mean_square", "rrms_ready", "coef_ready", "out_ready"))
        s_out = [sem(f"out_stored{s}") for s in range(2)]

        block = es.enter_context(nc.Block())

        HI, LO = 0, 1

        def wait_apart(engine, semaphore, value):
            engine.wait_ge(semaphore, value)
            engine.sem_inc(s_apart, 1)

        def probs_at(i):
            return probs[i % 3]

        def piece_loads(n):
            return 4 if n < FT else (5 if n - FT < 5 else 2)

        PASSES = ((HI, HI), (HI, LO), (LO, HI))

        def product(out_ap, lhs, rhs, tiles, first=True):
            last = None
            for t in range(tiles):
                for p, (a, b) in enumerate(PASSES):
                    last = nc.tensor.matmul(out_ap, lhs(a, t), rhs(b, t), start=first and t == 0 and p == 0,
                                            stop=t == tiles - 1 and p == 2)
            return last

        JOBS = ([f"V{b}" for b in range(NB)] + ["K0"] + [f"X{b}" for b in range(NB)] + ["Q0"]
                + [f"{k}{hg}" for hg in range(1, HG) for k in "KQ"] + [f"{k}{b}" for b in range(NB) for k in "GO"])
        JOB = {name: n for n, name in enumerate(JOBS)}
        PER_BANK = len(JOBS) // 2
        HI_JOBS = [n for n in JOBS if n[0] in "VKXQ"]

        def job_bank(name):
            return JOB[name] % 2

        def job_count(g, name):
            return g * PER_BANK + JOB[name] // 2 + 1

        def hi_count(g, name):
            return g * len(HI_JOBS) + HI_JOBS.index(name) + 1

        def wants_full(engine):
            engine.wait_ge(s_setup, 6)
            return engine.value_load(headkeep[0:1, 0:1], min_val=0, max_val=1)

        FULL_JOBS = [f"V{c}" for c in range(CHUNKS)] + ["X"] + [f"{k}{hg}" for hg in range(HG) for k in "KQ"]

        def full_count(b, name):
            return len(FULL_JOBS) * b + FULL_JOBS.index(name) + 1

        FJ, FSC, FPT, FPV, FO = bank[0], bank[2:5], bank[5], bank[6], bank[7]

        @block.sync
        def _(sp):
            sp.dma_start(ctx_raw[:, :, :], ctx_tail[0]).then_inc(s_ctx, 16)
            for n, w in enumerate((wv, wk, wq, wg, wo)):
                if n >= 2:
                    sp.wait_ge(s_splitlo, n - 1)
                sp.dma_start(raw[n % 2][:, :, :], w.rearrange("(k p) n -> p k n", p=128)).then_inc(s_w[n % 2], 16)
                if n == 1:
                    for b in range(NB):
                        sp.dma_start(xa[:, b, :], x[b]).then_inc(s_x[b], 16)
                    sp.dma_start(normw[:, :], norm_w).then_inc(s_const, 16)
                    sp.dma_start(ident[:, :], identity).then_inc(s_const, 16)
                    sp.dma_start(gates[:, 0:1], g_xattn.unsqueeze(0).broadcast_to([128, 1])).then_inc(s_const, 16)
                    sp.dma_start(gates[:, 1:2], g_ffn.unsqueeze(0).broadcast_to([128, 1])).then_inc(s_const, 16)
                    sp.dma_start(shift[:, :], shifts).then_inc(s_const, 16)
                    sp.dma_start(maskall[:, :, :], mask.unsqueeze(0).broadcast_to([L, B, M])).then_inc(s_mask, 16)
                    sp.dma_start(masktail[:, :, :], mask_tail.unsqueeze(0)).then_inc(s_mask, 16)

            def group(g, last):
                if not last:
                    sp.wait_ge(s_ctxlo, KT * (g + 1))
                    sp.dma_start(ctx_raw[:, :, :], ctx_tail[bass.ds(g + 1, 1)].rearrange("o p k c -> (o p) k c"))\
                      .then_inc(s_ctx, 16)
                for b in range(NB):
                    sp.wait_ge(s_x1, NB * g + b + 1)
                    sp.dma_start(x1_dram[bass.ds(NB * g + b, 1)].rearrange("o t d -> (o t) d"), xa[:, b, :])\
                      .then_inc(s_x1st[b], 16)
                if not last:
                    for b in range(NB):
                        sp.wait_ge(s_x1st[b], 16 * (g + 1))
                        sp.dma_start(xa[:, b, :], x[bass.ds(NB * (g + 1) + b, 1)].rearrange("o t d -> (o t) d"))\
                          .then_inc(s_x[b], 16)

            def full_loads(b):
                sp.dma_start(ctx_raw[:, :, 0:M], ctx_full[bass.ds(b, 1)].rearrange("o k p c -> p (o k) c")).then_inc(f_load, 16)
                sp.dma_start(xa[:, 0, :], x[bass.ds(b, 1)].rearrange("o t d -> (o t) d")).then_inc(f_load, 16)
                sp.dma_start(maskrow[:, 0:M], mask[bass.ds(b, 1), :]).then_inc(f_load, 16)

            def full_store(b):
                sp.wait_ge(f_x1, b + 1)
                sp.dma_start(x1_dram[bass.ds(b, 1)].rearrange("o t d -> (o t) d"), xa[:, 0, :]).then_inc(f_st, 16)
                sp.wait_ge(f_st, 16 * (b + 1))

            with sp.If(wants_full(sp)):
                sp.wait_ge(s_ctxlo, KT)
                for b in range(NB):
                    sp.wait_ge(s_x[b], 16)
                full_loads(0)
                with sp.Fori(0, B - 1) as b:
                    full_store(b)
                    full_loads(b + 1)
                full_store(B - 1)
            with sp.Else():
                with sp.Fori(0, GROUPS - 1) as g:
                    group(g, False)
                group(GROUPS - 1, True)
                for b in range(NB):
                    sp.wait_ge(s_x1st[b], 16 * GROUPS)
            sp.sem_inc(s_pa, 1)

            sp.wait_ge(s_pa, 5)

            def load_piece(n):
                s = n % 2
                if n >= 2:
                    sp.wait_ge(s_wlo, n - 1)
                if n < FT:
                    cols = slice(256 * n, 256 * n + 256)
                    for half in range(2):
                        p = slice(64 * half, 64 * half + 64)
                        sp.dma_start(words[s][p, 0:256], gu_packed[:, cols]).then_inc(s_words[s], 16)
                        sp.dma_start(scale[s][p, 0:256], gu_scales[:, cols].unsqueeze(1).broadcast_to([4, 16, 256]))\
                          .then_inc(s_words[s], 16)
                else:
                    c = n - FT
                    rep, nw = (4, 32) if c < 5 else (8, 16)
                    sp.dma_start(words[s][:, :], dn_packed[32 * c:32 * c + nw, :].unsqueeze(0).broadcast_to([rep, nw, D]))\
                      .then_inc(s_words[s], 16)
                    if c < 5:
                        for r in range(rep):
                            sp.dma_start(scale[s][32 * r:32 * r + 32, :],
                                         dn_scales[2 * c:2 * c + 2, :].unsqueeze(1).broadcast_to([2, 16, D]))\
                              .then_inc(s_words[s], 16)
                    else:
                        sp.dma_start(scale[s][:, :], dn_scales[10:11, :].broadcast_to([128, D])).then_inc(s_words[s], 16)

            x1_flat = x1_dram.rearrange("b t d -> (b t) d")
            out_flat = out.rearrange("b t d -> (b t) d")

            def load_x1(j, slot):
                sp.dma_start(xb[slot][:, 0:2, :], x1_flat[bass.ds(TG * j, 256), :].rearrange("(m p) d -> p m d", p=128))\
                  .then_inc(s_xb[slot], 16)
                sp.dma_start(xb[slot][0:64, 2, :], x1_flat[bass.ds(TG * j + 256, 64), :]).then_inc(s_xb[slot], 16)

            def store_tiles(h, par):
                j = 2 * h + par
                for m, rows in enumerate(ROWS):
                    slot = (par + m) % 2
                    sp.wait_ge(s_yo, 3 * j + m + 1)
                    sp.dma_start(out_flat[bass.ds(TG * j + 128 * m, rows), :], yo[slot][0:rows, :])\
                      .then_inc(s_out[slot], 16)

            load_x1(0, 0)
            for n in range(PIECES):
                load_piece(n)
            with sp.Fori(0, (FGROUPS - 1) // 2) as h:
                for par in range(2):
                    load_x1(2 * h + par + 1, (par + 1) % 2)
                    store_tiles(h, par)
            store_tiles((FGROUPS - 1) // 2, 0)
            for s in range(2):
                sp.wait_ge(s_out[s], 16 * ((3 * FGROUPS + 1 - s) // 2))

        @block.gpsimd
        def _(pool):
            nc.gpsimd.memset(halfpow[:, :], -0.5).then_inc(s_pconst, 1)
            nc.gpsimd.memset(ones[:, :], 1.0).then_inc(s_pconst, 1)
            for s in range(2):
                for half in range(2):
                    nc.gpsimd.memset(kblk[s][half][:, :, :].bitcast(F32), 0.0).then_inc(s_zero, 1)

            def ctx_lo(g, k):
                pool.wait_ge(s_ctxhi, KT * g + k + 1)
                nc.gpsimd.tensor_tensor(ctxT[LO][:, k, :], ctx_raw[:, k, :], ctxT[HI][:, k, :].bitcast(F32),
                                        ALU.subtract).then_inc(s_ctxlo, 1)

            for k in range(KT):
                ctx_lo(0, k)
            pool.wait_ge(s_pconst, 2)

            def group(g, last):
                for b in range(NB):
                    pool.wait_ge(s_ln, 3 * (NB * g + b) + 3)
                    nc.gpsimd.tensor_tensor(rstd[0:L, b:b + 1], var[0:L, b:b + 1], halfpow[0:L, b:b + 1], ALU.pow)\
                      .then_inc(s_pow, 1)
                for i in range(STEPS):
                    n = STEPS * g + i
                    pool.wait_ge(s_inv, n + 1)
                    nc.gpsimd.tensor_tensor(probs_at(i)[:, :, :], probs_at(i)[:, :, :],
                                            rinv[:, i % 4, :].unsqueeze(2).broadcast_to([L, HPG, TAIL]), ALU.mult)\
                      .then_inc(s_norm, 1)
                    if not last and i >= STEPS - KT:
                        ctx_lo(g + 1, i - (STEPS - KT))

            with pool.If(wants_full(pool)):
                pool.wait_ge(s_zero, 4)
                with pool.Fori(0, B) as b:
                    pool.wait_ge(f_ln, 3 * b + 3)
                    nc.gpsimd.tensor_tensor(rstd[0:L, 0:1], var[0:L, 0:1], halfpow[0:L, 0:1], ALU.pow).then_inc(f_pow, 1)
                    for hg in range(HG):
                        pool.wait_ge(f_inv, HG * b + hg + 1)
                        nc.gpsimd.tensor_tensor(probs_full, probs_full, rinv[:, 0, :].unsqueeze(2).broadcast_to([L, HPG, KC]),
                                                ALU.mult).then_inc(f_norm, 1)
                pool.wait_ge(f_norm, HG * B)
            with pool.Else():
                with pool.Fori(0, GROUPS - 1) as g:
                    group(g, False)
                group(GROUPS - 1, True)
                pool.wait_ge(s_norm, GROUPS * STEPS)
            pool.sem_inc(s_pa, 1)

            pool.wait_ge(s_pa, 5)

            def piece_lo(n):
                pool.wait_ge(s_dec, n + 1)
                gu = n < FT
                halves = fp4[n % 2][:, :].bitcast(F16).rearrange("p (c two) -> p c two", two=2)
                if gu:
                    for r in range(2):
                        for half in range(2):
                            last = nc.gpsimd.tensor_tensor(wgu[LO][:, 2 * half + r, 256 * n:256 * n + 256],
                                                           halves[:, 256 * r:256 * r + 256, half],
                                                           scale_b[:, 0:256], ALU.mult)
                else:
                    for half in range(2 if n - FT < 5 else 1):
                        last = nc.gpsimd.tensor_tensor(wdn[LO][:, 2 * (n - FT) + half, :], halves[:, :, half],
                                                       scale_b[:, :], ALU.mult)
                last.then_inc(s_wlo, 1)

            def hidden_lo(j, par, t):
                pool.wait_ge(s_hhi, FT * j + t + 1)
                nc.gpsimd.tensor_tensor(hT[LO][:, t, :], hidden[(par + t) % 2][:, :], hT[HI][:, t, :].bitcast(F32),
                                        ALU.subtract).then_inc(s_hlo, 1)

            def ffn_rstd(j):
                pool.wait_ge(s_bln, 3 * j + 3)
                nc.gpsimd.tensor_tensor(rstd[:, 0:3], var[:, 0:3], halfpow[:, 0:3], ALU.pow).then_inc(s_bpow, 1)

            def rms_tiles(j, par):
                for m in range(3):
                    slot = (par + m) % 2
                    pool.wait_ge(s_ms, 3 * j + m + 1)
                    nc.gpsimd.tensor_tensor(rrms[0:ROWS[m], slot:slot + 1], ms[0:ROWS[m], slot:slot + 1],
                                            halfpow[0:ROWS[m], 0:1], ALU.pow).then_inc(s_rr, 1)

            ffn_rstd(0)
            for t in range(FT):
                piece_lo(t)
                if t >= 1:
                    hidden_lo(0, 0, t - 1)
            hidden_lo(0, 0, FT - 1)
            for n in range(FT, PIECES):
                piece_lo(n)
            with pool.Fori(0, (FGROUPS - 1) // 2) as h:
                for par in range(2):
                    ffn_rstd(2 * h + par + 1)
                    rms_tiles(2 * h + par, par)
                    for t in range(FT):
                        hidden_lo(2 * h + par + 1, (par + 1) % 2, t)
            rms_tiles(FGROUPS - 1, 0)

        @block.scalar
        def _(act):
            def split_hi(n, name):
                w = raw[n % 2]
                act.wait_ge(s_w[n % 2], 16 * (n // 2 + 1))
                for k in range(KT):
                    if name in ("wq", "wg"):
                        last = nc.scalar.activation(W[name][HI][:, k, :], w[:, k, :], ACT.Copy, scale=normw[:, k:k + 1])
                    else:
                        last = nc.scalar.activation(W[name][HI][:, k, :], w[:, k, :], ACT.Copy)
                last.then_inc(s_split, 1)

            def ctx_hi(g, k):
                if k == 0:
                    act.wait_ge(s_ctx, 16 * (g + 1))
                nc.scalar.activation(ctxT[HI][:, k, :], ctx_raw[:, k, :], ACT.Copy).then_inc(s_ctxhi, 1)

            for k in range(KT):
                ctx_hi(0, k)
            for n, name in enumerate(("wv", "wk", "wq", "wg", "wo")):
                if n == 2:
                    act.wait_ge(s_const, 16 * CONSTS)
                    nc.scalar.activation(tanhs[:, :], gates[:, :], ACT.Tanh).then_inc(s_tanh, 1)
                split_hi(n, name)

            def read_job(g, name):
                act.wait_ge(s_pj[job_bank(name)], job_count(g, name))

            def job_hi(g, name):
                read_job(g, name)
                src = PJ[job_bank(name)]
                kind, n = name[0], int(name[1])
                if kind == "V":
                    last = nc.scalar.activation(vv[HI][0:TAIL, n, :], src[0:TAIL, :], ACT.Copy)
                elif kind == "X":
                    last = nc.scalar.activation(xT[HI][:, :, L * n:L * n + L],
                                                src[:, 0:KT * L].rearrange("p (k t) -> p k t", k=KT), ACT.Copy)
                elif kind == "Q":
                    last = nc.scalar.activation(qT[n % 2][HI][:, :], src[:, 0:GT], ACT.Copy, scale=HD ** -0.5)
                else:
                    for h in range(HPG):
                        p = slice(HD * h, HD * h + HD)
                        last = nc.scalar.activation(kblk[n % 2][HI][p, h, :], src[p, 0:KC], ACT.Copy)
                last.then_inc(s_pjhi, 1)

            def exp_step(g, i):
                n = STEPS * g + i
                act.wait_ge(s_max, n + 1)
                if i >= 3:
                    act.wait_ge(s_pt, n - 2)
                for h in range(HPG):
                    last = nc.scalar.activation(probs_at(i)[:, h, :], SC[i % 2][0:L, TAIL * h:TAIL * h + TAIL], ACT.Exp,
                                                bias=nmax[:, i % 4, h:h + 1], accum_out=rsum[:, i % 4, h:h + 1])
                last.then_inc(s_exp, 1)

            def probsT_hi(g, i):
                n = STEPS * g + i
                act.wait_ge(s_pt, n + 1)
                if i >= 2:
                    act.wait_ge(s_pv, n - 1)
                nc.scalar.activation(pT[i % 2][HI][0:TAIL, :, :].rearrange("k h t -> k (h t)"), PT[i % 2][0:TAIL, 0:GT],
                                     ACT.Copy).then_inc(s_pthi, 1)

            def attn_hi(g, i):
                n = STEPS * g + i
                hg, b = i // NB, i % NB
                act.wait_ge(s_pv, n + 1)
                for h in range(HPG):
                    p = slice(HD * h, HD * h + HD)
                    last = nc.scalar.activation(oT[HI][p, hg, L * b:L * b + L], PV[i % 2][p, L * h:L * h + L], ACT.Copy)
                last.then_inc(s_ohi, 1)

            def group(g, last):
                for name in JOBS[0:10]:
                    job_hi(g, name)
                exp_step(g, 0)
                for i in range(STEPS):
                    hg, b = i // NB, i % NB
                    if i + 1 < STEPS:
                        exp_step(g, i + 1)
                    if hg + 1 < HG and b < 2:
                        job_hi(g, "KQ"[b] + str(hg + 1))
                    if i >= STEPS - KT and not last:
                        ctx_hi(g + 1, i - (STEPS - KT))
                    probsT_hi(g, i)
                    if i >= 1:
                        attn_hi(g, i - 1)
                attn_hi(g, STEPS - 1)
                for b in range(NB):
                    name = f"G{b}"
                    read_job(g, name)
                    if b >= 2:
                        act.wait_ge(s_gated, NB * g + b - 1)
                    nc.scalar.activation(gate[b % 2][:, :], PJ[job_bank(name)][0:L, :], ACT.Tanh, scale=0.5)\
                      .then_inc(s_gate, 1)
                    act.wait_ge(s_gate, NB * g + b + 1)
                    act.sem_inc(s_pjfree[job_bank(name)], 1)

            def full_hi(b, name):
                act.wait_ge(f_pj, full_count(b, name))
                n = int(name[1:] or 0)
                if name[0] == "V":
                    last = nc.scalar.activation(vv[HI][:, n, :], FJ[:, :], ACT.Copy)
                elif name[0] == "X":
                    last = nc.scalar.activation(xT[HI][:, :, 0:L], FJ[:, 0:KT * L].rearrange("p (k t) -> p k t", k=KT), ACT.Copy)
                elif name[0] == "Q":
                    last = nc.scalar.activation(qT[0][HI][:, 0:L], FJ[:, 0:L], ACT.Copy, scale=HD ** -0.5)
                else:
                    for h in range(HPG):
                        p = slice(HD * h, HD * h + HD)
                        last = nc.scalar.activation(kblk[0][HI][p, h, :], FJ[p, 0:KC], ACT.Copy)
                last.then_inc(f_pjhi, 1)

            with act.If(wants_full(act)):
                act.wait_ge(s_zero, 4)
                with act.Fori(0, B) as b:
                    act.wait_ge(f_load, 48 * b + 48)
                    for k in range(KT):
                        last = nc.scalar.activation(ctxT[HI][:, k, 0:M], ctx_raw[:, k, 0:M], ACT.Copy)
                    last.then_inc(f_ctxhi, 1)
                    for name in FULL_JOBS[0:CHUNKS + 1]:
                        full_hi(b, name)
                    for hg in range(HG):
                        i = HG * b + hg
                        full_hi(b, f"K{hg}")
                        full_hi(b, f"Q{hg}")
                        act.wait_ge(f_max, i + 1)
                        for c in range(CHUNKS):
                            for h in range(HPG):
                                last = nc.scalar.activation(probs_full[:, h, CHUNK * c:CHUNK * c + CHUNK],
                                                            FSC[c][0:L, CHUNK * h:CHUNK * h + CHUNK], ACT.Exp,
                                                            bias=nmax[:, 0, h:h + 1], accum_out=rsum_c[:, c, h:h + 1])
                        last.then_inc(f_exp, 1)
                        for c in range(CHUNKS):
                            act.wait_ge(f_pt, CHUNKS * i + c + 1)
                            if c:
                                act.wait_ge(f_pv, CHUNKS * i + c)
                            nc.scalar.activation(pT[0][HI][:, :, :].rearrange("k h t -> k (h t)"), FPT[:, 0:GT], ACT.Copy)\
                              .then_inc(f_pthi, 1)
                        act.wait_ge(f_pv, CHUNKS * i + CHUNKS)
                        for h in range(HPG):
                            p = slice(HD * h, HD * h + HD)
                            last = nc.scalar.activation(oT[HI][p, hg, 0:L], FPV[p, L * h:L * h + L], ACT.Copy)
                        last.then_inc(f_ohi, 1)
                    act.wait_ge(f_g, b + 1)
                    nc.scalar.activation(gate[0][:, :], FJ[0:L, :], ACT.Tanh, scale=0.5).then_inc(f_gate, 1)
                act.wait_ge(f_gate, B)
            with act.Else():
                with act.Fori(0, GROUPS - 1) as g:
                    group(g, False)
                group(GROUPS - 1, True)
                act.wait_ge(s_gate, GROUPS * NB)
            act.sem_inc(s_pa, 1)

            act.wait_ge(s_pa, 5)

            def mT_hi(j, par, m):
                n = 3 * j + m
                bank_t = bank[4 + (par + m) % 2]
                act.wait_ge(s_mt, n + 1)
                rows = ROWS[m]
                nc.scalar.activation(mT[HI][:, :, 128 * m:128 * m + rows],
                                     bank_t[:, 0:KT * rows].rearrange("p (k t) -> p k t", k=KT), ACT.Copy).then_inc(s_mthi, 1)

            def gate_up(j, par, t):
                n = FT * j + t
                act.wait_ge(s_gu, n + 1)
                act.wait_ge(s_sg, n)
                nc.scalar.activation(tgate[:, :], bank[2 * ((par + t) % 2)][:, 0:TG], ACT.Tanh, scale=0.5).then_inc(s_tg, 1)

            def hidden_hi(j, par, t):
                act.wait_ge(s_h, FT * j + t + 1)
                nc.scalar.activation(hT[HI][:, t, :], hidden[(par + t) % 2][:, :], ACT.Copy).then_inc(s_hhi, 1)

            def square(j, par, m):
                n = 3 * j + m
                slot, rows = (par + m) % 2, ROWS[m]
                act.wait_ge(s_y, n + 1)
                return nc.scalar.activation(yo[slot][0:rows, :], bank[6 + slot][0:rows, :], ACT.Square,
                                            accum_out=ssq[0:rows, slot:slot + 1]).then_inc(s_sq, 1)

            def all_gate_up(j, par):
                for t in range(FT):
                    gate_up(j, par, t)
                    if t >= 1:
                        hidden_hi(j, par, t - 1)
                hidden_hi(j, par, FT - 1)

            for m in range(3):
                mT_hi(0, 0, m)
            all_gate_up(0, 0)
            with act.Fori(0, (FGROUPS - 1) // 2) as h:
                for par in range(2):
                    j = 2 * h + par
                    for m in range(3):
                        if m < 2:
                            act.wait_ge(s_out[(par + m) % 2], 16 * (3 * h + (3 * par + m) // 2))
                        else:
                            act.wait_ge(s_out[par], 16 * (3 * h + (3 * par + 2) // 2))
                        square(j, par, m)
                        mT_hi(j + 1, (par + 1) % 2, m)
                    all_gate_up(j + 1, (par + 1) % 2)
            for m in range(3):
                act.wait_ge(s_out[m % 2], 16 * (3 * ((FGROUPS - 1) // 2) + m // 2))
                square(FGROUPS - 1, 0, m)

        @block.vector
        def _(dve):
            nc.vector.memset(mv[:, :, :], 0.0).then_inc(s_setup, 1)
            nc.vector.memset(mbias[:, :, :], 0.0).then_inc(s_setup, 1)

            def split_lo(n, name):
                dve.wait_ge(s_split, n + 1)
                w = raw[n % 2]
                for k in range(KT):
                    hi = W[name][HI][:, k, :].bitcast(F32)
                    if name in ("wq", "wg"):
                        last = nc.vector.scalar_tensor_tensor(W[name][LO][:, k, :], w[:, k, :], normw[:, k:k + 1], hi,
                                                              ALU.mult, ALU.subtract)
                    else:
                        last = nc.vector.tensor_tensor(W[name][LO][:, k, :], w[:, k, :], hi, ALU.subtract)
                last.then_inc(s_splitlo, 1)

            split_lo(0, "wv")
            split_lo(1, "wk")
            dve.wait_ge(s_mask, 32)
            nc.vector.tensor_reduce(anykeep[0:L, :], maskall[:, :, :], AXIS_X, ALU.max).then_inc(s_setup, 1)
            dve.wait_ge(s_setup, 2)
            nc.vector.tensor_scalar(mbias[0:1, :, :], masktail[:, :, :], 1.0, MASKED, ALU.subtract, ALU.mult).then_inc(s_setup, 1)
            nc.vector.tensor_reduce(headmax[:, :], maskall[0:1, :, 0:M - TAIL], mybir.AxisListType.XY, ALU.max).then_inc(s_setup, 1)
            dve.wait_ge(s_setup, 5)
            nc.vector.tensor_copy(headkeep[:, :], headmax[:, :]).then_inc(s_setup, 1)
            dve.wait_ge(s_tanh, 1)
            nc.vector.tensor_scalar(coef_a[0:L, :], anykeep[0:L, :], tanhs[0:L, 0:1], 0.5, ALU.mult, ALU.mult).then_inc(s_setup, 1)
            for n, name in ((2, "wq"), (3, "wg"), (4, "wo")):
                split_lo(n, name)

            def job_lo(g, name):
                dve.wait_ge(s_pjhi, hi_count(g, name))
                src = PJ[job_bank(name)]
                kind, n = name[0], int(name[1])
                if kind == "V":
                    last = nc.vector.tensor_tensor(vv[LO][0:TAIL, n, :], src[0:TAIL, :], vv[HI][0:TAIL, n, :].bitcast(F32), ALU.subtract)
                elif kind == "X":
                    last = nc.vector.tensor_tensor(xT[LO][:, :, L * n:L * n + L], src[:, 0:KT * L].rearrange("p (k t) -> p k t", k=KT),
                                                   xT[HI][:, :, L * n:L * n + L].bitcast(F32), ALU.subtract)
                elif kind == "Q":
                    last = nc.vector.scalar_tensor_tensor(qT[n % 2][LO][:, :], src[:, 0:GT], HD ** -0.5,
                                                          qT[n % 2][HI][:, :].bitcast(F32), ALU.mult, ALU.subtract)
                else:
                    for h in range(HPG):
                        p = slice(HD * h, HD * h + HD)
                        last = nc.vector.tensor_tensor(kblk[n % 2][LO][p, h, :], src[p, 0:KC],
                                                       kblk[n % 2][HI][p, h, :].bitcast(F32), ALU.subtract)
                last.then_inc(s_pjfree[job_bank(name)], 1)

            def layer_stats(g, b):
                c = 3 * (NB * g + b)
                dve.wait_ge(s_x[b], 16 * (g + 1))
                nc.vector.bn_stats(stats[0:L, b, :], xa[:, b, :]).then_inc(s_ln, 1)
                wait_apart(dve, s_ln, c + 1)
                nc.vector.bn_aggr(mv[0:L, b, :], stats[0:L, b, :]).then_inc(s_ln, 1)
                dve.wait_ge(s_ln, c + 2)
                nc.vector.tensor_scalar(var[0:L, b:b + 1], mv[0:L, b, 1:2], 1.0 + RMS_EPS, LN_EPS * RMS_EPS, ALU.mult, ALU.add)\
                  .then_inc(s_ln, 1)

            def normalise(g, b):
                dve.wait_ge(s_pow, NB * g + b + 1)
                if b >= 2:
                    name = f"X{b - 2}"
                    dve.wait_ge(s_pj[job_bank(name)], job_count(g, name))
                nc.vector.tensor_scalar(xn[:, b % 2, :], xa[:, b, :], mv[0:L, b, 0:1], rstd[0:L, b:b + 1], ALU.subtract, ALU.mult)\
                  .then_inc(s_xn, 1)

            def row_max(g, i):
                n = STEPS * g + i
                dve.wait_ge(s_sc, n + 1)
                nc.vector.tensor_reduce(nmax[:, i % 4, :], SC[i % 2][0:L, 0:KC].rearrange("t (h k) -> t h k", h=HPG),
                                        AXIS_X, ALU.max, negate=True).then_inc(s_max, 1)

            def row_inverse(g, i):
                dve.wait_ge(s_exp, STEPS * g + i + 1)
                nc.vector.reciprocal(rinv[:, i % 4, :], rsum[:, i % 4, :]).then_inc(s_inv, 1)

            def probsT_lo(g, i):
                dve.wait_ge(s_pthi, STEPS * g + i + 1)
                nc.vector.tensor_tensor(pT[i % 2][LO][0:TAIL, :, :].rearrange("k h t -> k (h t)"), PT[i % 2][0:TAIL, 0:GT],
                                        pT[i % 2][HI][0:TAIL, :, :].rearrange("k h t -> k (h t)").bitcast(F32), ALU.subtract)\
                  .then_inc(s_ptlo, 1)

            def attn_lo(g, i):
                hg, b = i // NB, i % NB
                dve.wait_ge(s_ohi, STEPS * g + i + 1)
                for h in range(HPG):
                    p = slice(HD * h, HD * h + HD)
                    last = nc.vector.tensor_tensor(oT[LO][p, hg, L * b:L * b + L], PV[i % 2][p, L * h:L * h + L],
                                                   oT[HI][p, hg, L * b:L * b + L].bitcast(F32), ALU.subtract)
                last.then_inc(s_olo, 1)

            def output(g, b):
                name = f"O{b}"
                dve.wait_ge(s_gate, NB * g + b + 1)
                dve.wait_ge(s_pj[job_bank(name)], job_count(g, name))
                if b >= 1:
                    dve.wait_ge(s_x1, NB * g + b)
                nc.vector.scalar_tensor_tensor(gated[:, :], gate[b % 2][:, :], 1.0, PJ[job_bank(name)][0:L, :],
                                               ALU.add, ALU.mult).then_inc(s_gated, 1)
                dve.wait_ge(s_gated, NB * g + b + 1)
                dve.sem_inc(s_pjfree[job_bank(name)], 1)
                nc.vector.scalar_tensor_tensor(xa[:, b, :], gated[:, :], coef_a[0:L, bass.ds(NB * g + b, 1)], xa[:, b, :],
                                               ALU.mult, ALU.add).then_inc(s_x1, 1)

            def group(g, last):
                for what, n in (("V", 0), ("s", 0), ("V", 1), ("s", 1), ("n", 0), ("V", 2), ("s", 2), ("n", 1), ("V", 3), ("s", 3),
                                ("K", 0), ("n", 2), ("X", 0), ("n", 3), ("X", 1), ("X", 2), ("X", 3), ("Q", 0)):
                    if what == "s":
                        layer_stats(g, n)
                    elif what == "n":
                        normalise(g, n)
                    else:
                        job_lo(g, f"{what}{n}")
                row_max(g, 0)
                for i in range(STEPS):
                    hg, b = i // NB, i % NB
                    row_inverse(g, i)
                    if i + 1 < STEPS:
                        row_max(g, i + 1)
                    if hg + 1 < HG and b < 2:
                        job_lo(g, "KQ"[b] + str(hg + 1))
                    probsT_lo(g, i)
                    if i >= 1:
                        attn_lo(g, i - 1)
                attn_lo(g, STEPS - 1)
                for b in range(NB):
                    output(g, b)

            def full_lo(b, name):
                dve.wait_ge(f_pjhi, full_count(b, name))
                n = int(name[1:] or 0)
                if name[0] == "V":
                    last = nc.vector.tensor_tensor(vv[LO][:, n, :], FJ[:, :], vv[HI][:, n, :].bitcast(F32), ALU.subtract)
                elif name[0] == "X":
                    last = nc.vector.tensor_tensor(xT[LO][:, :, 0:L], FJ[:, 0:KT * L].rearrange("p (k t) -> p k t", k=KT),
                                                   xT[HI][:, :, 0:L].bitcast(F32), ALU.subtract)
                elif name[0] == "Q":
                    last = nc.vector.scalar_tensor_tensor(qT[0][LO][:, 0:L], FJ[:, 0:L], HD ** -0.5, qT[0][HI][:, 0:L].bitcast(F32),
                                                          ALU.mult, ALU.subtract)
                else:
                    for h in range(HPG):
                        p = slice(HD * h, HD * h + HD)
                        last = nc.vector.tensor_tensor(kblk[0][LO][p, h, :], FJ[p, 0:KC], kblk[0][HI][p, h, :].bitcast(F32),
                                                       ALU.subtract)
                last.then_inc(f_pjlo, 1)

            with dve.If(wants_full(dve)):
                dve.wait_ge(s_ctxlo, KT)
                dve.wait_ge(s_zero, 4)
                for half in range(2):
                    nc.vector.memset(ctxT[half][:, :, M:KC].bitcast(F32), 0.0).then_inc(f_ctx, 1)
                nc.vector.memset(mbias_full[0:1, M:KC], -MASKED).then_inc(f_bias, 1)
                with dve.Fori(0, B) as b:
                    dve.wait_ge(f_load, 48 * b + 48)
                    nc.vector.tensor_scalar(mbias_full[0:1, 0:M], maskrow[:, 0:M], 1.0, MASKED, ALU.subtract, ALU.mult)\
                      .then_inc(f_bias, 1)
                    nc.vector.bn_stats(stats[0:L, 0, :], xa[:, 0, :]).then_inc(f_ln, 1)
                    wait_apart(dve, f_ln, 3 * b + 1)
                    nc.vector.bn_aggr(mv[0:L, 0, :], stats[0:L, 0, :]).then_inc(f_ln, 1)
                    dve.wait_ge(f_ln, 3 * b + 2)
                    nc.vector.tensor_scalar(var[0:L, 0:1], mv[0:L, 0, 1:2], 1.0 + RMS_EPS, LN_EPS * RMS_EPS, ALU.mult, ALU.add)\
                      .then_inc(f_ln, 1)
                    dve.wait_ge(f_pow, b + 1)
                    nc.vector.tensor_scalar(xn[:, 0, :], xa[:, 0, :], mv[0:L, 0, 0:1], rstd[0:L, 0:1], ALU.subtract, ALU.mult)\
                      .then_inc(f_xn, 1)
                    dve.wait_ge(f_ctxhi, b + 1)
                    for k in range(KT):
                        last = nc.vector.tensor_tensor(ctxT[LO][:, k, 0:M], ctx_raw[:, k, 0:M], ctxT[HI][:, k, 0:M].bitcast(F32),
                                                       ALU.subtract)
                    last.then_inc(f_ctx, 1)
                    for name in FULL_JOBS[0:CHUNKS + 1]:
                        full_lo(b, name)
                    for hg in range(HG):
                        i = HG * b + hg
                        full_lo(b, f"K{hg}")
                        full_lo(b, f"Q{hg}")
                        dve.wait_ge(f_sc, i + 1)
                        for c in range(CHUNKS):
                            nc.vector.tensor_reduce(nmax_c[:, c, :], FSC[c][0:L, :].rearrange("t (h k) -> t h k", h=HPG),
                                                    AXIS_X, ALU.max, negate=True).then_inc(f_maxc, 1)
                        dve.wait_ge(f_maxc, 4 * i + 3)
                        nc.vector.tensor_tensor(nmax[:, 0, :], nmax_c[:, 0, :], nmax_c[:, 1, :], ALU.min).then_inc(f_maxc, 1)
                        dve.wait_ge(f_maxc, 4 * i + 4)
                        nc.vector.tensor_tensor(nmax[:, 0, :], nmax[:, 0, :], nmax_c[:, 2, :], ALU.min).then_inc(f_max, 1)
                        dve.wait_ge(f_exp, i + 1)
                        nc.vector.tensor_tensor(rsum[:, 0, :], rsum_c[:, 0, :], rsum_c[:, 1, :], ALU.add).then_inc(f_sum, 1)
                        dve.wait_ge(f_sum, 2 * i + 1)
                        nc.vector.tensor_tensor(rsum[:, 0, :], rsum[:, 0, :], rsum_c[:, 2, :], ALU.add).then_inc(f_sum, 1)
                        dve.wait_ge(f_sum, 2 * i + 2)
                        nc.vector.reciprocal(rinv[:, 0, :], rsum[:, 0, :]).then_inc(f_inv, 1)
                        for c in range(CHUNKS):
                            dve.wait_ge(f_pthi, CHUNKS * i + c + 1)
                            nc.vector.tensor_tensor(pT[0][LO][:, :, :].rearrange("k h t -> k (h t)"), FPT[:, 0:GT],
                                                    pT[0][HI][:, :, :].rearrange("k h t -> k (h t)").bitcast(F32), ALU.subtract)\
                              .then_inc(f_ptlo, 1)
                        dve.wait_ge(f_ohi, i + 1)
                        for h in range(HPG):
                            p = slice(HD * h, HD * h + HD)
                            last = nc.vector.tensor_tensor(oT[LO][p, hg, 0:L], FPV[p, L * h:L * h + L],
                                                           oT[HI][p, hg, 0:L].bitcast(F32), ALU.subtract)
                        last.then_inc(f_olo, 1)
                    dve.wait_ge(f_gate, b + 1)
                    dve.wait_ge(f_o, b + 1)
                    nc.vector.scalar_tensor_tensor(gated[:, :], gate[0][:, :], 1.0, FO[0:L, :], ALU.add, ALU.mult)\
                      .then_inc(f_gated, 1)
                    dve.wait_ge(f_gated, b + 1)
                    nc.vector.scalar_tensor_tensor(xa[:, 0, :], gated[:, :], coef_a[0:L, bass.ds(b, 1)], xa[:, 0, :],
                                                   ALU.mult, ALU.add).then_inc(f_x1, 1)
                dve.wait_ge(f_x1, B)
            with dve.Else():
                with dve.Fori(0, GROUPS - 1) as g:
                    group(g, False)
                group(GROUPS - 1, True)
                dve.wait_ge(s_x1, GROUPS * NB)
            dve.sem_inc(s_pa, 1)

            dve.wait_ge(s_pa, 5)
            count = [0]

            def chained(ins):
                count[0] += 1
                ins.then_inc(s_dq, 1)
                dve.wait_ge(s_dq, count[0])

            SIGN, MAGNITUDE = 0x80008000 - (1 << 32), 0x0E000E00

            words_in = [0, 0]

            def dequant(n):
                s = n % 2
                gu = n < FT
                cols = 256 if gu else D
                words_in[s] += 16 * piece_loads(n)
                if n >= 1:
                    dve.wait_ge(s_whi, n)
                dve.wait_ge(s_words[s], words_in[s])
                chained(nc.vector.tensor_scalar(scale_a[:, 0:cols].bitcast(I16), scale[s][:, 0:cols].bitcast(I16), -2, None,
                                                ALU.bitwise_and))
                if gu:
                    nc.vector.tensor_scalar(shifted[:, 0:256], words[s][:, 0:256], shift[:, 0:1], None, ALU.logical_shift_left)
                    chained(nc.vector.tensor_scalar(shifted[:, 256:512], words[s][:, 0:256], shift[:, 1:2], None,
                                                    ALU.logical_shift_left))
                elif n - FT < 5:
                    chained(nc.vector.tensor_scalar(shifted[:, :], words[s][:, :], shift[:, 2:3], None, ALU.logical_shift_left))
                else:
                    chained(nc.vector.tensor_scalar(shifted[:, :], words[s][:, :], shift[:, 3:4], shift[:, 4:5],
                                                    ALU.logical_shift_right, ALU.logical_shift_left))
                chained(nc.vector.tensor_scalar(fp4[s][:, :], shifted[:, :], 3, MAGNITUDE, ALU.logical_shift_right, ALU.bitwise_and))
                chained(nc.vector.scalar_tensor_tensor(fp4[s][:, :], shifted[:, :], SIGN, fp4[s][:, :], ALU.bitwise_and, ALU.bitwise_or))
                if n >= 1:
                    dve.wait_ge(s_wlo, n)
                chained(nc.vector.tensor_tensor(scale_b[:, 0:cols], scale[s][:, 0:cols], scale_a[:, 0:cols], ALU.subtract))
                nc.vector.tensor_scalar(scale_b[:, 0:cols], scale_b[:, 0:cols], FP4_UNIT, None, ALU.mult).then_inc(s_dec, 1)
                halves = fp4[s][:, :].bitcast(F16).rearrange("p (c two) -> p c two", two=2)
                if gu:
                    for r in range(2):
                        for half in range(2):
                            last = nc.vector.scalar_tensor_tensor(wgu[HI][:, 2 * half + r, 256 * n:256 * n + 256],
                                                                  halves[:, 256 * r:256 * r + 256, half], FP4_UNIT,
                                                                  scale_a[:, 0:256], ALU.mult, ALU.mult)
                else:
                    for half in range(2 if n - FT < 5 else 1):
                        last = nc.vector.scalar_tensor_tensor(wdn[HI][:, 2 * (n - FT) + half, :], halves[:, :, half], FP4_UNIT,
                                                              scale_a[:, :], ALU.mult, ALU.mult)
                last.then_inc(s_whi, 1)

            def ffn_stats(h, par):
                j = 2 * h + par
                dve.wait_ge(s_xb[par], 32 * (h + 1))
                for m, rows in enumerate(ROWS):
                    last = nc.vector.bn_stats(stats[0:rows, m, :], xb[par][0:rows, m, :])
                last.then_inc(s_bln, 1)
                wait_apart(dve, s_bln, 3 * j + 1)
                for m, rows in enumerate(ROWS):
                    last = nc.vector.bn_aggr(mv[0:rows, m, :], stats[0:rows, m, :])
                last.then_inc(s_bln, 1)
                dve.wait_ge(s_bln, 3 * j + 2)
                nc.vector.tensor_scalar(var[:, 0:3], mv[:, 0:3, 1], LN_EPS, None, ALU.add).then_inc(s_bln, 1)

            def ffn_normalise(j, par, m):
                rows = ROWS[m]
                dve.wait_ge(s_bpow, j + 1)
                dve.wait_ge(s_mt, 3 * j + m)
                nc.vector.tensor_scalar(mn[0:rows, :].rearrange("t (e p) -> t p e", e=8),
                                        xb[par][0:rows, m, :].rearrange("t (p e) -> t p e", e=8), mv[0:rows, m, 0:1], rstd[0:rows, m:m + 1],
                                        ALU.subtract, ALU.mult).then_inc(s_mn, 1)

            def mT_lo(j, par, m):
                rows = ROWS[m]
                dve.wait_ge(s_mthi, 3 * j + m + 1)
                nc.vector.tensor_tensor(mT[LO][:, :, 128 * m:128 * m + rows],
                                        bank[4 + (par + m) % 2][:, 0:KT * rows].rearrange("p (k t) -> p k t", k=KT),
                                        mT[HI][:, :, 128 * m:128 * m + rows].bitcast(F32), ALU.subtract).then_inc(s_mtlo, 1)

            def hidden_tile(j, par, t):
                n = FT * j + t
                gate_bank, up_bank = (bank[2 * ((par + t) % 2) + i] for i in range(2))
                dve.wait_ge(s_tg, n + 1)
                if t >= 2:
                    dve.wait_ge(s_hlo, n - 1)
                tile = hidden[(par + t) % 2]
                nc.vector.scalar_tensor_tensor(tile[:, :], tgate[:, :], 1.0, gate_bank[:, 0:TG], ALU.add, ALU.mult)\
                  .then_inc(s_sg, 1)
                dve.wait_ge(s_sg, n + 1)
                nc.vector.tensor_tensor(tile[:, :], tile[:, :], up_bank[:, 0:TG], ALU.mult).then_inc(s_h, 1)

            def output_tile(j, par, m):
                n = 3 * j + m
                slot, rows = (par + m) % 2, ROWS[m]
                dve.wait_ge(s_sq, n + 1)
                nc.vector.tensor_scalar(ms[0:rows, slot:slot + 1], ssq[0:rows, slot:slot + 1], 1.0 / D, 4 * RMS_EPS,
                                        ALU.mult, ALU.add).then_inc(s_ms, 1)
                dve.wait_ge(s_rr, n + 1)
                nc.vector.tensor_scalar(coef_y[0:rows, slot:slot + 1], rrms[0:rows, slot:slot + 1], tanhs[0:rows, 1:2], None,
                                        ALU.mult).then_inc(s_cy, 1)
                dve.wait_ge(s_cy, n + 1)
                nc.vector.scalar_tensor_tensor(yo[slot][0:rows, :], bank[6 + slot][0:rows, :], coef_y[0:rows, slot:slot + 1],
                                               xb[par][0:rows, m, :], ALU.mult, ALU.add).then_inc(s_yo, 1)

            ffn_stats(0, 0)
            for m in range(3):
                ffn_normalise(0, 0, m)
                mT_lo(0, 0, m)
            for t in range(FT):
                dequant(t)
                if t >= 1:
                    hidden_tile(0, 0, t - 1)
            hidden_tile(0, 0, FT - 1)
            for n in range(FT, PIECES):
                dequant(n)
            with dve.Fori(0, (FGROUPS - 1) // 2) as h:
                for par in range(2):
                    j, par1 = 2 * h + par, (par + 1) % 2
                    ffn_stats(h + par, par1)
                    for m in range(3):
                        ffn_normalise(j + 1, par1, m)
                        output_tile(j, par, m)
                        mT_lo(j + 1, par1, m)
                    for t in range(FT):
                        hidden_tile(j + 1, par1, t)
            for m in range(3):
                output_tile(FGROUPS - 1, 0, m)

        @block.tensor
        def _(pe):
            def open_bank(g, name):
                pe.wait_ge(s_pjfree[job_bank(name)], job_count(g, name) - 1)

            def done(g, name, last):
                last.then_inc(s_pj[job_bank(name)], 1)

            def job(g, name):
                kind, n = name[0], int(name[1])
                dst = PJ[job_bank(name)]
                if kind == "V":
                    if n == 0:
                        pe.wait_ge(s_ctxlo, KT * (g + 1))
                    open_bank(g, name)
                    last = product(dst[0:TAIL, :], lambda a, k: ctxT[a][:, k, TAIL * n:TAIL * n + TAIL],
                                   lambda a, k: W["wv"][a][:, k, :], KT)
                elif kind == "K":
                    open_bank(g, name)
                    last = product(dst[:, 0:KC], lambda a, k: W["wk"][a][:, k, 128 * n:128 * n + 128],
                                   lambda a, k: ctxT[a][:, k, :], KT)
                elif kind == "X":
                    open_bank(g, name)
                    pe.wait_ge(s_xn, NB * g + n + 1)
                    for k in range(KT):
                        last = nc.tensor.transpose(dst[:, L * k:L * k + L], xn[:, n % 2, 128 * k:128 * k + 128], ident[0:L, 0:L])
                elif kind == "Q":
                    open_bank(g, name)
                    if n == 0:
                        pe.wait_ge(s_pjfree[job_bank("X3")], job_count(g, "X3"))
                        pe.wait_ge(s_pjfree[job_bank("X2")], job_count(g, "X2"))
                    last = product(dst[:, 0:GT], lambda a, k: W["wq"][a][:, k, 128 * n:128 * n + 128],
                                   lambda a, k: xT[a][:, k, :], KT)
                elif kind == "G":
                    open_bank(g, name)
                    last = product(dst[0:L, :], lambda a, k: xT[a][:, k, L * n:L * n + L], lambda a, k: W["wg"][a][:, k, :], KT)
                else:
                    open_bank(g, name)
                    if n == 0:
                        pe.wait_ge(s_olo, STEPS * (g + 1))
                    last = product(dst[0:L, :], lambda a, k: oT[a][:, k, L * n:L * n + L], lambda a, k: W["wo"][a][:, k, :], KT)
                done(g, name, last)

            def scores(g, i):
                n = STEPS * g + i
                hg, b = i // NB, i % NB
                dst = SC[i % 2][0:L, 0:KC].rearrange("t (h k) -> t h k", h=HPG)
                if b == 0:
                    for name in (f"K{hg}", f"Q{hg}"):
                        pe.wait_ge(s_pjfree[job_bank(name)], job_count(g, name))
                if i >= 2:
                    pe.wait_ge(s_exp, n - 1)
                nc.tensor.matmul(dst, ones[:, :], mbias[:, bass.ds(NB * g + b, 1), :].broadcast_to([128, HPG, TAIL]),
                                 start=True, stop=False)
                product(dst, lambda a, t: qT[hg % 2][a][:, L * b:L * b + L],
                        lambda a, t: kblk[hg % 2][a][:, :, TAIL * b:TAIL * b + TAIL], 1, first=False).then_inc(s_sc, 1)

            def transpose_probs(g, i):
                n = STEPS * g + i
                pe.wait_ge(s_norm, n + 1)
                if i >= 2:
                    pe.wait_ge(s_ptlo, n - 1)
                for h in range(HPG):
                    last = nc.tensor.transpose(PT[i % 2][0:TAIL, L * h:L * h + L], probs_at(i)[:, h, :], ident[0:L, 0:L])
                last.then_inc(s_pt, 1)

            def attend(g, i):
                n = STEPS * g + i
                hg, b = i // NB, i % NB
                pe.wait_ge(s_ptlo, n + 1)
                if i >= 2:
                    pe.wait_ge(s_olo, n - 1)
                product(PV[i % 2][:, 0:GT], lambda a, t: vv[a][0:TAIL, b, 128 * hg:128 * hg + 128],
                        lambda a, t: pT[i % 2][a][0:TAIL, :, :].rearrange("k h t -> k (h t)"), 1).then_inc(s_pv, 1)

            def group(g, last):
                for name in JOBS[0:10]:
                    job(g, name)
                scores(g, 0)
                for i in range(STEPS):
                    hg, b = i // NB, i % NB
                    if i + 1 < STEPS:
                        scores(g, i + 1)
                    if i >= 1:
                        attend(g, i - 1)
                    if hg + 1 < HG and b < 2:
                        job(g, "KQ"[b] + str(hg + 1))
                    transpose_probs(g, i)
                for name in ("G0",):
                    job(g, name)
                attend(g, STEPS - 1)
                for name in JOBS[JOB["O0"]:]:
                    job(g, name)

            pe.wait_ge(s_splitlo, 5)
            pe.wait_ge(s_const, 16 * CONSTS)
            pe.wait_ge(s_zero, 4)
            pe.wait_ge(s_pconst, 2)
            pe.wait_ge(s_setup, 6)
            def full_job(b, name):
                n = int(name[1:] or 0)
                if name == FULL_JOBS[0]:
                    pe.wait_ge(f_ctx, b + 3)
                else:
                    pe.wait_ge(f_pjlo, full_count(b, name) - 1)
                if name[0] == "V":
                    last = product(FJ[:, :], lambda a, k: ctxT[a][:, k, CHUNK * n:CHUNK * n + CHUNK],
                                   lambda a, k: W["wv"][a][:, k, :], KT)
                elif name[0] == "X":
                    pe.wait_ge(f_xn, b + 1)
                    for k in range(KT):
                        last = nc.tensor.transpose(FJ[:, L * k:L * k + L], xn[:, 0, 128 * k:128 * k + 128], ident[0:L, 0:L])
                elif name[0] == "Q":
                    last = product(FJ[:, 0:L], lambda a, k: W["wq"][a][:, k, 128 * n:128 * n + 128],
                                   lambda a, k: xT[a][:, k, 0:L], KT)
                else:
                    last = product(FJ[:, 0:KC], lambda a, k: W["wk"][a][:, k, 128 * n:128 * n + 128],
                                   lambda a, k: ctxT[a][:, k, :], KT)
                last.then_inc(f_pj, 1)

            with pe.If(wants_full(pe)):
                with pe.Fori(0, B) as b:
                    for name in FULL_JOBS[0:CHUNKS + 1]:
                        full_job(b, name)
                    pe.wait_ge(f_bias, b + 2)
                    for hg in range(HG):
                        i = HG * b + hg
                        full_job(b, f"K{hg}")
                        full_job(b, f"Q{hg}")
                        pe.wait_ge(f_pjlo, full_count(b, f"Q{hg}"))
                        for c in range(CHUNKS):
                            cols = slice(CHUNK * c, CHUNK * c + CHUNK)
                            dst = FSC[c][0:L, :].rearrange("t (h k) -> t h k", h=HPG)
                            nc.tensor.matmul(dst, ones[:, :], mbias_full[:, cols].unsqueeze(1).broadcast_to([128, HPG, CHUNK]),
                                             start=True, stop=False)
                            last = product(dst, lambda a, t: qT[0][a][:, 0:L], lambda a, t: kblk[0][a][:, :, cols], 1, first=False)
                        last.then_inc(f_sc, 1)
                        pe.wait_ge(f_norm, i + 1)
                        if hg:
                            pe.wait_ge(f_olo, i)
                        for c in range(CHUNKS):
                            n = CHUNKS * i + c
                            if c:
                                pe.wait_ge(f_ptlo, n)
                            for h in range(HPG):
                                last = nc.tensor.transpose(FPT[:, L * h:L * h + L], probs_full[:, h, CHUNK * c:CHUNK * c + CHUNK],
                                                           ident[0:L, 0:L])
                            last.then_inc(f_pt, 1)
                            pe.wait_ge(f_ptlo, n + 1)
                            for p, (a, v) in enumerate(PASSES):
                                last = nc.tensor.matmul(FPV[:, 0:GT], vv[v][:, c, 128 * hg:128 * hg + 128],
                                                        pT[0][a][:, :, :].rearrange("k h t -> k (h t)"),
                                                        start=c == 0 and p == 0, stop=c == CHUNKS - 1 and p == 2)
                            last.then_inc(f_pv, 1)
                    product(FJ[0:L, :], lambda a, k: xT[a][:, k, 0:L], lambda a, k: W["wg"][a][:, k, :], KT).then_inc(f_g, 1)
                    pe.wait_ge(f_olo, HG * b + HG)
                    product(FO[0:L, :], lambda a, k: oT[a][:, k, 0:L], lambda a, k: W["wo"][a][:, k, :], KT).then_inc(f_o, 1)
                pe.wait_ge(f_o, B)
            with pe.Else():
                with pe.Fori(0, GROUPS - 1) as g:
                    group(g, False)
                group(GROUPS - 1, True)
                for i in range(2):
                    pe.wait_ge(s_pj[i], GROUPS * PER_BANK)
            pe.sem_inc(s_pa, 1)

            pe.wait_ge(s_pa, 5)

            def transpose_tile(j, par, m):
                rows = ROWS[m]
                if m == 2:
                    pe.wait_ge(s_mtlo, 3 * j + 1)
                wait_apart(pe, s_mn, 3 * j + m + 1)
                for k in range(KT):
                    last = nc.tensor.transpose(bank[4 + (par + m) % 2][:, rows * k:rows * k + rows],
                                               mn[0:rows, 128 * k:128 * k + 128], ident[0:rows, 0:rows])
                last.then_inc(s_mt, 1)

            def gate_up(j, par, t, first=False):
                n = FT * j + t
                if t == 0:
                    pe.wait_ge(s_mtlo, 3 * j + 3)
                if first:
                    pe.wait_ge(s_whi, t + 1)
                    pe.wait_ge(s_wlo, t + 1)
                if not first or t >= 2:
                    pe.wait_ge(s_h, n - 1)
                for i in range(2):
                    cols = slice(256 * t + 128 * i, 256 * t + 128 * i + 128)
                    last = product(bank[2 * ((par + t) % 2) + i][:, 0:TG], lambda a, k: wgu[a][:, k, cols],
                                   lambda a, k: mT[a][:, k, :], KT)
                last.then_inc(s_gu, 1)

            def down(j, par, m, first=False):
                slot, rows = (par + m) % 2, ROWS[m]
                pe.wait_ge(s_yo, max(m - 1, 0) + 3 * j)
                for t in range(FT):
                    if m == 0:
                        pe.wait_ge(s_hlo, FT * j + t + 1)
                        if first:
                            pe.wait_ge(s_whi, FT + t // 2 + 1)
                            pe.wait_ge(s_wlo, FT + t // 2 + 1)
                    for p, (a, b) in enumerate(PASSES):
                        last = nc.tensor.matmul(bank[6 + slot][0:rows, :], hT[a][:, t, 128 * m:128 * m + rows], wdn[b][:, t, :],
                                                start=t == 0 and p == 0, stop=t == FT - 1 and p == 2)
                last.then_inc(s_y, 1)

            for m in range(3):
                transpose_tile(0, 0, m)
            for t in range(FT):
                gate_up(0, 0, t, True)
            pe.wait_ge(s_wlo, PIECES)
            pe.wait_ge(s_whi, PIECES)
            with pe.Fori(0, (FGROUPS - 1) // 2) as h:
                for par in range(2):
                    j, par1 = 2 * h + par, (par + 1) % 2
                    for m in range(3):
                        down(j, par, m)
                        transpose_tile(j + 1, par1, m)
                    for t in range(FT):
                        gate_up(j + 1, par1, t)
            for m in range(3):
                down(FGROUPS - 1, 0, m)


INPUTS = ("x", "ctx_tail", "ctx_full", "mask", "mask_tail", "g_xattn", "g_ffn", "norm_w", "wq", "wk", "wv", "wo", "wg",
          "gu_packed", "gu_scales", "dn_packed", "dn_scales", "identity", "shifts")


def hidden_order(a, axis):
    a = np.moveaxis(a, axis, 0)
    rest = a.shape[1:]
    pairs = a[:1280].reshape(5, 32, 2, 4, *rest).transpose(0, 2, 3, 1, *range(4, 4 + len(rest))).reshape(1280, *rest)
    last = a[1280:].reshape(16, 8, *rest).transpose(1, 0, *range(2, 2 + len(rest))).reshape(128, *rest)
    return np.moveaxis(np.concatenate([pairs, last]), 0, axis)


def lay_out(inputs):
    a = {k: np.asarray(v) for k, v in inputs.items()}
    ctx = a["ctx_2048"]
    keep = a["mask_BxS2_bk0"]
    ctx_t = ctx.transpose(0, 2, 1).reshape(B, KT, 128, M)
    tail = ctx_t[..., M - TAIL:].reshape(GROUPS, NB, KT, 128, TAIL).transpose(0, 3, 2, 1, 4).reshape(GROUPS, 128, KT, KC)
    gu = a["L0_ffn_gate_up_packed"].T
    gs = a["L0_ffn_gate_up_scales"]

    def interleave(w):
        both = [hidden_order(w[:, i * FF:(i + 1) * FF], 1).reshape(w.shape[0], FT, 1, 128) for i in range(2)]
        return np.concatenate(both, 2).reshape(w.shape[0], 2 * FF)

    p = np.arange(128)
    shifts = np.stack([12 - 4 * (p // 64), 4 - 4 * (p // 64), 12 - 4 * (p // 32), 16 * (p // 64), 12 - 4 * (p // 16 % 4)], 1)
    return {
        "x": a["x"], "ctx_tail": tail, "ctx_full": ctx_t, "mask": keep, "mask_tail": keep[:, M - TAIL:],
        "g_xattn": a["g_xattn"], "g_ffn": a["g_ffn"], "norm_w": a["L0_xattn_norm_w"].reshape(KT, 128).T,
        **{n: a[f"L0_xattn_{n}"].T for n in ("wq", "wk", "wv", "wo", "wg")},
        "gu_packed": interleave(gu), "gu_scales": interleave(gs),
        "dn_packed": a["L0_ffn_down_packed"].T, "dn_scales": a["L0_ffn_down_scales"],
        "identity": np.eye(128, dtype=np.float32), "shifts": shifts.astype(np.int32),
    }


def kernel(**inputs):
    import concourse.bacc as bacc
    from concourse.bass_utils import run_bass_kernel_spmd

    nc = bacc.Bacc("TRN2", target_bir_lowering=False, num_devices=1)
    arrays, args = {}, []
    laid = lay_out(inputs)
    for name in INPUTS:
        a = np.ascontiguousarray(laid[name])
        arrays[f"in_{name}"] = a
        args.append(nc.dram_tensor(f"in_{name}", a.shape, mybir.dt.from_np(a.dtype), kind="ExternalInput").ap())
    args.append(nc.dram_tensor("x1_scratch", (B, L, D), F32, kind="Internal").ap())
    args.append(nc.dram_tensor("out_x", (B, L, D), F32, kind="ExternalOutput").ap())
    build(nc, *args)
    r = run_bass_kernel_spmd(nc, [arrays], core_ids=[0])
    return r.results[0]["out_x"]
```

```python
from contextlib import ExitStack

import numpy as np

import concourse.bass as bass
from concourse import mybir

F32, F32R, BF16, F16 = mybir.dt.float32, mybir.dt.float32r, mybir.dt.bfloat16, mybir.dt.float16
I32, I16, U8 = mybir.dt.int32, mybir.dt.int16, mybir.dt.uint8
ALU = mybir.AluOpType
ACT = mybir.ActivationFunctionType
AXIS_X = mybir.AxisListType.X

B, L, D = 16, 100, 512
M = 361
HEADS, HD = 16, 32
KT = D // 128
NB = 4
GROUPS = B // NB
GT = NB * L
HG = 4
HPG = HEADS // HG
TAIL = 96
KC = NB * TAIL
CHUNK = 128
CHUNKS = KC // CHUNK
STEPS = HG * NB
CONSTS = 4
FF = 1408
FT = FF // 128
TOKENS = B * L
TG = 320
FGROUPS = TOKENS // TG
ROWS = (128, 128, 64)
FP4_UNIT = 16384.0
MASKED = 1e30
NEXT_TILES = ((0, 1), (2,), ())
PIECES = FT + 6
LN_EPS, RMS_EPS = 1e-5, 1e-6


def build(nc, x, ctx_tail, ctx_full, mask, mask_tail, g_xattn, g_ffn, norm_w, wq, wk, wv, wo, wg,
          gu_packed, gu_scales, dn_packed, dn_scales, identity, shifts, x1_dram, out):
    es = ExitStack()
    with es:
        def sem(name):
            return es.enter_context(nc.semaphore(name))

        def sb(stack, name, shape, dt):
            return stack.enter_context(nc.sbuf_tensor(name, shape, dt))

        ident = sb(es, "ident", [128, 128], F32)
        shift = sb(es, "shift", [128, 5], I32)
        normw = sb(es, "normw", [128, KT], F32)
        gates = sb(es, "gates", [128, 2], F32)
        tanhs = sb(es, "tanhs", [128, 2], F32)
        halfpow = sb(es, "halfpow", [128, 4], F32)
        coef_a = sb(es, "coef_a", [128, B], F32)
        headkeep = sb(es, "headkeep", [1, 1], I32)
        headmax = sb(es, "headmax", [1, 1], F32)
        stats = sb(es, "stats", [128, 4, 6], F32)
        mv = sb(es, "mv", [128, 4, 2], F32)
        var = sb(es, "var", [128, 4], F32)
        rstd = sb(es, "rstd", [128, 4], F32)

        phase_a, phase_b, setup_a = ExitStack(), ExitStack(), ExitStack()
        W = {}

        def weight(name):
            W[name] = [sb(phase_a, f"{name}_{half}", [128, KT, D], F32R) for half in ("hi", "lo")]

        weight("wv")
        ctx_raw = sb(phase_a, "ctx_raw", [128, KT, KC], F32)
        xn = sb(phase_a, "xn", [L, NB, D], F32)
        weight("wk")
        ctxT = [sb(phase_a, f"ctxT_{half}", [128, KT, KC], F32R) for half in ("hi", "lo")]
        weight("wq")
        weight("wg")
        xT = [sb(phase_a, f"xT_{half}", [128, KT, GT], F32R) for half in ("hi", "lo")]
        kblk = [[sb(phase_a, f"kblk{s}_{half}", [128, HPG, KC], F32R) for half in ("hi", "lo")] for s in range(2)]
        vv = [sb(phase_a, f"v_{half}", [128, NB, D], F32R) for half in ("hi", "lo")]
        qT = [[sb(phase_a, f"qT{s}_{half}", [128, GT], F32R) for half in ("hi", "lo")] for s in range(2)]
        mbias = sb(phase_a, "mbias", [128, B, TAIL], BF16)
        ones = sb(phase_a, "ones", [128, L], BF16)
        nmax = sb(phase_a, "nmax", [L, 4, HPG], F32)
        rsum = sb(phase_a, "rsum", [L, 4, HPG], F32)
        rinv = sb(phase_a, "rinv", [L, 4, HPG], F32)
        probs = [sb(phase_a, f"probs{s}", [L, HPG, TAIL], F32) for s in range(2)]
        pT = [[sb(phase_a, f"pT{s}_{half}", [128, HPG, L], F32R) for half in ("hi", "lo")] for s in range(2)]
        flags = sb(phase_a, "flags", [B, 2], F32)
        flagdiag = sb(phase_a, "flagdiag", [B, 2, B], BF16)
        weight("wo")
        xa = sb(phase_a, "xa", [L, 2, D], F32)
        raw = [sb(setup_a, f"raw{s}", [128, KT, D], F32) for s in range(2)]
        maskall = sb(setup_a, "maskall", [B, M], U8)
        masktail = sb(setup_a, "masktail", [1, B, TAIL], U8)
        setup_a.close()
        oT = [sb(phase_a, f"oT_{half}", [128, HG, GT], F32R) for half in ("hi", "lo")]
        gate = [sb(phase_a, f"gate{b}", [L, D], F32) for b in range(NB)]
        maskrow = sb(phase_a, "maskrow", [1, KC], U8)
        nmax_c = sb(phase_a, "nmax_c", [L, CHUNKS, HPG], F32)
        rsum_c = sb(phase_a, "rsum_c", [L, CHUNKS, HPG], F32)
        probs_full = xn[:, 1:NB, :].rearrange("t b d -> t (b d)").rearrange("t (h k) -> t h k", h=HPG)
        mbias_full = mbias[:, 0:NB, :].rearrange("p b k -> p (b k)")
        phase_a.close()
        words = [sb(phase_b, f"words{s}", [128, D], I32) for s in range(2)]
        scale = [sb(phase_b, f"scale{s}", [128, D], F16) for s in range(2)]
        scale_a = sb(phase_b, "scale_a", [128, D], F16)
        scale_b = [sb(phase_b, f"scale_b{s}", [128, D], F16) for s in range(2)]
        shifted = sb(phase_b, "shifted", [128, D], I32)
        fp4 = [sb(phase_b, f"fp4_{s}", [128, D], I32) for s in range(2)]
        wgu = [[sb(phase_b, f"wgu{t}_{half}", [128, KT, 256], F32R) for half in ("hi", "lo")] for t in range(FT)]
        xb = [sb(phase_b, "xb0", [128, 3, D], F32)]
        mT = [sb(phase_b, f"mT_{half}", [128, KT, TG], F32R) for half in ("hi", "lo")]
        mn = [sb(phase_b, f"mn{s}", [128, D], F32) for s in range(2)]
        hT = [sb(phase_b, f"hT_{half}", [128, FT, TG], F32R) for half in ("hi", "lo")]
        tgate = sb(phase_b, "tgate", [128, TG], F32)
        hidden = [sb(phase_b, f"hidden{s}", [128, TG], F32) for s in range(2)]
        wdn = [[sb(phase_b, f"wdn{c}_{half}", [128, 2 if c < 5 else 1, D], F32R) for half in ("hi", "lo")] for c in range(6)]
        xb.append(sb(phase_b, "xb1", [128, 3, D], F32))
        yo = [words[s][:, :].bitcast(F32) for s in range(2)]
        ssq = sb(phase_b, "ssq", [128, 2], F32)
        ms = sb(phase_b, "ms", [128, 2], F32)
        rrms = sb(phase_b, "rrms", [128, 2], F32)
        coef_y = sb(phase_b, "coef_y", [128, 2], F32)
        phase_b.close()

        bank = [es.enter_context(nc.psum_tensor(f"bank{i}", [128, 512], F32)) for i in range(8)]
        PJ, SC, PT, PV = bank[0:2], bank[2:4], bank[4:6], bank[6:8]
        FLAGS = bank[7]

        s_const = sem("consts_loaded")
        s_mask = sem("masks_loaded")
        s_normw = sem("norm_w_loaded")
        s_w = [sem(f"weight_loaded{s}") for s in range(2)]
        s_x = [sem(f"x_loaded{b}") for b in range(NB)]
        s_x1st = [sem(f"x1_stored{b}") for b in range(NB)]
        s_ctx = sem("ctx_loaded")
        s_split = sem("weights_split_hi")
        s_splitlo = sem("weights_split_lo")
        s_zero = sem("kblk_zeroed")
        s_setup = sem("dve_setup")
        s_tanh = sem("gates_tanh")
        s_flags = sem("flags_spread")
        s_pconst = sem("pool_consts")
        s_ctxhi, s_ctxlo = sem("ctx_hi_done"), sem("ctx_lo_done")
        s_ln = sem("ln_chain")
        s_pow = sem("rstd_ready")
        s_xn = sem("xn_ready")
        s_xa = [sem(f"residual_loaded{s}") for s in range(2)]
        s_pj, s_pjhi, s_pjlo = sem("projected"), sem("projection_hi"), sem("projection_lo")
        s_g, s_o = sem("gate_projected"), sem("out_projected")
        s_sc, s_max, s_exp, s_inv, s_norm = (sem(n) for n in ("scores_ready", "max_ready", "exp_done", "inverse_ready", "probs_normed"))
        s_pt, s_pthi, s_ptlo = sem("probsT_ready"), sem("probsT_hi"), sem("probsT_lo")
        s_pv, s_ohi, s_olo = sem("attn_ready"), sem("attn_hi"), sem("attn_lo")
        s_gate, s_gated, s_x1 = sem("gate_ready"), sem("gated_ready"), sem("x1_ready")
        f_load, f_ctxhi, f_ctx, f_bias = sem("full_loaded"), sem("full_ctx_hi"), sem("full_ctx_split"), sem("full_bias")
        f_ln, f_pow, f_xn = sem("full_ln_chain"), sem("full_rstd"), sem("full_xn_ready")
        f_pj, f_pjhi, f_pjlo = sem("full_projected"), sem("full_projection_hi"), sem("full_projection_lo")
        f_sc, f_maxc, f_max, f_exp, f_sum, f_inv, f_norm = (sem(f"full_{n}") for n in (
            "scores_ready", "max_chain", "max_ready", "exp_done", "sum_chain", "inverse_ready", "probs_normed"))
        f_pt, f_pthi, f_ptlo = sem("full_probsT_ready"), sem("full_probsT_hi"), sem("full_probsT_lo")
        f_pv, f_ohi, f_olo = sem("full_attn_ready"), sem("full_attn_hi"), sem("full_attn_lo")
        f_g, f_o, f_gate, f_gated, f_x1, f_st = (sem(f"full_{n}") for n in (
            "gate_projected", "out_projected", "gate_ready", "gated_ready", "x1_ready", "x1_stored"))
        s_apart = sem("waits_apart")
        s_pa = sem("full_path_done")
        s_stored = sem("x1_all_stored")
        s_words = [sem(f"words_loaded{s}") for s in range(2)]
        s_dq = sem("dequant_chain")
        s_dec = sem("piece_decoded")
        s_whi, s_wlo = sem("ffn_weight_hi"), sem("ffn_weight_lo")
        s_xb = [sem(f"x1_loaded{s}") for s in range(2)]
        s_bln, s_bpow, s_mn = sem("ffn_ln_chain"), sem("ffn_rstd"), sem("mn_ready")
        s_mt, s_mthi, s_mtlo = sem("mT_ready"), sem("mT_hi"), sem("mT_lo")
        s_gu, s_tg, s_sg, s_h, s_hhi, s_hlo = (sem(n) for n in ("gate_up_ready", "tanh_gate", "silu_gate", "hidden_ready", "hidden_hi", "hidden_lo"))
        s_y, s_sq, s_ms, s_rr, s_cy, s_yo = (sem(n) for n in ("y_ready", "y_squared", "mean_square", "rrms_ready", "coef_ready", "out_ready"))
        s_out = [sem(f"out_stored{s}") for s in range(2)]

        block = es.enter_context(nc.Block())

        HI, LO = 0, 1

        def wait_apart(engine, semaphore, value):
            engine.wait_ge(semaphore, value)
            engine.sem_inc(s_apart, 1)

        def words_loaded(n):
            return sum(16 * (4 if m < FT else (5 if m - FT < 5 else 2)) for m in range(n % 2, n + 1, 2))

        def piece_operands(n, half):
            codes = fp4[n % 2][:, :].bitcast(F16)
            factor = scale_a if half == HI else scale_b[n % 2]
            if n < FT:
                return (wgu[n][half][:, :, :].rearrange("p (two r) c -> p two r c", two=2),
                        codes.rearrange("p (r c two) -> p two r c", r=2, two=2),
                        factor[:, 0:256].unsqueeze(1).unsqueeze(1).broadcast_to([128, 2, 2, 256]))
            tiles = 2 if n < PIECES - 1 else 1
            return (wdn[n - FT][half][:, :, :], codes.rearrange("p (c two) -> p two c", two=2)[:, 0:tiles, :],
                    factor[:, :].unsqueeze(1).broadcast_to([128, tiles, D]))

        def phase_barrier(engine):
            engine.sem_inc(s_pa, 1)
            engine.wait_ge(s_pa, 5)

        PASSES = ((HI, HI), (HI, LO), (LO, HI))

        def product(out_ap, lhs, rhs, tiles, first=True):
            last = None
            for t in range(tiles):
                for p, (a, b) in enumerate(PASSES):
                    last = nc.tensor.matmul(out_ap, lhs(a, t), rhs(b, t), start=first and t == 0 and p == 0,
                                            stop=t == tiles - 1 and p == 2)
            return last

        CYCLE = ["X0", "X1", "X2", "X3", "Q0", "K0", "V0", "V1", "O0", "V2", "O1", "K1", "O2", "Q1", "O3", "V3",
                 "G0", "K2", "Q2", "G1", "K3", "Q3", "G2", "G3"]
        SPLIT_JOBS = [n for n in CYCLE if n[0] in "VKXQ"]
        HEAD = ["X0", "X1", "X2", "X3", "Q0", "K0", "V0", "V1", "V2"]
        BESIDE = {0: ["K1", "O2"], 1: ["Q1", "O3"], 2: ["V3", "G0"], 3: ["K2"], 4: ["Q2"], 5: ["G1"], 6: ["K3"], 7: ["Q3"],
                  8: ["G2", "X0"], 9: ["G3", "X1"], 10: ["X2", "X3"], 11: ["Q0"], 12: ["K0"], 13: ["V0"],
                  14: ["V1", "O0"], 15: ["V2", "O1"]}
        LOOP_FROM, NEXT_FROM = 4, 8
        AHEAD = 2
        EARLY_AT = {4: 0, **{i: i - 6 for i in range(7, STEPS)}}
        EARLY = len(EARLY_AT)
        def job_bank(name):
            return PJ[CYCLE.index(name) % 2]

        def split_count(c, name):
            return len(SPLIT_JOBS) * c + SPLIT_JOBS.index(name) + 1

        def exists(c, name):
            return not isinstance(c, int) or (1 <= c if name[0] == "O" else 0 <= c < GROUPS)

        def before_in_bank(c, name):
            at = CYCLE.index(name) - 2
            while True:
                if at < 0:
                    at, c = at + len(CYCLE), c - 1
                if isinstance(c, int) and c < 0:
                    return None
                if exists(c, CYCLE[at]):
                    return c, CYCLE[at]
                at -= 2

        def beside(g, i):
            jobs = [(g + 1 if i >= NEXT_FROM and n[0] != "G" else g, n) for n in BESIDE[i]]
            return [job for job in jobs if exists(*job)]

        def step_ahead(g, i):
            g, i = (g, i + AHEAD) if i + AHEAD < STEPS else (g + 1, i + AHEAD - STEPS)
            return [(g, i)] if not isinstance(g, int) or g < GROUPS else []

        def last_step(g, i):
            return (g, i - 1) if i else (g - 1, STEPS - 1)

        def wants_full(engine):
            engine.wait_ge(s_setup, SETUP)
            return engine.value_load(headkeep[0:1, 0:1], min_val=0, max_val=1)

        FULL_JOBS = [f"V{c}" for c in range(CHUNKS)] + ["X"] + [f"{k}{hg}" for hg in range(HG) for k in "KQ"]

        def full_count(b, name):
            return len(FULL_JOBS) * b + FULL_JOBS.index(name) + 1

        SETUP = 10

        FJ, FSC, FPT, FPV, FO = bank[0], bank[2:5], bank[5], bank[6], bank[7]

        @block.sync
        def _(sp):
            for b in range(NB):
                sp.dma_start(xn[:, b, :], x[b]).then_inc(s_x[b], 16)
            sp.dma_start(normw[:, :], norm_w).then_inc(s_normw, 16)

            def load_weight(n, w):
                if n >= 2:
                    sp.wait_ge(s_splitlo, n - 1)
                sp.dma_start(raw[n % 2][:, :, :], w.rearrange("(k p) n -> p k n", p=128)).then_inc(s_w[n % 2], 16)

            load_weight(0, wq)
            sp.dma_start(ident[:, :], identity).then_inc(s_const, 16)
            sp.dma_start(maskall[:, :], mask).then_inc(s_mask, 16)
            sp.dma_start(masktail[:, :, :], mask_tail.unsqueeze(0)).then_inc(s_mask, 16)
            sp.dma_start(gates[:, 0:1], g_xattn.unsqueeze(0).broadcast_to([128, 1])).then_inc(s_const, 16)
            sp.dma_start(gates[:, 1:2], g_ffn.unsqueeze(0).broadcast_to([128, 1])).then_inc(s_const, 16)
            sp.dma_start(shift[:, :], shifts).then_inc(s_const, 16)
            sp.dma_start(ctx_raw[:, :, :], ctx_tail[0]).then_inc(s_ctx, 16)
            for n, w in ((1, wk), (2, wv), (3, wg), (4, wo)):
                load_weight(n, w)

            def load_residual(g, b):
                sp.dma_start(xa[:, b % 2, :], x[bass.ds(NB * g + b, 1)].rearrange("o t d -> (o t) d")).then_inc(s_xa[b % 2], 16)

            def load_next(g):
                for b in range(NB):
                    sp.wait_ge(s_pj, split_count(g, f"X{b}"))
                    sp.dma_start(xn[:, b, :], x[bass.ds(NB * (g + 1) + b, 1)].rearrange("o t d -> (o t) d")).then_inc(s_x[b], 16)
                sp.wait_ge(s_ctxlo, KT * (g + 1))
                sp.dma_start(ctx_raw[:, :, :], ctx_tail[bass.ds(g + 1, 1)].rearrange("o p k c -> (o p) k c")).then_inc(s_ctx, 16)

            def outputs(g, last):
                for b in range(NB):
                    if last and b < 3:
                        load_piece(EARLY - 1 + b)
                    sp.wait_ge(s_x1, NB * g + b + 1)
                    sp.dma_start(x1_dram[bass.ds(NB * g + b, 1)].rearrange("o t d -> (o t) d"), gate[b][:, :])\
                      .then_inc(s_x1st[b], 16)
                    if b + 2 < NB:
                        load_residual(g, b + 2)
                    elif not last:
                        load_residual(g + 1, b - 2)

            def load_piece(n):
                s = n % 2
                if n >= 2:
                    sp.wait_ge(s_dec, n - 1)
                if n < FT:
                    cols = slice(256 * n, 256 * n + 256)
                    for half in range(2):
                        p = slice(64 * half, 64 * half + 64)
                        sp.dma_start(words[s][p, 0:256], gu_packed[:, cols]).then_inc(s_words[s], 16)
                        sp.dma_start(scale[s][p, 0:256], gu_scales[:, cols].unsqueeze(1).broadcast_to([4, 16, 256]))\
                          .then_inc(s_words[s], 16)
                else:
                    c = n - FT
                    rep, nw = (4, 32) if c < 5 else (8, 16)
                    sp.dma_start(words[s][:, :], dn_packed[32 * c:32 * c + nw, :].unsqueeze(0).broadcast_to([rep, nw, D]))\
                      .then_inc(s_words[s], 16)
                    if c < 5:
                        for r in range(rep):
                            sp.dma_start(scale[s][32 * r:32 * r + 32, :],
                                         dn_scales[2 * c:2 * c + 2, :].unsqueeze(1).broadcast_to([2, 16, D]))\
                              .then_inc(s_words[s], 16)
                    else:
                        sp.dma_start(scale[s][:, :], dn_scales[10:11, :].broadcast_to([128, D])).then_inc(s_words[s], 16)

            x1_flat = x1_dram.rearrange("b t d -> (b t) d")
            out_flat = out.rearrange("b t d -> (b t) d")

            def load_x1(j, slot):
                sp.dma_start(xb[slot][:, 0:2, :], x1_flat[bass.ds(TG * j, 256), :].rearrange("(m p) d -> p m d", p=128))\
                  .then_inc(s_xb[slot], 16)
                sp.dma_start(xb[slot][0:64, 2, :], x1_flat[bass.ds(TG * j + 256, 64), :]).then_inc(s_xb[slot], 16)

            def full_loads(b):
                sp.dma_start(ctx_raw[:, :, 0:M], ctx_full[bass.ds(b, 1)].rearrange("o k p c -> p (o k) c")).then_inc(f_load, 16)
                sp.dma_start(xa[:, 0, :], x[bass.ds(b, 1)].rearrange("o t d -> (o t) d")).then_inc(f_load, 16)
                sp.dma_start(maskrow[:, 0:M], mask[bass.ds(b, 1), :]).then_inc(f_load, 16)

            def full_store(b):
                sp.wait_ge(f_x1, b + 1)
                sp.dma_start(x1_dram[bass.ds(b, 1)].rearrange("o t d -> (o t) d"), xa[:, 0, :]).then_inc(f_st, 16)
                sp.wait_ge(f_st, 16 * (b + 1))

            with sp.If(wants_full(sp)):
                sp.wait_ge(s_pjlo, len(HEAD))
                full_loads(0)
                with sp.Fori(0, B - 1) as b:
                    full_store(b)
                    full_loads(b + 1)
                full_store(B - 1)
                phase_barrier(sp)
                for n in range(EARLY + 2):
                    load_piece(n)
                load_x1(0, 0)
            with sp.Else():
                for b in range(NB):
                    sp.sem_inc(s_x1st[b], 16)
                for b in range(2):
                    load_residual(0, b)
                with sp.Fori(0, GROUPS - 1) as g:
                    load_next(g)
                    outputs(g, False)
                sp.wait_ge(s_pj, split_count(GROUPS - 1, "V3"))
                for n in range(EARLY - 1):
                    load_piece(n)
                sp.wait_ge(s_sc, STEPS * (GROUPS - 1) + 12)
                for b in range(NB):
                    sp.wait_ge(s_x1st[b], 32)
                load_x1(0, 0)
                outputs(GROUPS - 1, True)
                for b in range(NB):
                    sp.wait_ge(s_x1st[b], 16 * (GROUPS + 1))
            sp.sem_inc(s_stored, 1)

            for s in range(2):
                sp.sem_inc(s_out[s], 16)

            def store_tiles(h, par):
                j = 2 * h + par
                for m, rows in enumerate(ROWS):
                    slot = (par + m) % 2
                    sp.wait_ge(s_yo, 3 * j + m + 3)
                    sp.dma_start(out_flat[bass.ds(TG * j + 128 * m, rows), :], yo[slot][0:rows, :])\
                      .then_inc(s_out[slot], 16)

            for n in range(EARLY + 2, PIECES):
                load_piece(n)
            with sp.Fori(0, (FGROUPS - 1) // 2) as h:
                for par in range(2):
                    load_x1(2 * h + par + 1, (par + 1) % 2)
                    store_tiles(h, par)
            store_tiles((FGROUPS - 1) // 2, 0)
            for s in range(2):
                sp.wait_ge(s_out[s], 16 * ((3 * FGROUPS + 1 - s) // 2 + 1))

        @block.gpsimd
        def _(pool):
            nc.gpsimd.memset(halfpow[:, :], -0.5).then_inc(s_pconst, 1)
            nc.gpsimd.memset(ones[:, :], 1.0).then_inc(s_pconst, 1)
            for s in range(2):
                for half in range(2):
                    nc.gpsimd.memset(kblk[s][half][:, :, :].bitcast(F32), 0.0).then_inc(s_zero, 1)

            def ctx_lo(g, k):
                pool.wait_ge(s_ctxhi, KT * g + k + 1)
                nc.gpsimd.tensor_tensor(ctxT[LO][:, k, :], ctx_raw[:, k, :], ctxT[HI][:, k, :].bitcast(F32),
                                        ALU.subtract).then_inc(s_ctxlo, 1)

            def layer_pow(g, b):
                pool.wait_ge(s_ln, 3 * (NB * g + b) + 3)
                nc.gpsimd.tensor_tensor(rstd[0:L, b:b + 1], var[0:L, b:b + 1], halfpow[0:L, b:b + 1], ALU.pow)\
                  .then_inc(s_pow, 1)

            def normalise_probs(g, i):
                n = STEPS * g + i
                pool.wait_ge(s_inv, n + 1)
                nc.gpsimd.tensor_tensor(probs[i % 2][:, :, :], probs[i % 2][:, :, :],
                                        rinv[:, i % 4, :].unsqueeze(2).broadcast_to([L, HPG, TAIL]), ALU.mult)\
                  .then_inc(s_norm, 1)

            def step(g, i, last=False):
                for ahead in step_ahead(g, i):
                    normalise_probs(*ahead)
                if last:
                    piece_lo(EARLY_AT[i]) if i in EARLY_AT else None
                if not last and 4 <= i < 4 + NB:
                    layer_pow(g + 1, i - 4)
                if not last and 8 <= i < 8 + KT:
                    ctx_lo(g + 1, i - 8)

            pool.wait_ge(s_pconst, 2)
            for b in range(NB):
                layer_pow(0, b)
            for k in range(KT):
                ctx_lo(0, k)

            def piece_lo(n):
                pool.wait_ge(s_dec, n + 1)
                nc.gpsimd.tensor_tensor(*piece_operands(n, LO), ALU.mult).then_inc(s_wlo, 1)

            def ffn_rstd(j):
                pool.wait_ge(s_bln, 3 * j + 3)
                nc.gpsimd.tensor_tensor(rstd[:, 0:3], var[:, 0:3], halfpow[:, 0:3], ALU.pow).then_inc(s_bpow, 1)

            with pool.If(wants_full(pool)):
                pool.wait_ge(s_zero, 4)
                with pool.Fori(0, B) as b:
                    pool.wait_ge(f_ln, 3 * b + 3)
                    nc.gpsimd.tensor_tensor(rstd[0:L, 0:1], var[0:L, 0:1], halfpow[0:L, 0:1], ALU.pow).then_inc(f_pow, 1)
                    for hg in range(HG):
                        pool.wait_ge(f_inv, HG * b + hg + 1)
                        nc.gpsimd.tensor_tensor(probs_full, probs_full, rinv[:, 0, :].unsqueeze(2).broadcast_to([L, HPG, KC]),
                                                ALU.mult).then_inc(f_norm, 1)
                pool.wait_ge(f_norm, HG * B)
                phase_barrier(pool)
                for n in range(EARLY):
                    piece_lo(n)
                ffn_rstd(0)
            with pool.Else():
                for i in range(AHEAD):
                    normalise_probs(0, i)
                for i in range(LOOP_FROM):
                    step(0, i)
                with pool.Fori(0, GROUPS - 1) as g:
                    for i in range(LOOP_FROM, STEPS):
                        step(g, i)
                    for i in range(LOOP_FROM):
                        step(g + 1, i)
                for i in range(LOOP_FROM, STEPS):
                    step(GROUPS - 1, i, True)
                ffn_rstd(0)
            def hidden_lo(j, par, t):
                pool.wait_ge(s_hhi, FT * j + t + 1)
                nc.gpsimd.tensor_tensor(hT[LO][:, t, :], hidden[(par + t) % 2][:, :], hT[HI][:, t, :].bitcast(F32),
                                        ALU.subtract).then_inc(s_hlo, 1)

            def rms_tiles(j, par):
                for m in range(3):
                    slot = (par + m) % 2
                    pool.wait_ge(s_ms, 3 * j + m + 1)
                    nc.gpsimd.tensor_tensor(rrms[0:ROWS[m], slot:slot + 1], ms[0:ROWS[m], slot:slot + 1],
                                            halfpow[0:ROWS[m], 0:1], ALU.pow).then_inc(s_rr, 1)

            piece_lo(EARLY)
            for t in range(FT):
                if EARLY + 1 + t < PIECES:
                    piece_lo(EARLY + 1 + t)
                hidden_lo(0, 0, t)
            with pool.Fori(0, (FGROUPS - 1) // 2) as h:
                for par in range(2):
                    ffn_rstd(2 * h + par + 1)
                    rms_tiles(2 * h + par, par)
                    for t in range(FT):
                        hidden_lo(2 * h + par + 1, (par + 1) % 2, t)
            rms_tiles(FGROUPS - 1, 0)

        @block.scalar
        def _(act):
            def split_hi(n, name):
                w = raw[n % 2]
                act.wait_ge(s_w[n % 2], 16 * (n // 2 + 1))
                for k in range(KT):
                    if name in ("wq", "wg"):
                        last = nc.scalar.activation(W[name][HI][:, k, :], w[:, k, :], ACT.Copy, scale=normw[:, k:k + 1])
                    else:
                        last = nc.scalar.activation(W[name][HI][:, k, :], w[:, k, :], ACT.Copy)
                last.then_inc(s_split, 1)

            def ctx_hi(g, k):
                if k == 0:
                    act.wait_ge(s_ctx, 16 * (g + 1))
                    if not isinstance(g, int) or g:
                        act.wait_ge(s_pj, split_count(g - 1, "K3"))
                nc.scalar.activation(ctxT[HI][:, k, :], ctx_raw[:, k, :], ACT.Copy).then_inc(s_ctxhi, 1)

            def job_hi(c, name):
                n = int(name[1])
                src = job_bank(name)
                if name[0] == "G":
                    act.wait_ge(s_g, NB * c + n + 1)
                    if not isinstance(c, int) or c:
                        act.wait_ge(s_x1st[n], 16 * c + 16)
                    nc.scalar.activation(gate[n][:, :], src[0:L, :], ACT.Tanh, scale=0.5).then_inc(s_gate, 1)
                    return
                act.wait_ge(s_pj, split_count(c, name))
                if name[0] == "V":
                    last = nc.scalar.activation(vv[HI][0:TAIL, n, :], src[0:TAIL, :], ACT.Copy)
                elif name[0] == "X":
                    last = nc.scalar.activation(xT[HI][:, :, L * n:L * n + L],
                                                src[:, 0:KT * L].rearrange("p (k t) -> p k t", k=KT), ACT.Copy)
                elif name[0] == "Q":
                    last = nc.scalar.activation(qT[n % 2][HI][:, :], src[:, 0:GT], ACT.Copy, scale=HD ** -0.5)
                else:
                    for h in range(HPG):
                        p = slice(HD * h, HD * h + HD)
                        last = nc.scalar.activation(kblk[n % 2][HI][p, h, :], src[p, 0:KC], ACT.Copy)
                last.then_inc(s_pjhi, 1)

            def exp_step(g, i):
                n = STEPS * g + i
                act.wait_ge(s_max, n + 1)
                if not isinstance(n, int) or n >= 2:
                    act.wait_ge(s_pt, n - 1)
                for h in range(HPG):
                    last = nc.scalar.activation(probs[i % 2][:, h, :], SC[i % 2][0:L, TAIL * h:TAIL * h + TAIL], ACT.Exp,
                                                bias=nmax[:, i % 4, h:h + 1], accum_out=rsum[:, i % 4, h:h + 1])
                last.then_inc(s_exp, 1)

            def probsT_hi(g, i):
                n = STEPS * g + i
                act.wait_ge(s_pt, n + 1)
                if not isinstance(n, int) or n >= 2:
                    act.wait_ge(s_pv, n - 1)
                nc.scalar.activation(pT[i % 2][HI][0:TAIL, :, :].rearrange("k h t -> k (h t)"), PT[i % 2][0:TAIL, 0:GT],
                                     ACT.Copy).then_inc(s_pthi, 1)

            def attn_hi(g, i):
                hg, b = i // NB, i % NB
                act.wait_ge(s_pv, STEPS * g + i + 1)
                for h in range(HPG):
                    p = slice(HD * h, HD * h + HD)
                    last = nc.scalar.activation(oT[HI][p, hg, L * b:L * b + L], PV[i % 2][p, L * h:L * h + L], ACT.Copy)
                last.then_inc(s_ohi, 1)

            def step(g, i, last=False):
                probsT_hi(g, i)
                if not isinstance(g, int) or g or i:
                    attn_hi(*last_step(g, i))
                for ahead in step_ahead(g, i):
                    exp_step(*ahead)
                for job in beside(g, i):
                    if job[1][0] != "O":
                        job_hi(*job)
                if not last and 8 <= i < 8 + KT:
                    ctx_hi(g + 1, i - 8)

            act.wait_ge(s_normw, 16)
            split_hi(0, "wq")
            for b in range(NB):
                job_hi(0, f"X{b}")
            act.wait_ge(s_const, 16 * CONSTS)
            nc.scalar.activation(tanhs[:, :], gates[:, :], ACT.Tanh).then_inc(s_tanh, 1)
            for k in range(KT):
                ctx_hi(0, k)
            split_hi(1, "wk")
            job_hi(0, "Q0")
            split_hi(2, "wv")
            act.wait_ge(s_zero, 4)
            job_hi(0, "K0")
            split_hi(3, "wg")
            job_hi(0, "V0")
            job_hi(0, "V1")
            job_hi(0, "V2")
            split_hi(4, "wo")

            def full_hi(b, name):
                act.wait_ge(f_pj, full_count(b, name))
                n = int(name[1:] or 0)
                if name[0] == "V":
                    last = nc.scalar.activation(vv[HI][:, n, :], FJ[:, :], ACT.Copy)
                elif name[0] == "X":
                    last = nc.scalar.activation(xT[HI][:, :, 0:L], FJ[:, 0:KT * L].rearrange("p (k t) -> p k t", k=KT), ACT.Copy)
                elif name[0] == "Q":
                    last = nc.scalar.activation(qT[0][HI][:, 0:L], FJ[:, 0:L], ACT.Copy, scale=HD ** -0.5)
                else:
                    for h in range(HPG):
                        p = slice(HD * h, HD * h + HD)
                        last = nc.scalar.activation(kblk[0][HI][p, h, :], FJ[p, 0:KC], ACT.Copy)
                last.then_inc(f_pjhi, 1)

            with act.If(wants_full(act)):
                act.wait_ge(s_pjlo, len(HEAD))
                act.wait_ge(s_splitlo, 5)
                with act.Fori(0, B) as b:
                    act.wait_ge(f_load, 48 * b + 48)
                    for k in range(KT):
                        last = nc.scalar.activation(ctxT[HI][:, k, 0:M], ctx_raw[:, k, 0:M], ACT.Copy)
                    last.then_inc(f_ctxhi, 1)
                    for name in FULL_JOBS[0:CHUNKS + 1]:
                        full_hi(b, name)
                    for hg in range(HG):
                        i = HG * b + hg
                        full_hi(b, f"K{hg}")
                        full_hi(b, f"Q{hg}")
                        act.wait_ge(f_max, i + 1)
                        for c in range(CHUNKS):
                            for h in range(HPG):
                                last = nc.scalar.activation(probs_full[:, h, CHUNK * c:CHUNK * c + CHUNK],
                                                            FSC[c][0:L, CHUNK * h:CHUNK * h + CHUNK], ACT.Exp,
                                                            bias=nmax[:, 0, h:h + 1], accum_out=rsum_c[:, c, h:h + 1])
                        last.then_inc(f_exp, 1)
                        for c in range(CHUNKS):
                            act.wait_ge(f_pt, CHUNKS * i + c + 1)
                            if c:
                                act.wait_ge(f_pv, CHUNKS * i + c)
                            nc.scalar.activation(pT[0][HI][:, :, :].rearrange("k h t -> k (h t)"), FPT[:, 0:GT], ACT.Copy)\
                              .then_inc(f_pthi, 1)
                        act.wait_ge(f_pv, CHUNKS * i + CHUNKS)
                        for h in range(HPG):
                            p = slice(HD * h, HD * h + HD)
                            last = nc.scalar.activation(oT[HI][p, hg, 0:L], FPV[p, L * h:L * h + L], ACT.Copy)
                        last.then_inc(f_ohi, 1)
                    act.wait_ge(f_g, b + 1)
                    nc.scalar.activation(gate[0][:, :], FJ[0:L, :], ACT.Tanh, scale=0.5).then_inc(f_gate, 1)
                act.wait_ge(f_gate, B)
                phase_barrier(act)
            with act.Else():
                for i in range(AHEAD):
                    exp_step(0, i)
                act.wait_ge(s_splitlo, 5)
                for i in range(LOOP_FROM):
                    step(0, i)
                with act.Fori(0, GROUPS - 1) as g:
                    for i in range(LOOP_FROM, STEPS):
                        step(g, i)
                    for i in range(LOOP_FROM):
                        step(g + 1, i)
                for i in range(LOOP_FROM, STEPS):
                    step(GROUPS - 1, i, True)
                attn_hi(GROUPS - 1, STEPS - 1)

            def mT_hi(j, par, m):
                n = 3 * j + m
                bank_t = bank[4 + (par + m) % 2]
                act.wait_ge(s_mt, n + 1)
                rows = ROWS[m]
                nc.scalar.activation(mT[HI][:, :, 128 * m:128 * m + rows],
                                     bank_t[:, 0:KT * rows].rearrange("p (k t) -> p k t", k=KT), ACT.Copy).then_inc(s_mthi, 1)

            def gate_up(j, par, t):
                n = FT * j + t
                act.wait_ge(s_gu, n + 1)
                if not isinstance(n, int) or n:
                    act.wait_ge(s_sg, n)
                nc.scalar.activation(tgate[:, :], bank[2 * ((par + t) % 2)][:, 0:TG], ACT.Tanh, scale=0.5 * FP4_UNIT).then_inc(s_tg, 1)

            def hidden_hi(j, par, t):
                act.wait_ge(s_h, FT * j + t + 1)
                nc.scalar.activation(hT[HI][:, t, :], hidden[(par + t) % 2][:, :], ACT.Copy).then_inc(s_hhi, 1)

            def square(h, par, m):
                n, n_half = 3 * (2 * h + par) + m, 3 * h + (3 * par + m) // 2
                slot, rows = (par + m) % 2, ROWS[m]
                act.wait_ge(s_out[slot], 16 * (n_half + 1))
                act.wait_ge(s_y, n + 1)
                return nc.scalar.activation(yo[slot][0:rows, :], bank[6 + slot][0:rows, :], ACT.Square,
                                            accum_out=ssq[0:rows, slot:slot + 1]).then_inc(s_sq, 1)

            def all_gate_up(j, par):
                for t in range(FT):
                    gate_up(j, par, t)
                    if t >= 1:
                        hidden_hi(j, par, t - 1)
                hidden_hi(j, par, FT - 1)

            for m in range(3):
                mT_hi(0, 0, m)
            all_gate_up(0, 0)
            act.wait_ge(s_stored, 1)
            with act.Fori(0, (FGROUPS - 1) // 2) as h:
                for par in range(2):
                    j = 2 * h + par
                    for m in range(3):
                        square(h, par, m)
                        for tile in NEXT_TILES[m]:
                            mT_hi(j + 1, (par + 1) % 2, tile)
                    all_gate_up(j + 1, (par + 1) % 2)
            for m in range(3):
                square((FGROUPS - 1) // 2, 0, m)

        @block.vector
        def _(dve):
            nc.vector.memset(mv[:, :, :], 0.0).then_inc(s_setup, 1)
            nc.vector.memset(mbias[:, :, :], 0.0).then_inc(s_setup, 1)

            def split_lo(n, name):
                dve.wait_ge(s_split, n + 1)
                w = raw[n % 2]
                for k in range(KT):
                    hi = W[name][HI][:, k, :].bitcast(F32)
                    if name in ("wq", "wg"):
                        last = nc.vector.scalar_tensor_tensor(W[name][LO][:, k, :], w[:, k, :], normw[:, k:k + 1], hi,
                                                              ALU.mult, ALU.subtract)
                    else:
                        last = nc.vector.tensor_tensor(W[name][LO][:, k, :], w[:, k, :], hi, ALU.subtract)
                last.then_inc(s_splitlo, 1)

            def job_lo(c, name):
                n = int(name[1])
                dve.wait_ge(s_pjhi, split_count(c, name))
                src = job_bank(name)
                if name[0] == "V":
                    last = nc.vector.tensor_tensor(vv[LO][0:TAIL, n, :], src[0:TAIL, :], vv[HI][0:TAIL, n, :].bitcast(F32), ALU.subtract)
                elif name[0] == "X":
                    last = nc.vector.tensor_tensor(xT[LO][:, :, L * n:L * n + L], src[:, 0:KT * L].rearrange("p (k t) -> p k t", k=KT),
                                                   xT[HI][:, :, L * n:L * n + L].bitcast(F32), ALU.subtract)
                elif name[0] == "Q":
                    last = nc.vector.scalar_tensor_tensor(qT[n % 2][LO][:, :], src[:, 0:GT], HD ** -0.5,
                                                          qT[n % 2][HI][:, :].bitcast(F32), ALU.mult, ALU.subtract)
                else:
                    for h in range(HPG):
                        p = slice(HD * h, HD * h + HD)
                        last = nc.vector.tensor_tensor(kblk[n % 2][LO][p, h, :], src[p, 0:KC],
                                                       kblk[n % 2][HI][p, h, :].bitcast(F32), ALU.subtract)
                last.then_inc(s_pjlo, 1)

            def layer_stats(g, b):
                c = 3 * (NB * g + b)
                dve.wait_ge(s_x[b], 16 * (g + 1))
                nc.vector.bn_stats(stats[0:L, b, :], xn[:, b, :]).then_inc(s_ln, 1)
                wait_apart(dve, s_ln, c + 1)
                nc.vector.bn_aggr(mv[0:L, b, :], stats[0:L, b, :]).then_inc(s_ln, 1)
                dve.wait_ge(s_ln, c + 2)
                nc.vector.tensor_scalar(var[0:L, b:b + 1], mv[0:L, b, 1:2], 1.0 + RMS_EPS, LN_EPS * RMS_EPS, ALU.mult, ALU.add)\
                  .then_inc(s_ln, 1)

            def normalise(g, b):
                dve.wait_ge(s_pow, NB * g + b + 1)
                nc.vector.tensor_scalar(xn[:, b, :], xn[:, b, :], mv[0:L, b, 0:1], rstd[0:L, b:b + 1], ALU.subtract, ALU.mult)\
                  .then_inc(s_xn, 1)

            def row_max(g, i):
                n = STEPS * g + i
                dve.wait_ge(s_sc, n + 1)
                nc.vector.tensor_reduce(nmax[:, i % 4, :], SC[i % 2][0:L, 0:KC].rearrange("t (h k) -> t h k", h=HPG),
                                        AXIS_X, ALU.max, negate=True).then_inc(s_max, 1)

            def row_inverse(g, i):
                dve.wait_ge(s_exp, STEPS * g + i + 1)
                nc.vector.reciprocal(rinv[:, i % 4, :], rsum[:, i % 4, :]).then_inc(s_inv, 1)

            def probsT_lo(g, i):
                dve.wait_ge(s_pthi, STEPS * g + i + 1)
                nc.vector.tensor_tensor(pT[i % 2][LO][0:TAIL, :, :].rearrange("k h t -> k (h t)"), PT[i % 2][0:TAIL, 0:GT],
                                        pT[i % 2][HI][0:TAIL, :, :].rearrange("k h t -> k (h t)").bitcast(F32), ALU.subtract)\
                  .then_inc(s_ptlo, 1)

            def attn_lo(g, i):
                hg, b = i // NB, i % NB
                dve.wait_ge(s_ohi, STEPS * g + i + 1)
                for h in range(HPG):
                    p = slice(HD * h, HD * h + HD)
                    last = nc.vector.tensor_tensor(oT[LO][p, hg, L * b:L * b + L], PV[i % 2][p, L * h:L * h + L],
                                                   oT[HI][p, hg, L * b:L * b + L].bitcast(F32), ALU.subtract)
                last.then_inc(s_olo, 1)

            def output(g, b):
                n = NB * g + b
                dve.wait_ge(s_gate, n + 1)
                dve.wait_ge(s_o, n + 1)
                nc.vector.scalar_tensor_tensor(gate[b][:, :], gate[b][:, :], 1.0, job_bank(f"O{b}")[0:L, :],
                                               ALU.add, ALU.mult).then_inc(s_gated, 1)
                dve.wait_ge(s_gated, n + 1)
                dve.wait_ge(s_xa[b % 2], 32 * g + 16 * (b // 2 + 1))
                nc.vector.scalar_tensor_tensor(gate[b][:, :], gate[b][:, :], coef_a[0:L, bass.ds(n, 1)], xa[:, b % 2, :],
                                               ALU.mult, ALU.add).then_inc(s_x1, 1)

            def step(g, i, last=False):
                probsT_lo(g, i)
                for ahead in step_ahead(g, i):
                    row_max(*ahead)
                if not last and 4 <= i < 4 + NB:
                    layer_stats(g + 1, i - 4)
                if not isinstance(g, int) or g or i:
                    attn_lo(*last_step(g, i))
                if last and i in EARLY_AT:
                    decode(EARLY_AT[i])
                for ahead in step_ahead(g, i):
                    row_inverse(*ahead)
                if not last and 5 <= i < 5 + NB:
                    normalise(g + 1, i - 5)
                for c, name in beside(g, i):
                    if name[0] == "O":
                        output(c - 1, int(name[1]))
                    elif name[0] != "G":
                        job_lo(c, name)
                if last and i in EARLY_AT:
                    weights_hi(EARLY_AT[i])

            for b in range(NB):
                layer_stats(0, b)
            for b in range(NB):
                normalise(0, b)
            split_lo(0, "wq")
            for b in range(NB):
                job_lo(0, f"X{b}")
            dve.wait_ge(s_mask, 32)
            nc.vector.tensor_reduce(flags[:, 0:1], maskall[:, :], AXIS_X, ALU.max).then_inc(s_setup, 1)
            nc.vector.tensor_reduce(flags[:, 1:2], maskall[:, 0:M - TAIL], AXIS_X, ALU.max).then_inc(s_setup, 1)
            dve.wait_ge(s_const, 16 * CONSTS)
            dve.wait_ge(s_setup, 4)
            for f in range(2):
                nc.vector.tensor_scalar(flagdiag[:, f, :], ident[0:B, 0:B], flags[:, f:f + 1], None, ALU.mult).then_inc(s_setup, 1)
            nc.vector.tensor_scalar(mbias[0:1, :, :], masktail[:, :, :], 1.0, MASKED, ALU.subtract, ALU.mult).then_inc(s_setup, 1)
            split_lo(1, "wk")
            job_lo(0, "Q0")
            split_lo(2, "wv")
            dve.wait_ge(s_flags, 1)
            nc.vector.tensor_reduce(headmax[:, :], FLAGS[0:1, B:2 * B], AXIS_X, ALU.max).then_inc(s_setup, 1)
            dve.wait_ge(s_setup, 8)
            nc.vector.tensor_copy(headkeep[:, :], headmax[:, :]).then_inc(s_setup, 1)
            dve.wait_ge(s_tanh, 1)
            nc.vector.tensor_scalar(coef_a[0:L, :], FLAGS[0:L, 0:B], tanhs[0:L, 0:1], 0.5, ALU.mult, ALU.mult).then_inc(s_setup, 1)
            job_lo(0, "K0")
            split_lo(3, "wg")
            job_lo(0, "V0")
            job_lo(0, "V1")
            job_lo(0, "V2")
            split_lo(4, "wo")

            SIGN, MAGNITUDE = 0x80008000 - (1 << 32), 0x0E000E00

            def decode(n):
                s = n % 2
                cols = 256 if n < FT else D
                done = 5 * n
                if n >= 1:
                    dve.wait_ge(s_whi, n)
                if n >= 2:
                    dve.wait_ge(s_wlo, n - 1)
                dve.wait_ge(s_words[s], words_loaded(n))
                nc.vector.tensor_scalar(scale_a[:, 0:cols].bitcast(I16), scale[s][:, 0:cols].bitcast(I16), -2, None,
                                        ALU.bitwise_and).then_inc(s_dq, 1)
                if n < FT:
                    nc.vector.tensor_scalar(shifted[:, 0:256], words[s][:, 0:256], shift[:, 0:1], None, ALU.logical_shift_left)
                    last = nc.vector.tensor_scalar(shifted[:, 256:512], words[s][:, 0:256], shift[:, 1:2], None,
                                                   ALU.logical_shift_left)
                elif n < PIECES - 1:
                    last = nc.vector.tensor_scalar(shifted[:, :], words[s][:, :], shift[:, 2:3], None, ALU.logical_shift_left)
                else:
                    last = nc.vector.tensor_scalar(shifted[:, :], words[s][:, :], shift[:, 3:4], shift[:, 4:5],
                                                   ALU.logical_shift_right, ALU.logical_shift_left)
                last.then_inc(s_dq, 1)
                dve.wait_ge(s_dq, done + 2)
                nc.vector.tensor_scalar(fp4[s][:, :], shifted[:, :], 3, MAGNITUDE, ALU.logical_shift_right, ALU.bitwise_and)\
                  .then_inc(s_dq, 1)
                dve.wait_ge(s_dq, done + 3)
                nc.vector.scalar_tensor_tensor(fp4[s][:, :], shifted[:, :], SIGN, fp4[s][:, :], ALU.bitwise_and, ALU.bitwise_or)\
                  .then_inc(s_dq, 1)
                nc.vector.tensor_tensor(scale_b[s][:, 0:cols], scale[s][:, 0:cols], scale_a[:, 0:cols], ALU.subtract)\
                  .then_inc(s_dq, 1)
                dve.wait_ge(s_dq, done + 5)
                dve.sem_inc(s_dec, 1)

            def weights_hi(n):
                nc.vector.tensor_tensor(*piece_operands(n, HI), ALU.mult).then_inc(s_whi, 1)

            def ffn_stats(h, par):
                j = 2 * h + par
                dve.wait_ge(s_xb[par], 32 * (h + 1))
                for m, rows in enumerate(ROWS):
                    last = nc.vector.bn_stats(stats[0:rows, m, :], xb[par][0:rows, m, :])
                last.then_inc(s_bln, 1)
                wait_apart(dve, s_bln, 3 * j + 1)
                for m, rows in enumerate(ROWS):
                    last = nc.vector.bn_aggr(mv[0:rows, m, :], stats[0:rows, m, :])
                last.then_inc(s_bln, 1)
                dve.wait_ge(s_bln, 3 * j + 2)
                nc.vector.tensor_scalar(var[:, 0:3], mv[:, 0:3, 1], LN_EPS, None, ALU.add).then_inc(s_bln, 1)

            def ffn_normalise(j, par, m):
                rows = ROWS[m]
                dve.wait_ge(s_bpow, j + 1)
                if not isinstance(j, int) or m >= 2:
                    dve.wait_ge(s_mt, 3 * j + m - 1)
                nc.vector.tensor_scalar(mn[(par + m) % 2][0:rows, :].rearrange("t (e p) -> t p e", e=8),
                                        xb[par][0:rows, m, :].rearrange("t (p e) -> t p e", e=8), mv[0:rows, m, 0:1], rstd[0:rows, m:m + 1],
                                        ALU.subtract, ALU.mult).then_inc(s_mn, 1)

            def full_lo(b, name):
                dve.wait_ge(f_pjhi, full_count(b, name))
                n = int(name[1:] or 0)
                if name[0] == "V":
                    last = nc.vector.tensor_tensor(vv[LO][:, n, :], FJ[:, :], vv[HI][:, n, :].bitcast(F32), ALU.subtract)
                elif name[0] == "X":
                    last = nc.vector.tensor_tensor(xT[LO][:, :, 0:L], FJ[:, 0:KT * L].rearrange("p (k t) -> p k t", k=KT),
                                                   xT[HI][:, :, 0:L].bitcast(F32), ALU.subtract)
                elif name[0] == "Q":
                    last = nc.vector.scalar_tensor_tensor(qT[0][LO][:, 0:L], FJ[:, 0:L], HD ** -0.5, qT[0][HI][:, 0:L].bitcast(F32),
                                                          ALU.mult, ALU.subtract)
                else:
                    for h in range(HPG):
                        p = slice(HD * h, HD * h + HD)
                        last = nc.vector.tensor_tensor(kblk[0][LO][p, h, :], FJ[p, 0:KC], kblk[0][HI][p, h, :].bitcast(F32),
                                                       ALU.subtract)
                last.then_inc(f_pjlo, 1)

            with dve.If(wants_full(dve)):
                dve.wait_ge(s_pjlo, len(HEAD))
                for half in range(2):
                    nc.vector.memset(ctxT[half][:, :, M:KC].bitcast(F32), 0.0).then_inc(f_ctx, 1)
                nc.vector.memset(mbias_full[0:1, M:KC], -MASKED).then_inc(f_bias, 1)
                with dve.Fori(0, B) as b:
                    dve.wait_ge(f_load, 48 * b + 48)
                    nc.vector.tensor_scalar(mbias_full[0:1, 0:M], maskrow[:, 0:M], 1.0, MASKED, ALU.subtract, ALU.mult)\
                      .then_inc(f_bias, 1)
                    nc.vector.bn_stats(stats[0:L, 0, :], xa[:, 0, :]).then_inc(f_ln, 1)
                    wait_apart(dve, f_ln, 3 * b + 1)
                    nc.vector.bn_aggr(mv[0:L, 0, :], stats[0:L, 0, :]).then_inc(f_ln, 1)
                    dve.wait_ge(f_ln, 3 * b + 2)
                    nc.vector.tensor_scalar(var[0:L, 0:1], mv[0:L, 0, 1:2], 1.0 + RMS_EPS, LN_EPS * RMS_EPS, ALU.mult, ALU.add)\
                      .then_inc(f_ln, 1)
                    dve.wait_ge(f_pow, b + 1)
                    nc.vector.tensor_scalar(xn[:, 0, :], xa[:, 0, :], mv[0:L, 0, 0:1], rstd[0:L, 0:1], ALU.subtract, ALU.mult)\
                      .then_inc(f_xn, 1)
                    dve.wait_ge(f_ctxhi, b + 1)
                    for k in range(KT):
                        last = nc.vector.tensor_tensor(ctxT[LO][:, k, 0:M], ctx_raw[:, k, 0:M], ctxT[HI][:, k, 0:M].bitcast(F32),
                                                       ALU.subtract)
                    last.then_inc(f_ctx, 1)
                    for name in FULL_JOBS[0:CHUNKS + 1]:
                        full_lo(b, name)
                    for hg in range(HG):
                        i = HG * b + hg
                        full_lo(b, f"K{hg}")
                        full_lo(b, f"Q{hg}")
                        dve.wait_ge(f_sc, i + 1)
                        for c in range(CHUNKS):
                            nc.vector.tensor_reduce(nmax_c[:, c, :], FSC[c][0:L, :].rearrange("t (h k) -> t h k", h=HPG),
                                                    AXIS_X, ALU.max, negate=True).then_inc(f_maxc, 1)
                        dve.wait_ge(f_maxc, 4 * i + 3)
                        nc.vector.tensor_tensor(nmax[:, 0, :], nmax_c[:, 0, :], nmax_c[:, 1, :], ALU.min).then_inc(f_maxc, 1)
                        dve.wait_ge(f_maxc, 4 * i + 4)
                        nc.vector.tensor_tensor(nmax[:, 0, :], nmax[:, 0, :], nmax_c[:, 2, :], ALU.min).then_inc(f_max, 1)
                        dve.wait_ge(f_exp, i + 1)
                        nc.vector.tensor_tensor(rsum[:, 0, :], rsum_c[:, 0, :], rsum_c[:, 1, :], ALU.add).then_inc(f_sum, 1)
                        dve.wait_ge(f_sum, 2 * i + 1)
                        nc.vector.tensor_tensor(rsum[:, 0, :], rsum[:, 0, :], rsum_c[:, 2, :], ALU.add).then_inc(f_sum, 1)
                        dve.wait_ge(f_sum, 2 * i + 2)
                        nc.vector.reciprocal(rinv[:, 0, :], rsum[:, 0, :]).then_inc(f_inv, 1)
                        for c in range(CHUNKS):
                            dve.wait_ge(f_pthi, CHUNKS * i + c + 1)
                            nc.vector.tensor_tensor(pT[0][LO][:, :, :].rearrange("k h t -> k (h t)"), FPT[:, 0:GT],
                                                    pT[0][HI][:, :, :].rearrange("k h t -> k (h t)").bitcast(F32), ALU.subtract)\
                              .then_inc(f_ptlo, 1)
                        dve.wait_ge(f_ohi, i + 1)
                        for h in range(HPG):
                            p = slice(HD * h, HD * h + HD)
                            last = nc.vector.tensor_tensor(oT[LO][p, hg, 0:L], FPV[p, L * h:L * h + L],
                                                           oT[HI][p, hg, 0:L].bitcast(F32), ALU.subtract)
                        last.then_inc(f_olo, 1)
                    dve.wait_ge(f_gate, b + 1)
                    dve.wait_ge(f_o, b + 1)
                    nc.vector.scalar_tensor_tensor(gate[1][:, :], gate[0][:, :], 1.0, FO[0:L, :], ALU.add, ALU.mult)\
                      .then_inc(f_gated, 1)
                    dve.wait_ge(f_gated, b + 1)
                    nc.vector.scalar_tensor_tensor(xa[:, 0, :], gate[1][:, :], coef_a[0:L, bass.ds(b, 1)], xa[:, 0, :],
                                                   ALU.mult, ALU.add).then_inc(f_x1, 1)
                phase_barrier(dve)
                for n in range(EARLY):
                    decode(n)
                    weights_hi(n)
                ffn_stats(0, 0)
                for m in range(2):
                    ffn_normalise(0, 0, m)
            with dve.Else():
                for i in range(AHEAD):
                    row_max(0, i)
                    row_inverse(0, i)
                for i in range(LOOP_FROM):
                    step(0, i)
                with dve.Fori(0, GROUPS - 1) as g:
                    for i in range(LOOP_FROM, STEPS):
                        step(g, i)
                    for i in range(LOOP_FROM):
                        step(g + 1, i)
                for i in range(LOOP_FROM, STEPS):
                    step(GROUPS - 1, i, True)
                attn_lo(GROUPS - 1, STEPS - 1)
                ffn_stats(0, 0)
                for m in range(2):
                    output(GROUPS - 1, m + 2)
                    ffn_normalise(0, 0, m)

            dve.sem_inc(s_yo, 2)

            def mT_lo(j, par, m):
                rows = ROWS[m]
                dve.wait_ge(s_mthi, 3 * j + m + 1)
                nc.vector.tensor_tensor(mT[LO][:, :, 128 * m:128 * m + rows],
                                        bank[4 + (par + m) % 2][:, 0:KT * rows].rearrange("p (k t) -> p k t", k=KT),
                                        mT[HI][:, :, 128 * m:128 * m + rows].bitcast(F32), ALU.subtract).then_inc(s_mtlo, 1)

            def hidden_tile(j, par, t):
                n = FT * j + t
                gate_bank, up_bank = (bank[2 * ((par + t) % 2) + i] for i in range(2))
                dve.wait_ge(s_tg, n + 1)
                if t >= 2:
                    dve.wait_ge(s_hlo, n - 1)
                tile = hidden[(par + t) % 2]
                nc.vector.scalar_tensor_tensor(tile[:, :], tgate[:, :], 1.0, gate_bank[:, 0:TG], ALU.add, ALU.mult)\
                  .then_inc(s_sg, 1)
                dve.wait_ge(s_sg, n + 1)
                nc.vector.scalar_tensor_tensor(tile[:, :], tile[:, :], FP4_UNIT * FP4_UNIT, up_bank[:, 0:TG], ALU.mult, ALU.mult)\
                  .then_inc(s_h, 1)

            def output_tile(j, par, m):
                n = 3 * j + m
                slot, rows = (par + m) % 2, ROWS[m]
                dve.wait_ge(s_sq, n + 1)
                nc.vector.tensor_scalar(ms[0:rows, slot:slot + 1], ssq[0:rows, slot:slot + 1], 1.0 / D, RMS_EPS * (2 / FP4_UNIT) ** 2,
                                        ALU.mult, ALU.add).then_inc(s_ms, 1)
                dve.wait_ge(s_rr, n + 1)
                nc.vector.tensor_scalar(coef_y[0:rows, slot:slot + 1], rrms[0:rows, slot:slot + 1], tanhs[0:rows, 1:2], None,
                                        ALU.mult).then_inc(s_cy, 1)
                dve.wait_ge(s_cy, n + 1)
                nc.vector.scalar_tensor_tensor(yo[slot][0:rows, :], bank[6 + slot][0:rows, :], coef_y[0:rows, slot:slot + 1],
                                               xb[par][0:rows, m, :], ALU.mult, ALU.add).then_inc(s_yo, 1)

            for m in range(3):
                if m == 2:
                    ffn_normalise(0, 0, m)
                mT_lo(0, 0, m)
            decode(EARLY)
            weights_hi(EARLY)
            for t in range(FT):
                n = EARLY + 1 + t
                if n == FT:
                    dve.wait_ge(s_stored, 1)
                if n < PIECES:
                    decode(n)
                    weights_hi(n)
                hidden_tile(0, 0, t)
            with dve.Fori(0, (FGROUPS - 1) // 2) as h:
                for par in range(2):
                    j, par1 = 2 * h + par, (par + 1) % 2
                    ffn_stats(h + par, par1)
                    for m in range(3):
                        for tile in NEXT_TILES[m]:
                            ffn_normalise(j + 1, par1, tile)
                        output_tile(j, par, m)
                        for tile in NEXT_TILES[m]:
                            mT_lo(j + 1, par1, tile)
                    for t in range(FT):
                        hidden_tile(j + 1, par1, t)
            for m in range(3):
                output_tile(FGROUPS - 1, 0, m)

        @block.tensor
        def _(pe):
            def open_bank(c, name):
                before = before_in_bank(c, name)
                if before is None:
                    return
                c, other = before
                if other[0] == "G":
                    pe.wait_ge(s_gate, NB * c + int(other[1]) + 1)
                elif other[0] == "O":
                    pe.wait_ge(s_gated, NB * (c - 1) + int(other[1]) + 1)
                else:
                    pe.wait_ge(s_pjlo, split_count(c, other))

            def job(c, name):
                n = int(name[1])
                dst = job_bank(name)
                open_bank(c, name)
                if name[0] == "V":
                    last = product(dst[0:TAIL, :], lambda a, k: ctxT[a][:, k, TAIL * n:TAIL * n + TAIL],
                                   lambda a, k: W["wv"][a][:, k, :], KT)
                elif name[0] == "K":
                    if n == 0:
                        pe.wait_ge(s_ctxlo, KT * (c + 1))
                    last = product(dst[:, 0:KC], lambda a, k: W["wk"][a][:, k, 128 * n:128 * n + 128],
                                   lambda a, k: ctxT[a][:, k, :], KT)
                elif name[0] == "X":
                    pe.wait_ge(s_xn, NB * c + n + 1)
                    for k in range(KT):
                        last = nc.tensor.transpose(dst[:, L * k:L * k + L], xn[:, n, 128 * k:128 * k + 128], ident[0:L, 0:L])
                elif name[0] == "Q":
                    if n == 0:
                        pe.wait_ge(s_pjlo, split_count(c, "X3"))
                    last = product(dst[:, 0:GT], lambda a, k: W["wq"][a][:, k, 128 * n:128 * n + 128],
                                   lambda a, k: xT[a][:, k, :], KT)
                elif name[0] == "G":
                    last = product(dst[0:L, :], lambda a, k: xT[a][:, k, L * n:L * n + L], lambda a, k: W["wg"][a][:, k, :], KT)
                    last.then_inc(s_g, 1)
                    return
                else:
                    pe.wait_ge(s_olo, STEPS * (c - 1) + NB * (HG - 1) + n + 1)
                    last = product(dst[0:L, :], lambda a, k: oT[a][:, k, L * n:L * n + L], lambda a, k: W["wo"][a][:, k, :], KT)
                    last.then_inc(s_o, 1)
                    return
                last.then_inc(s_pj, 1)

            def scores(g, i):
                n = STEPS * g + i
                hg, b = i // NB, i % NB
                dst = SC[i % 2][0:L, 0:KC].rearrange("t (h k) -> t h k", h=HPG)
                if b == 0:
                    pe.wait_ge(s_pjlo, split_count(g, max(f"K{hg}", f"Q{hg}", key=CYCLE.index)))
                if not isinstance(n, int) or n >= 2:
                    pe.wait_ge(s_exp, n - 1)
                nc.tensor.matmul(dst, ones[:, :], mbias[:, bass.ds(NB * g + b, 1), :].broadcast_to([128, HPG, TAIL]),
                                 start=True, stop=False)
                product(dst, lambda a, t: qT[hg % 2][a][:, L * b:L * b + L],
                        lambda a, t: kblk[hg % 2][a][:, :, TAIL * b:TAIL * b + TAIL], 1, first=False).then_inc(s_sc, 1)

            def transpose_probs(g, i):
                n = STEPS * g + i
                pe.wait_ge(s_norm, n + 1)
                if not isinstance(n, int) or n >= 2:
                    pe.wait_ge(s_ptlo, n - 1)
                for h in range(HPG):
                    last = nc.tensor.transpose(PT[i % 2][0:TAIL, L * h:L * h + L], probs[i % 2][:, h, :], ident[0:L, 0:L])
                last.then_inc(s_pt, 1)

            def attend(g, i):
                n = STEPS * g + i
                hg, b = i // NB, i % NB
                pe.wait_ge(s_ptlo, n + 1)
                if hg == 0:
                    pe.wait_ge(s_pjlo, split_count(g, f"V{b}"))
                if not isinstance(n, int) or n >= 2:
                    pe.wait_ge(s_olo, n - 1)
                product(PV[i % 2][:, 0:GT], lambda a, t: vv[a][0:TAIL, b, 128 * hg:128 * hg + 128],
                        lambda a, t: pT[i % 2][a][0:TAIL, :, :].rearrange("k h t -> k (h t)"), 1).then_inc(s_pv, 1)

            def step(g, i, last=False):
                transpose_probs(g, i)
                for ahead in step_ahead(g, i):
                    scores(*ahead)
                if not isinstance(g, int) or g or i:
                    attend(*last_step(g, i))
                for c, name in beside(g, i):
                    job(c, name)

            pe.wait_ge(s_const, 16 * CONSTS)
            for b in range(NB):
                job(0, f"X{b}")
            pe.wait_ge(s_splitlo, 1)
            job(0, "Q0")
            pe.wait_ge(s_pconst, 2)
            pe.wait_ge(s_setup, 7)
            nc.tensor.matmul(FLAGS[0:L, 0:2 * B], ones[0:B, :], flagdiag[:, :, :].rearrange("p f b -> p (f b)"), start=True, stop=True)\
              .then_inc(s_flags, 1)
            pe.wait_ge(s_splitlo, 2)
            job(0, "K0")
            pe.wait_ge(s_splitlo, 3)
            job(0, "V0")
            job(0, "V1")
            job(0, "V2")
            pe.wait_ge(s_pjlo, len(HEAD))

            def full_job(b, name):
                n = int(name[1:] or 0)
                if name == FULL_JOBS[0]:
                    pe.wait_ge(f_ctx, b + 3)
                else:
                    pe.wait_ge(f_pjlo, full_count(b, name) - 1)
                if name[0] == "V":
                    last = product(FJ[:, :], lambda a, k: ctxT[a][:, k, CHUNK * n:CHUNK * n + CHUNK],
                                   lambda a, k: W["wv"][a][:, k, :], KT)
                elif name[0] == "X":
                    pe.wait_ge(f_xn, b + 1)
                    for k in range(KT):
                        last = nc.tensor.transpose(FJ[:, L * k:L * k + L], xn[:, 0, 128 * k:128 * k + 128], ident[0:L, 0:L])
                elif name[0] == "Q":
                    last = product(FJ[:, 0:L], lambda a, k: W["wq"][a][:, k, 128 * n:128 * n + 128],
                                   lambda a, k: xT[a][:, k, 0:L], KT)
                else:
                    last = product(FJ[:, 0:KC], lambda a, k: W["wk"][a][:, k, 128 * n:128 * n + 128],
                                   lambda a, k: ctxT[a][:, k, :], KT)
                last.then_inc(f_pj, 1)

            with pe.If(wants_full(pe)):
                pe.wait_ge(s_splitlo, 5)
                with pe.Fori(0, B) as b:
                    for name in FULL_JOBS[0:CHUNKS + 1]:
                        full_job(b, name)
                    pe.wait_ge(f_bias, b + 2)
                    for hg in range(HG):
                        i = HG * b + hg
                        full_job(b, f"K{hg}")
                        full_job(b, f"Q{hg}")
                        pe.wait_ge(f_pjlo, full_count(b, f"Q{hg}"))
                        for c in range(CHUNKS):
                            cols = slice(CHUNK * c, CHUNK * c + CHUNK)
                            dst = FSC[c][0:L, :].rearrange("t (h k) -> t h k", h=HPG)
                            nc.tensor.matmul(dst, ones[:, :], mbias_full[:, cols].unsqueeze(1).broadcast_to([128, HPG, CHUNK]),
                                             start=True, stop=False)
                            last = product(dst, lambda a, t: qT[0][a][:, 0:L], lambda a, t: kblk[0][a][:, :, cols], 1, first=False)
                        last.then_inc(f_sc, 1)
                        pe.wait_ge(f_norm, i + 1)
                        if hg:
                            pe.wait_ge(f_olo, i)
                        for c in range(CHUNKS):
                            n = CHUNKS * i + c
                            if c:
                                pe.wait_ge(f_ptlo, n)
                            for h in range(HPG):
                                last = nc.tensor.transpose(FPT[:, L * h:L * h + L], probs_full[:, h, CHUNK * c:CHUNK * c + CHUNK],
                                                           ident[0:L, 0:L])
                            last.then_inc(f_pt, 1)
                            pe.wait_ge(f_ptlo, n + 1)
                            for p, (a, v) in enumerate(PASSES):
                                last = nc.tensor.matmul(FPV[:, 0:GT], vv[v][:, c, 128 * hg:128 * hg + 128],
                                                        pT[0][a][:, :, :].rearrange("k h t -> k (h t)"),
                                                        start=c == 0 and p == 0, stop=c == CHUNKS - 1 and p == 2)
                            last.then_inc(f_pv, 1)
                    product(FJ[0:L, :], lambda a, k: xT[a][:, k, 0:L], lambda a, k: W["wg"][a][:, k, :], KT).then_inc(f_g, 1)
                    pe.wait_ge(f_olo, HG * b + HG)
                    product(FO[0:L, :], lambda a, k: oT[a][:, k, 0:L], lambda a, k: W["wo"][a][:, k, :], KT).then_inc(f_o, 1)
                phase_barrier(pe)
            with pe.Else():
                for i in range(AHEAD):
                    scores(0, i)
                pe.wait_ge(s_splitlo, 5)
                for i in range(LOOP_FROM):
                    step(0, i)
                with pe.Fori(0, GROUPS - 1) as g:
                    for i in range(LOOP_FROM, STEPS):
                        step(g, i)
                    for i in range(LOOP_FROM):
                        step(g + 1, i)
                for i in range(LOOP_FROM, STEPS):
                    step(GROUPS - 1, i, True)
                attend(GROUPS - 1, STEPS - 1)
                for b in (2, 3):
                    job(GROUPS, f"O{b}")
                pe.wait_ge(s_gated, GROUPS * NB)
                pe.wait_ge(s_ptlo, GROUPS * STEPS)

            def transpose_tile(j, par, m):
                rows = ROWS[m]
                if m == 2:
                    pe.wait_ge(s_mtlo, 3 * j + 1)
                wait_apart(pe, s_mn, 3 * j + m + 1)
                for k in range(KT):
                    last = nc.tensor.transpose(bank[4 + (par + m) % 2][:, rows * k:rows * k + rows],
                                               mn[(par + m) % 2][0:rows, 128 * k:128 * k + 128], ident[0:rows, 0:rows])
                last.then_inc(s_mt, 1)

            def gate_up(j, par, t, first=False):
                n = FT * j + t
                if t == 0:
                    pe.wait_ge(s_mtlo, 3 * j + 3)
                if first:
                    pe.wait_ge(s_whi, t + 1)
                    pe.wait_ge(s_wlo, t + 1)
                if not first or t >= 2:
                    pe.wait_ge(s_h, n - 1)
                for i in range(2):
                    cols = slice(128 * i, 128 * i + 128)
                    last = product(bank[2 * ((par + t) % 2) + i][:, 0:TG], lambda a, k: wgu[t][a][:, k, cols],
                                   lambda a, k: mT[a][:, k, :], KT)
                last.then_inc(s_gu, 1)

            def down(j, par, m):
                slot, rows = (par + m) % 2, ROWS[m]
                pe.wait_ge(s_yo, 3 * j + m + 1)
                for t in range(FT):
                    if m == 0:
                        pe.wait_ge(s_hlo, FT * j + t + 1)
                    for p, (a, b) in enumerate(PASSES):
                        last = nc.tensor.matmul(bank[6 + slot][0:rows, :], hT[a][:, t, 128 * m:128 * m + rows], wdn[t // 2][b][:, t % 2, :],
                                                start=t == 0 and p == 0, stop=t == FT - 1 and p == 2)
                last.then_inc(s_y, 1)

            for m in range(3):
                transpose_tile(0, 0, m)
            for t in range(FT):
                gate_up(0, 0, t, True)
            pe.wait_ge(s_wlo, PIECES)
            pe.wait_ge(s_whi, PIECES)
            with pe.Fori(0, (FGROUPS - 1) // 2) as h:
                for par in range(2):
                    j, par1 = 2 * h + par, (par + 1) % 2
                    for m in range(3):
                        down(j, par, m)
                        for tile in NEXT_TILES[m]:
                            transpose_tile(j + 1, par1, tile)
                    for t in range(FT):
                        gate_up(j + 1, par1, t)
            for m in range(3):
                down(FGROUPS - 1, 0, m)


INPUTS = ("x", "ctx_tail", "ctx_full", "mask", "mask_tail", "g_xattn", "g_ffn", "norm_w", "wq", "wk", "wv", "wo", "wg",
          "gu_packed", "gu_scales", "dn_packed", "dn_scales", "identity", "shifts")


def hidden_order(a, axis):
    a = np.moveaxis(a, axis, 0)
    rest = a.shape[1:]
    pairs = a[:1280].reshape(5, 32, 2, 4, *rest).transpose(0, 2, 3, 1, *range(4, 4 + len(rest))).reshape(1280, *rest)
    last = a[1280:].reshape(16, 8, *rest).transpose(1, 0, *range(2, 2 + len(rest))).reshape(128, *rest)
    return np.moveaxis(np.concatenate([pairs, last]), 0, axis)


def lay_out(inputs):
    a = {k: np.asarray(v) for k, v in inputs.items()}
    ctx = a["ctx_2048"]
    keep = a["mask_BxS2_bk0"]
    ctx_t = ctx.transpose(0, 2, 1).reshape(B, KT, 128, M)
    tail = ctx_t[..., M - TAIL:].reshape(GROUPS, NB, KT, 128, TAIL).transpose(0, 3, 2, 1, 4).reshape(GROUPS, 128, KT, KC)
    gu = a["L0_ffn_gate_up_packed"].T
    gs = a["L0_ffn_gate_up_scales"]

    def interleave(w):
        both = [hidden_order(w[:, i * FF:(i + 1) * FF], 1).reshape(w.shape[0], FT, 1, 128) for i in range(2)]
        return np.concatenate(both, 2).reshape(w.shape[0], 2 * FF)

    p = np.arange(128)
    shifts = np.stack([12 - 4 * (p // 64), 4 - 4 * (p // 64), 12 - 4 * (p // 32), 16 * (p // 64), 12 - 4 * (p // 16 % 4)], 1)
    return {
        "x": a["x"], "ctx_tail": tail, "ctx_full": ctx_t, "mask": keep, "mask_tail": keep[:, M - TAIL:],
        "g_xattn": a["g_xattn"], "g_ffn": a["g_ffn"], "norm_w": a["L0_xattn_norm_w"].reshape(KT, 128).T,
        **{n: a[f"L0_xattn_{n}"].T for n in ("wq", "wk", "wv", "wo", "wg")},
        "gu_packed": interleave(gu), "gu_scales": interleave(gs),
        "dn_packed": a["L0_ffn_down_packed"].T, "dn_scales": a["L0_ffn_down_scales"],
        "identity": np.eye(128, dtype=np.float32), "shifts": shifts.astype(np.int32),
    }


def kernel(**inputs):
    import concourse.bacc as bacc
    from concourse.bass_utils import run_bass_kernel_spmd

    nc = bacc.Bacc("TRN2", target_bir_lowering=False, num_devices=1)
    arrays, args = {}, []
    laid = lay_out(inputs)
    for name in INPUTS:
        a = np.ascontiguousarray(laid[name])
        arrays[f"in_{name}"] = a
        args.append(nc.dram_tensor(f"in_{name}", a.shape, mybir.dt.from_np(a.dtype), kind="ExternalInput").ap())
    args.append(nc.dram_tensor("x1_scratch", (B, L, D), F32, kind="Internal").ap())
    args.append(nc.dram_tensor("out_x", (B, L, D), F32, kind="ExternalOutput").ap())
    build(nc, *args)
    r = run_bass_kernel_spmd(nc, [arrays], core_ids=[0])
    return r.results[0]["out_x"]
```

```python
from contextlib import ExitStack

import numpy as np

import concourse.bass as bass
from concourse import mybir

F32, F32R, BF16, F16 = mybir.dt.float32, mybir.dt.float32r, mybir.dt.bfloat16, mybir.dt.float16
I32, I16, U8 = mybir.dt.int32, mybir.dt.int16, mybir.dt.uint8
ALU = mybir.AluOpType
ACT = mybir.ActivationFunctionType
AXIS_X = mybir.AxisListType.X

B, L, D = 16, 100, 512
M = 361
HEADS, HD = 16, 32
KT = D // 128
NB = 4
GROUPS = B // NB
GT = NB * L
HG = 4
HPG = HEADS // HG
TAIL = 96
KC = NB * TAIL
CHUNK = 128
CHUNKS = KC // CHUNK
STEPS = HG * NB
FF = 1408
FT = FF // 128
TOKENS = B * L
TG = 320
FGROUPS = TOKENS // TG
ROWS = (128, 128, 64)
PAIRS = (FGROUPS - 1) // 2
OUT_TILES = ((64, ((64, 128),)), (192, ((192, 128),)), (0, ((0, 64), (TG, 64))), (128, ((384, 128),)), (256, ((512, 128),)))
TILES_OF = ((0, 1), (2, 3, 4))
FP4_UNIT = 16384.0
MASKED = 1e30
PIECES = FT + 6
LN_EPS, RMS_EPS = 1e-5, 1e-6


def build(nc, x, ctx_tail, ctx_full, mask, mask_tail, g_xattn, g_ffn, norm_w, wq, wk, wv, wo, wg,
          gu_packed, gu_scales, dn_packed, dn_scales, identity, shifts, x1_dram, out):
    es = ExitStack()
    with es:
        def sem(name):
            return es.enter_context(nc.semaphore(name))

        def sb(stack, name, shape, dt):
            return stack.enter_context(nc.sbuf_tensor(name, shape, dt))

        ident = sb(es, "ident", [128, 128], F32)
        shift = sb(es, "shift", [128, 5], I32)
        normw = sb(es, "normw", [128, KT], F32)
        gates = sb(es, "gates", [128, 2], F32)
        tanhs = sb(es, "tanhs", [128, 2], F32)
        halfpow = sb(es, "halfpow", [128, 4], F32)
        coef_a = sb(es, "coef_a", [128, B], F32)
        headkeep = sb(es, "headkeep", [1, 1], I32)
        headmax = sb(es, "headmax", [1, 1], F32)
        stats = sb(es, "stats", [128, 4, 6], F32)
        mv = sb(es, "mv", [128, 4, 2], F32)
        var = sb(es, "var", [128, 4], F32)
        rstd = sb(es, "rstd", [128, 4], F32)

        phase_a, phase_b, setup_a = ExitStack(), ExitStack(), ExitStack()
        W, raw = {}, {}

        def weight(name):
            hi = sb(phase_a, f"{name}_hi", [128, KT, D], F32R)
            with ExitStack() as arrival:
                raw[name] = sb(arrival, f"{name}_raw", [128, KT, D], F32)
            W[name] = [hi, sb(phase_a, f"{name}_lo", [128, KT, D], F32R)]

        weight("wv")
        ctx_raw = sb(phase_a, "ctx_raw", [128, KT, KC], F32)
        xn = sb(phase_a, "xn", [L, NB, D], F32)
        weight("wk")
        ctxT = [sb(phase_a, f"ctxT_{half}", [128, KT, KC], F32R) for half in ("hi", "lo")]
        weight("wq")
        weight("wg")
        xT = [sb(phase_a, f"xT_{half}", [128, KT, GT], F32R) for half in ("hi", "lo")]
        kblk = [[sb(phase_a, f"kblk{s}_{half}", [128, HPG, KC], F32R) for half in ("hi", "lo")] for s in range(2)]
        vv = [sb(phase_a, f"v_{half}", [128, NB, D], F32R) for half in ("hi", "lo")]
        qT = [[sb(phase_a, f"qT{s}_{half}", [128, GT], F32R) for half in ("hi", "lo")] for s in range(2)]
        mbias = sb(phase_a, "mbias", [128, B, TAIL], BF16)
        ones = sb(phase_a, "ones", [128, L], BF16)
        nmax = sb(phase_a, "nmax", [L, 4, HPG], F32)
        rsum = sb(phase_a, "rsum", [L, 4, HPG], F32)
        rinv = sb(phase_a, "rinv", [L, 4, HPG], F32)
        probs = [sb(phase_a, f"probs{s}", [L, HPG, TAIL], F32) for s in range(2)]
        pT = [[sb(phase_a, f"pT{s}_{half}", [128, HPG, L], F32R) for half in ("hi", "lo")] for s in range(2)]
        flags = sb(phase_a, "flags", [B, 2], F32)
        flagdiag = sb(phase_a, "flagdiag", [B, 2, B], BF16)
        weight("wo")
        xa = sb(phase_a, "xa", [L, 2, D], F32)
        maskall = sb(setup_a, "maskall", [B, M], U8)
        masktail = sb(setup_a, "masktail", [1, B, TAIL], U8)
        setup_a.close()
        oT = [sb(phase_a, f"oT_{half}", [128, HG, GT], F32R) for half in ("hi", "lo")]
        gate = [sb(phase_a, f"gate{b}", [L, D], F32) for b in range(NB)]
        maskrow = sb(phase_a, "maskrow", [1, KC], U8)
        nmax_c = sb(phase_a, "nmax_c", [L, CHUNKS, HPG], F32)
        rsum_c = sb(phase_a, "rsum_c", [L, CHUNKS, HPG], F32)
        probs_full = xn[:, 1:NB, :].rearrange("t b d -> t (b d)").rearrange("t (h k) -> t h k", h=HPG)
        mbias_full = mbias[:, 0:NB, :].rearrange("p b k -> p (b k)")
        phase_a.close()
        words = [sb(phase_b, f"words{s}", [128, D], I32) for s in range(2)]
        scale = [sb(phase_b, f"scale{s}", [128, D], F16) for s in range(2)]
        scale_a = [sb(phase_b, f"scale_a{s}", [128, D], F16) for s in range(2)]
        scale_b = [sb(phase_b, f"scale_b{s}", [128, D], F16) for s in range(2)]
        fp4 = [sb(phase_b, f"fp4_{s}", [128, D], I32) for s in range(2)]
        wgu = [[sb(phase_b, f"wgu{t}_{half}", [128, KT, 256], F32R) for half in ("hi", "lo")] for t in range(FT)]
        xb = sb(phase_b, "xb", [128, 3, D], F32)
        mT = [sb(phase_b, f"mT_{half}", [128, KT, TG], F32R) for half in ("hi", "lo")]
        mn = [sb(phase_b, f"mn{m}", [128, D], F32) for m in range(3)]
        hT = [sb(phase_b, f"hT_{half}", [128, FT, TG + 64], F32R) for half in ("hi", "lo")]
        tgate = sb(phase_b, "tgate", [128, TG], F32)
        hidden = [sb(phase_b, f"hidden{s}", [128, TG], F32) for s in range(2)]
        wdn = [[sb(phase_b, f"wdn{c}_{half}", [128, 2 if c < 5 else 1, D], F32R) for half in ("hi", "lo")] for c in range(6)]
        yo = [words[s][:, :].bitcast(F32) for s in range(2)]
        xr = [fp4[s][:, :].bitcast(F32) for s in range(2)]
        ssq = sb(phase_b, "ssq", [128, 2], F32)
        ms = sb(phase_b, "ms", [128, 2], F32)
        rrms = sb(phase_b, "rrms", [128, 2], F32)
        coef_y = sb(phase_b, "coef_y", [128, 2], F32)
        phase_b.close()

        bank = [es.enter_context(nc.psum_tensor(f"bank{i}", [128, 512], F32)) for i in range(8)]
        PJ, SC, PT, PV = bank[0:2], bank[2:4], bank[4:6], bank[6:8]
        FLAGS = bank[7]

        s_ident = sem("identity_loaded")
        s_shift = sem("shifts_loaded")
        s_mask = sem("masks_loaded")
        s_normw = sem("norm_w_loaded")
        s_gates = sem("gate_scalars_loaded")
        s_w = {name: sem(f"{name}_loaded") for name in ("wq", "wk", "wv", "wg", "wo")}
        s_x = [sem(f"x_loaded{b}") for b in range(NB)]
        s_x1st = [sem(f"x1_stored{b}") for b in range(NB)]
        s_ctx = sem("ctx_loaded")
        s_whole = {name: sem(f"{name}_hi_done") for name in s_w}
        s_split = {name: sem(f"{name}_split") for name in s_w}
        s_zero = sem("kblk_zeroed")
        s_setup = sem("dve_setup")
        s_tanh = sem("gates_tanh")
        s_flags = sem("flags_spread")
        s_pconst = sem("pool_consts")
        s_ctxhi, s_ctxlo = sem("ctx_hi_done"), sem("ctx_lo_done")
        s_ln = sem("ln_chain")
        s_pow = sem("rstd_ready")
        s_xn = sem("xn_ready")
        s_xa = [sem(f"residual_loaded{s}") for s in range(2)]
        s_pj, s_pjhi, s_pjlo = sem("projected"), sem("projection_hi"), sem("projection_lo")
        s_g, s_o = sem("gate_projected"), sem("out_projected")
        s_sc, s_max, s_exp, s_inv, s_norm = (sem(n) for n in ("scores_ready", "max_ready", "exp_done", "inverse_ready", "probs_normed"))
        s_pt, s_pthi, s_ptlo = sem("probsT_ready"), sem("probsT_hi"), sem("probsT_lo")
        s_pv, s_ohi, s_olo = sem("attn_ready"), sem("attn_hi"), sem("attn_lo")
        s_gate, s_gated, s_x1 = sem("gate_ready"), sem("gated_ready"), sem("x1_ready")
        f_load, f_ctxhi, f_ctx, f_bias = sem("full_loaded"), sem("full_ctx_hi"), sem("full_ctx_split"), sem("full_bias")
        f_ln, f_pow, f_xn = sem("full_ln_chain"), sem("full_rstd"), sem("full_xn_ready")
        f_pj, f_pjhi, f_pjlo = sem("full_projected"), sem("full_projection_hi"), sem("full_projection_lo")
        f_sc, f_maxc, f_max, f_exp, f_sum, f_inv, f_norm = (sem(f"full_{n}") for n in (
            "scores_ready", "max_chain", "max_ready", "exp_done", "sum_chain", "inverse_ready", "probs_normed"))
        f_pt, f_pthi, f_ptlo = sem("full_probsT_ready"), sem("full_probsT_hi"), sem("full_probsT_lo")
        f_pv, f_ohi, f_olo = sem("full_attn_ready"), sem("full_attn_hi"), sem("full_attn_lo")
        f_g, f_o, f_gate, f_gated, f_x1, f_st = (sem(f"full_{n}") for n in (
            "gate_projected", "out_projected", "gate_ready", "gated_ready", "x1_ready", "x1_stored"))
        s_apart = sem("waits_apart")
        s_pa = sem("full_path_done")
        s_stored = sem("x1_all_stored")
        s_words = [sem(f"words_loaded{s}") for s in range(2)]
        s_scale, s_scaleb, s_shifted = sem("scale_cut"), sem("scale_last_bit"), sem("codes_shifted")
        s_dec = sem("piece_decoded")
        s_whi, s_wlo = sem("ffn_weight_hi"), sem("ffn_weight_lo")
        s_xb = sem("x1_loaded")
        s_xr = [sem(f"x1_residual_loaded{s}") for s in range(2)]
        s_bln, s_bpow, s_mn = sem("ffn_ln_chain"), sem("ffn_rstd"), sem("mn_ready")
        s_mt, s_mthi, s_mtlo = sem("mT_ready"), sem("mT_hi"), sem("mT_lo")
        s_gu, s_tg, s_sg, s_h, s_hhi, s_hlo = (sem(n) for n in ("gate_up_ready", "tanh_gate", "silu_gate", "hidden_ready", "hidden_hi", "hidden_lo"))
        s_y, s_sq, s_ms, s_rr, s_cy, s_yo = (sem(n) for n in ("y_ready", "y_squared", "mean_square", "rrms_ready", "coef_ready", "out_ready"))
        s_out = [sem(f"out_stored{s}") for s in range(2)]

        block = es.enter_context(nc.Block())

        HI, LO = 0, 1

        def wait_apart(engine, semaphore, value):
            engine.wait_ge(semaphore, value)
            engine.sem_inc(s_apart, 1)

        def words_loaded(n):
            return sum(16 * (4 if m < FT else (5 if m - FT < 5 else 2)) for m in range(n % 2, n + 1, 2))

        def piece_operands(n, half, part):
            codes, factor = fp4[n % 2][:, :].bitcast(F16), (scale_a if half == HI else scale_b)[n % 2]
            if n < FT:
                out_ap = wgu[n][half][:, :, :].rearrange("p (two r) c -> p two r c", two=2)
                code = codes.rearrange("p (r c two) -> p two r c", r=2, two=2)
                factor = factor[:, 0:256].unsqueeze(1).unsqueeze(1).broadcast_to([128, 2, 2, 256])
                if half == LO:
                    return out_ap, code, factor
                two, r = ((0, slice(0, 2)), (1, slice(0, 1)), (1, slice(1, 2)))[part]
                return out_ap[:, two, r, :], code[:, two, r, :], factor[:, two, r, :]
            tiles = 2 if n < PIECES - 1 else 1
            code = codes.rearrange("p (c two) -> p two c", two=2)
            if half == LO:
                return (wdn[n - FT][half][:, :, :], code[:, 0:tiles, :],
                        factor[:, :].unsqueeze(1).broadcast_to([128, tiles, D]))
            tile, cols = ((0, slice(0, D)), (1, slice(0, 256)), (1, slice(256, D)))[part]
            return wdn[n - FT][half][:, tile, cols], code[:, tile, cols], factor[:, cols]

        def tile_bank(par, m):
            return bank[4 + m] if m < 2 else bank[2 * par + 1]

        def hidden_cols(par):
            return slice(64 * par, 64 * par + TG)

        def tile_rows(i, last):
            return 64 if last and i == 2 else 128

        def tile_transfers(h, i, last=False):
            tiles = [m for m in range(i % 2, len(OUT_TILES), 2)]
            per_pair = sum(len(OUT_TILES[m][1]) for m in tiles)
            upto = sum(len(OUT_TILES[m][1]) for m in tiles if m <= i)
            return per_pair * h + (upto - 1 if last and i == 2 else upto)

        def phase_barrier(engine):
            engine.sem_inc(s_pa, 1)
            engine.wait_ge(s_pa, 5)

        PASSES = ((HI, HI), (HI, LO), (LO, HI))

        def product(out_ap, lhs, rhs, tiles, first=True):
            last = None
            for t in range(tiles):
                for p, (a, b) in enumerate(PASSES):
                    last = nc.tensor.matmul(out_ap, lhs(a, t), rhs(b, t), start=first and t == 0 and p == 0,
                                            stop=t == tiles - 1 and p == 2)
            return last

        CYCLE = ["X0", "X1", "X2", "X3", "Q0", "K0", "V0", "V1", "O0", "K1", "O1", "Q1", "V2", "O2", "V3", "O3",
                 "G0", "K2", "Q2", "G1", "K3", "Q3", "G2", "G3"]
        SPLIT_JOBS = [n for n in CYCLE if n[0] in "VKXQ"]
        HEAD = ["X0", "X1", "X2", "X3", "Q0", "K0", "V0"]
        BESIDE = {0: ["Q1", "V2"], 1: ["O2", "V3"], 2: ["O3", "G0"], 3: ["K2"], 4: ["Q2"], 5: ["G1"], 6: ["K3"], 7: ["Q3"],
                  8: ["G2"], 9: ["G3", "X0", "X1"], 10: ["X2", "X3"], 11: ["Q0"], 12: ["K0"], 13: ["V0"],
                  14: ["V1", "O0"], 15: ["K1", "O1"]}
        LOOP_FROM, NEXT_FROM = 4, 8
        NORM_AT = {4: 0, 5: 1, 7: 2, 8: 3}
        CTX_AT = {8: (0, 1), 9: (2,), 10: (3,)}
        AHEAD = 2
        EARLY_AT = {5: 0, 6: 1, **{i: i - 5 for i in range(7, STEPS - 1)}}
        EARLY = len(EARLY_AT)
        FIRST_CYCLE = [n for n in CYCLE if n[0] != "O"]
        LAST_CYCLE = [n for n in CYCLE if n[0] == "O"]

        def order(c):
            return {0: FIRST_CYCLE, GROUPS: LAST_CYCLE}.get(c, CYCLE) if isinstance(c, int) else CYCLE

        def job_bank(c, name):
            return PJ[order(c).index(name) % 2]

        def split_count(c, name):
            return len(SPLIT_JOBS) * c + SPLIT_JOBS.index(name) + 1

        def exists(c, name):
            return not isinstance(c, int) or (1 <= c if name[0] == "O" else 0 <= c < GROUPS)

        def before_in_bank(c, name):
            at = order(c).index(name) - 2
            while True:
                if at < 0:
                    c = c - 1
                    at += len(order(c))
                if isinstance(c, int) and c < 0:
                    return None
                if exists(c, order(c)[at]):
                    return c, order(c)[at]
                at -= 2

        def beside(g, i):
            jobs = [(g + 1 if i >= NEXT_FROM and n[0] != "G" else g, n) for n in BESIDE[i]]
            first = [(0, "V1"), (0, "K1")] if isinstance(g, int) and (g, i) == (0, 0) else []
            return first + [job for job in jobs if exists(*job)]

        def step_ahead(g, i):
            g, i = (g, i + AHEAD) if i + AHEAD < STEPS else (g + 1, i + AHEAD - STEPS)
            return [(g, i)] if not isinstance(g, int) or g < GROUPS else []

        def last_step(g, i):
            return (g, i - 1) if i else (g - 1, STEPS - 1)

        def wants_full(engine):
            engine.wait_ge(s_setup, SETUP)
            return engine.value_load(headkeep[0:1, 0:1], min_val=0, max_val=1)

        FULL_JOBS = [f"V{c}" for c in range(CHUNKS)] + ["X"] + [f"{k}{hg}" for hg in range(HG) for k in "KQ"]

        def full_count(b, name):
            return len(FULL_JOBS) * b + FULL_JOBS.index(name) + 1

        SETUP = 10

        FJ, FSC, FPT, FPV, FO = bank[0], bank[2:5], bank[5], bank[6], bank[7]

        @block.sync
        def _(sp):
            sp.dma_start(gates[:, 0:1], g_xattn.unsqueeze(0).broadcast_to([128, 1])).then_inc(s_gates, 16)
            sp.dma_start(gates[:, 1:2], g_ffn.unsqueeze(0).broadcast_to([128, 1])).then_inc(s_gates, 16)
            for b in range(NB):
                sp.dma_start(xn[:, b, :], x[b]).then_inc(s_x[b], 16)
            sp.dma_start(normw[:, :], norm_w).then_inc(s_normw, 16)

            def load_weight(name, w):
                sp.dma_start(raw[name][:, :, :], w.rearrange("(k p) n -> p k n", p=128)).then_inc(s_w[name], 16)

            load_weight("wq", wq)
            sp.dma_start(ident[:, :], identity).then_inc(s_ident, 16)
            sp.dma_start(ctx_raw[:, :, :], ctx_tail[0]).then_inc(s_ctx, 16)
            load_weight("wk", wk)
            sp.dma_start(maskall[:, :], mask).then_inc(s_mask, 16)
            sp.dma_start(masktail[:, :, :], mask_tail.unsqueeze(0)).then_inc(s_mask, 16)
            load_weight("wv", wv)
            load_weight("wg", wg)
            load_weight("wo", wo)
            sp.dma_start(shift[:, :], shifts).then_inc(s_shift, 16)

            def load_residual(g, b):
                sp.dma_start(xa[:, b % 2, :], x[bass.ds(NB * g + b, 1)].rearrange("o t d -> (o t) d")).then_inc(s_xa[b % 2], 16)

            def load_next(g):
                for b in range(NB):
                    sp.wait_ge(s_pj, split_count(g, f"X{b}"))
                    sp.dma_start(xn[:, b, :], x[bass.ds(NB * (g + 1) + b, 1)].rearrange("o t d -> (o t) d")).then_inc(s_x[b], 16)
                sp.wait_ge(s_ctxlo, KT * (g + 1))
                sp.dma_start(ctx_raw[:, :, :], ctx_tail[bass.ds(g + 1, 1)].rearrange("o p k c -> (o p) k c")).then_inc(s_ctx, 16)

            def outputs(g, last):
                for b in range(NB):
                    if last and b < 3:
                        load_piece(EARLY - 1 + b)
                    sp.wait_ge(s_x1, NB * g + b + 1)
                    sp.dma_start(x1_dram[bass.ds(NB * g + b, 1)].rearrange("o t d -> (o t) d"), gate[b][:, :])\
                      .then_inc(s_x1st[b], 16)
                    if b + 2 < NB:
                        load_residual(g, b + 2)
                    elif not last:
                        load_residual(g + 1, b - 2)

            def load_piece(n):
                s = n % 2
                if n >= 2:
                    sp.wait_ge(s_scaleb, n - 1)
                    sp.wait_ge(s_dec, n - 1)
                if n < FT:
                    cols = slice(256 * n, 256 * n + 256)
                    for half in range(2):
                        p = slice(64 * half, 64 * half + 64)
                        sp.dma_start(words[s][p, 0:256], gu_packed[:, cols]).then_inc(s_words[s], 16)
                        sp.dma_start(scale[s][p, 0:256], gu_scales[:, cols].unsqueeze(1).broadcast_to([4, 16, 256]))\
                          .then_inc(s_words[s], 16)
                else:
                    c = n - FT
                    rep, nw = (4, 32) if c < 5 else (8, 16)
                    sp.dma_start(words[s][:, :], dn_packed[32 * c:32 * c + nw, :].unsqueeze(0).broadcast_to([rep, nw, D]))\
                      .then_inc(s_words[s], 16)
                    if c < 5:
                        for r in range(rep):
                            sp.dma_start(scale[s][32 * r:32 * r + 32, :],
                                         dn_scales[2 * c:2 * c + 2, :].unsqueeze(1).broadcast_to([2, 16, D]))\
                              .then_inc(s_words[s], 16)
                    else:
                        sp.dma_start(scale[s][:, :], dn_scales[10:11, :].broadcast_to([128, D])).then_inc(s_words[s], 16)

            x1_flat = x1_dram.rearrange("b t d -> (b t) d")
            out_flat = out.rearrange("b t d -> (b t) d")

            def load_x1(j):
                sp.dma_start(xb[:, 0:2, :], x1_flat[bass.ds(TG * j, 256), :].rearrange("(m p) d -> p m d", p=128)).then_inc(s_xb, 16)
                sp.dma_start(xb[0:64, 2, :], x1_flat[bass.ds(TG * j + 256, 64), :]).then_inc(s_xb, 16)

            def full_loads(b):
                sp.dma_start(ctx_raw[:, :, 0:M], ctx_full[bass.ds(b, 1)].rearrange("o k p c -> p (o k) c")).then_inc(f_load, 16)
                sp.dma_start(xa[:, 0, :], x[bass.ds(b, 1)].rearrange("o t d -> (o t) d")).then_inc(f_load, 16)
                sp.dma_start(maskrow[:, 0:M], mask[bass.ds(b, 1), :]).then_inc(f_load, 16)

            def full_store(b):
                sp.wait_ge(f_x1, b + 1)
                sp.dma_start(x1_dram[bass.ds(b, 1)].rearrange("o t d -> (o t) d"), xa[:, 0, :]).then_inc(f_st, 16)
                sp.wait_ge(f_st, 16 * (b + 1))

            with sp.If(wants_full(sp)):
                sp.wait_ge(s_pjlo, len(HEAD))
                full_loads(0)
                with sp.Fori(0, B - 1) as b:
                    full_store(b)
                    full_loads(b + 1)
                full_store(B - 1)
                phase_barrier(sp)
                for n in range(EARLY + 2):
                    load_piece(n)
                load_x1(0)
            with sp.Else():
                for b in range(NB):
                    sp.sem_inc(s_x1st[b], 16)
                for b in range(2):
                    load_residual(0, b)
                with sp.Fori(0, GROUPS - 1) as g:
                    load_next(g)
                    outputs(g, False)
                sp.wait_ge(s_pj, split_count(GROUPS - 1, "V3"))
                for n in range(EARLY - 1):
                    load_piece(n)
                sp.wait_ge(s_sc, STEPS * (GROUPS - 1) + 12)
                for b in range(NB):
                    sp.wait_ge(s_x1st[b], 32)
                load_x1(0)
                outputs(GROUPS - 1, True)
                for b in range(NB):
                    sp.wait_ge(s_x1st[b], 16 * (GROUPS + 1))
            sp.sem_inc(s_stored, 1)

            for s in range(2):
                sp.sem_inc(s_out[s], 16)

            def tile_parts(h, i, last):
                parts, row = [], 0
                for first, count in OUT_TILES[i][1][:1 if last else 2]:
                    parts.append((slice(row, row + count), bass.ds(2 * TG * h + first, count)))
                    row += count
                return parts

            def load_residual_tile(h, i, last=False):
                for rows, tokens in tile_parts(h, i, last):
                    sp.dma_start(xr[i % 2][rows, :], x1_flat[tokens, :]).then_inc(s_xr[i % 2], 16)

            def store_tile(h, i, last=False):
                sp.wait_ge(s_yo, 5 * h + i + 3)
                for rows, tokens in tile_parts(h, i, last):
                    sp.dma_start(out_flat[tokens, :], yo[i % 2][rows, :]).then_inc(s_out[i % 2], 16)

            def next_x1(j):
                sp.wait_ge(s_mn, 3 * j)
                load_x1(j)

            for n in range(EARLY + 2, PIECES):
                load_piece(n)
            sp.wait_ge(s_whi, PIECES)
            sp.wait_ge(s_wlo, PIECES)
            for i in range(2):
                load_residual_tile(0, i)
            with sp.Fori(0, PAIRS) as h:
                next_x1(2 * h + 1)
                store_tile(h, 0)
                load_residual_tile(h, 2)
                store_tile(h, 1)
                load_residual_tile(h, 3)
                next_x1(2 * h + 2)
                store_tile(h, 2)
                load_residual_tile(h, 4)
                store_tile(h, 3)
                load_residual_tile(h + 1, 1)
                store_tile(h, 4)
                load_residual_tile(h + 1, 0)
            store_tile(PAIRS, 0)
            load_residual_tile(PAIRS, 2, True)
            store_tile(PAIRS, 1)
            store_tile(PAIRS, 2, True)
            sp.wait_ge(s_out[0], 16 * (tile_transfers(PAIRS, 2, True) + 1))
            sp.wait_ge(s_out[1], 16 * (tile_transfers(PAIRS, 1) + 1))

        @block.gpsimd
        def _(pool):
            nc.gpsimd.memset(halfpow[:, :], -0.5).then_inc(s_pconst, 1)
            nc.gpsimd.memset(ones[:, :], 1.0).then_inc(s_pconst, 1)
            for s in range(2):
                for half in range(2):
                    nc.gpsimd.memset(kblk[s][half][:, :, :].bitcast(F32), 0.0).then_inc(s_zero, 1)

            def ctx_lo(g, k):
                pool.wait_ge(s_ctxhi, KT * g + k + 1)
                nc.gpsimd.tensor_tensor(ctxT[LO][:, k, :], ctx_raw[:, k, :], ctxT[HI][:, k, :].bitcast(F32),
                                        ALU.subtract).then_inc(s_ctxlo, 1)

            def layer_pow(g, b):
                pool.wait_ge(s_ln, 3 * (NB * g + b) + 3)
                nc.gpsimd.tensor_tensor(rstd[0:L, b:b + 1], var[0:L, b:b + 1], halfpow[0:L, b:b + 1], ALU.pow)\
                  .then_inc(s_pow, 1)

            def normalise_probs(g, i):
                n = STEPS * g + i
                pool.wait_ge(s_inv, n + 1)
                nc.gpsimd.tensor_tensor(probs[i % 2][:, :, :], probs[i % 2][:, :, :],
                                        rinv[:, i % 4, :].unsqueeze(2).broadcast_to([L, HPG, TAIL]), ALU.mult)\
                  .then_inc(s_norm, 1)

            def step(g, i, last=False):
                for ahead in step_ahead(g, i):
                    normalise_probs(*ahead)
                if last and i == STEPS - 1:
                    ffn_rstd(0)
                if last and i in EARLY_AT:
                    piece_lo(EARLY_AT[i])
                if not last and i in NORM_AT:
                    layer_pow(g + 1, NORM_AT[i])
                if not last:
                    for k in CTX_AT.get(i, ()):
                        ctx_lo(g + 1, k)

            def weight_lo(name, k):
                pool.wait_ge(s_whole[name], k + 1)
                nc.gpsimd.tensor_tensor(W[name][LO][:, k, :], raw[name][:, k, :], W[name][HI][:, k, :].bitcast(F32), ALU.subtract)\
                  .then_inc(s_split[name], 1)

            pool.wait_ge(s_pconst, 2)
            for b in range(NB):
                layer_pow(0, b)
            for k in range(KT):
                ctx_lo(0, k)
            for name in ("wv", "wo"):
                for k in range(KT):
                    weight_lo(name, k)

            def ffn_rstd(j):
                pool.wait_ge(s_bln, 3 * j + 3)
                nc.gpsimd.tensor_tensor(rstd[:, 0:3], var[:, 0:3], halfpow[:, 0:3], ALU.pow).then_inc(s_bpow, 1)

            def piece_lo(n):
                s, cols = n % 2, 256 if n < FT else D
                pool.wait_ge(s_scale, n + 1)
                nc.gpsimd.tensor_tensor(scale_b[s][:, 0:cols], scale[s][:, 0:cols], scale_a[s][:, 0:cols], ALU.subtract)\
                  .then_inc(s_scaleb, 1)
                pool.wait_ge(s_dec, n + 1)
                if n < PIECES - 1:
                    nc.gpsimd.tensor_tensor(*piece_operands(n, HI, 2), ALU.mult)
                pool.wait_ge(s_scaleb, n + 1)
                nc.gpsimd.tensor_tensor(*piece_operands(n, LO, None), ALU.mult).then_inc(s_wlo, 1)

            with pool.If(wants_full(pool)):
                pool.wait_ge(s_zero, 4)
                with pool.Fori(0, B) as b:
                    pool.wait_ge(f_ln, 3 * b + 3)
                    nc.gpsimd.tensor_tensor(rstd[0:L, 0:1], var[0:L, 0:1], halfpow[0:L, 0:1], ALU.pow).then_inc(f_pow, 1)
                    for hg in range(HG):
                        pool.wait_ge(f_inv, HG * b + hg + 1)
                        nc.gpsimd.tensor_tensor(probs_full, probs_full, rinv[:, 0, :].unsqueeze(2).broadcast_to([L, HPG, KC]),
                                                ALU.mult).then_inc(f_norm, 1)
                pool.wait_ge(f_norm, HG * B)
                phase_barrier(pool)
                for n in range(EARLY):
                    piece_lo(n)
                ffn_rstd(0)
            with pool.Else():
                for i in range(AHEAD):
                    normalise_probs(0, i)
                for i in range(LOOP_FROM):
                    step(0, i)
                with pool.Fori(0, GROUPS - 1) as g:
                    for i in range(LOOP_FROM, STEPS):
                        step(g, i)
                    for i in range(LOOP_FROM):
                        step(g + 1, i)
                for i in range(LOOP_FROM, STEPS):
                    step(GROUPS - 1, i, True)

            def hidden_lo(j, par, t):
                pool.wait_ge(s_hhi, FT * j + t + 1)
                nc.gpsimd.tensor_tensor(hT[LO][:, t, hidden_cols(par)], hidden[(par + t) % 2][:, :], hT[HI][:, t, hidden_cols(par)].bitcast(F32),
                                        ALU.subtract).then_inc(s_hlo, 1)

            def rms_tile(h, i, last=False):
                slot, rows = i % 2, tile_rows(i, last)
                pool.wait_ge(s_ms, 5 * h + i + 1)
                nc.gpsimd.tensor_tensor(rrms[0:rows, slot:slot + 1], ms[0:rows, slot:slot + 1], halfpow[0:rows, 0:1], ALU.pow)\
                  .then_inc(s_rr, 1)

            for t in range(FT):
                if EARLY + t < PIECES:
                    piece_lo(EARLY + t)
                hidden_lo(0, 0, t)
            with pool.Fori(0, PAIRS) as h:
                for par in range(2):
                    ffn_rstd(2 * h + par + 1)
                    for i in TILES_OF[par]:
                        rms_tile(h, i)
                    for t in range(FT):
                        hidden_lo(2 * h + par + 1, (par + 1) % 2, t)
            for i in range(3):
                rms_tile(PAIRS, i, True)

        @block.scalar
        def _(act):
            def weight_hi(name, k):
                if k == 0:
                    act.wait_ge(s_w[name], 16)
                src = raw[name][:, k, :]
                if name in ("wq", "wg"):
                    nc.scalar.activation(W[name][HI][:, k, :], src, ACT.Copy, scale=normw[:, k:k + 1]).then_inc(s_whole[name], 1)
                else:
                    nc.scalar.activation(W[name][HI][:, k, :], src, ACT.Copy).then_inc(s_whole[name], 1)

            def ctx_hi(g, k):
                if k == 0:
                    act.wait_ge(s_ctx, 16 * (g + 1))
                    if not isinstance(g, int) or g:
                        act.wait_ge(s_pj, split_count(g - 1, "K3"))
                nc.scalar.activation(ctxT[HI][:, k, :], ctx_raw[:, k, :], ACT.Copy).then_inc(s_ctxhi, 1)

            def job_hi(c, name):
                n = int(name[1])
                src = job_bank(c, name)
                if name[0] == "G":
                    act.wait_ge(s_g, NB * c + n + 1)
                    if not isinstance(c, int) or c:
                        act.wait_ge(s_x1st[n], 16 * c + 16)
                    nc.scalar.activation(gate[n][:, :], src[0:L, :], ACT.Tanh, scale=0.5).then_inc(s_gate, 1)
                    return
                act.wait_ge(s_pj, split_count(c, name))
                if name[0] == "V":
                    last = nc.scalar.activation(vv[HI][0:TAIL, n, :], src[0:TAIL, :], ACT.Copy)
                elif name[0] == "X":
                    last = nc.scalar.activation(xT[HI][:, :, L * n:L * n + L],
                                                src[:, 0:KT * L].rearrange("p (k t) -> p k t", k=KT), ACT.Copy)
                elif name[0] == "Q":
                    last = nc.scalar.activation(qT[n % 2][HI][:, :], src[:, 0:GT], ACT.Copy, scale=HD ** -0.5)
                else:
                    for h in range(HPG):
                        p = slice(HD * h, HD * h + HD)
                        last = nc.scalar.activation(kblk[n % 2][HI][p, h, :], src[p, 0:KC], ACT.Copy)
                last.then_inc(s_pjhi, 1)

            def exp_step(g, i):
                n = STEPS * g + i
                act.wait_ge(s_max, n + 1)
                if not isinstance(n, int) or n >= 2:
                    act.wait_ge(s_pt, n - 1)
                for h in range(HPG):
                    last = nc.scalar.activation(probs[i % 2][:, h, :], SC[i % 2][0:L, TAIL * h:TAIL * h + TAIL], ACT.Exp,
                                                bias=nmax[:, i % 4, h:h + 1], accum_out=rsum[:, i % 4, h:h + 1])
                last.then_inc(s_exp, 1)

            def probsT_hi(g, i):
                n = STEPS * g + i
                act.wait_ge(s_pt, n + 1)
                if not isinstance(n, int) or n >= 2:
                    act.wait_ge(s_pv, n - 1)
                nc.scalar.activation(pT[i % 2][HI][0:TAIL, :, :].rearrange("k h t -> k (h t)"), PT[i % 2][0:TAIL, 0:GT],
                                     ACT.Copy).then_inc(s_pthi, 1)

            def attn_hi(g, i):
                hg, b = i // NB, i % NB
                act.wait_ge(s_pv, STEPS * g + i + 1)
                for h in range(HPG):
                    p = slice(HD * h, HD * h + HD)
                    last = nc.scalar.activation(oT[HI][p, hg, L * b:L * b + L], PV[i % 2][p, L * h:L * h + L], ACT.Copy)
                last.then_inc(s_ohi, 1)

            def step(g, i, last=False):
                probsT_hi(g, i)
                if not isinstance(g, int) or g or i:
                    attn_hi(*last_step(g, i))
                for ahead in step_ahead(g, i):
                    exp_step(*ahead)
                for job in beside(g, i):
                    if job[1][0] != "O":
                        job_hi(*job)
                if not last:
                    for k in CTX_AT.get(i, ()):
                        ctx_hi(g + 1, k)

            act.wait_ge(s_gates, 32)
            nc.scalar.activation(tanhs[:, :], gates[:, :], ACT.Tanh).then_inc(s_tanh, 1)
            act.wait_ge(s_normw, 16)
            for k in range(KT):
                weight_hi("wq", k)
                if k >= 2:
                    job_hi(0, f"X{k - 2}")
            for k in range(KT):
                if k < 2:
                    job_hi(0, f"X{k + 2}")
                ctx_hi(0, k)
            for k in range(KT):
                weight_hi("wk", k)
            for k in range(KT):
                weight_hi("wv", k)
            job_hi(0, "Q0")
            act.wait_ge(s_zero, 4)
            job_hi(0, "K0")
            for k in range(KT):
                weight_hi("wg", k)
            for k in range(KT):
                weight_hi("wo", k)

            def mT_hi(j, par, m):
                n = 3 * j + m
                bank_t = tile_bank(par, m)
                act.wait_ge(s_mt, n + 1)
                rows = ROWS[m]
                nc.scalar.activation(mT[HI][:, :, 128 * m:128 * m + rows],
                                     bank_t[:, 0:KT * rows].rearrange("p (k t) -> p k t", k=KT), ACT.Copy).then_inc(s_mthi, 1)

            def full_hi(b, name):
                act.wait_ge(f_pj, full_count(b, name))
                n = int(name[1:] or 0)
                if name[0] == "V":
                    last = nc.scalar.activation(vv[HI][:, n, :], FJ[:, :], ACT.Copy)
                elif name[0] == "X":
                    last = nc.scalar.activation(xT[HI][:, :, 0:L], FJ[:, 0:KT * L].rearrange("p (k t) -> p k t", k=KT), ACT.Copy)
                elif name[0] == "Q":
                    last = nc.scalar.activation(qT[0][HI][:, 0:L], FJ[:, 0:L], ACT.Copy, scale=HD ** -0.5)
                else:
                    for h in range(HPG):
                        p = slice(HD * h, HD * h + HD)
                        last = nc.scalar.activation(kblk[0][HI][p, h, :], FJ[p, 0:KC], ACT.Copy)
                last.then_inc(f_pjhi, 1)

            with act.If(wants_full(act)):
                job_hi(0, "V0")
                act.wait_ge(s_pjlo, len(HEAD))
                with act.Fori(0, B) as b:
                    act.wait_ge(f_load, 48 * b + 48)
                    for k in range(KT):
                        last = nc.scalar.activation(ctxT[HI][:, k, 0:M], ctx_raw[:, k, 0:M], ACT.Copy)
                    last.then_inc(f_ctxhi, 1)
                    for name in FULL_JOBS[0:CHUNKS + 1]:
                        full_hi(b, name)
                    for hg in range(HG):
                        i = HG * b + hg
                        full_hi(b, f"K{hg}")
                        full_hi(b, f"Q{hg}")
                        act.wait_ge(f_max, i + 1)
                        for c in range(CHUNKS):
                            for h in range(HPG):
                                last = nc.scalar.activation(probs_full[:, h, CHUNK * c:CHUNK * c + CHUNK],
                                                            FSC[c][0:L, CHUNK * h:CHUNK * h + CHUNK], ACT.Exp,
                                                            bias=nmax[:, 0, h:h + 1], accum_out=rsum_c[:, c, h:h + 1])
                        last.then_inc(f_exp, 1)
                        for c in range(CHUNKS):
                            act.wait_ge(f_pt, CHUNKS * i + c + 1)
                            if c:
                                act.wait_ge(f_pv, CHUNKS * i + c)
                            nc.scalar.activation(pT[0][HI][:, :, :].rearrange("k h t -> k (h t)"), FPT[:, 0:GT], ACT.Copy)\
                              .then_inc(f_pthi, 1)
                        act.wait_ge(f_pv, CHUNKS * i + CHUNKS)
                        for h in range(HPG):
                            p = slice(HD * h, HD * h + HD)
                            last = nc.scalar.activation(oT[HI][p, hg, 0:L], FPV[p, L * h:L * h + L], ACT.Copy)
                        last.then_inc(f_ohi, 1)
                    act.wait_ge(f_g, b + 1)
                    nc.scalar.activation(gate[0][:, :], FJ[0:L, :], ACT.Tanh, scale=0.5).then_inc(f_gate, 1)
                act.wait_ge(f_gate, B)
                phase_barrier(act)
                for m in range(3):
                    mT_hi(0, 0, m)
            with act.Else():
                for i in range(AHEAD):
                    exp_step(0, i)
                job_hi(0, "V0")
                for i in range(LOOP_FROM):
                    step(0, i)
                with act.Fori(0, GROUPS - 1) as g:
                    for i in range(LOOP_FROM, STEPS):
                        step(g, i)
                    for i in range(LOOP_FROM):
                        step(g + 1, i)
                for i in range(LOOP_FROM, STEPS):
                    step(GROUPS - 1, i, True)
                attn_hi(GROUPS - 1, STEPS - 1)
                for m in range(3):
                    mT_hi(0, 0, m)

            def gate_up(j, par, t):
                n = FT * j + t
                act.wait_ge(s_gu, n + 1)
                if not isinstance(n, int) or n:
                    act.wait_ge(s_sg, n)
                nc.scalar.activation(tgate[:, :], bank[2 * ((par + t) % 2)][:, 0:TG], ACT.Tanh, scale=0.5 * FP4_UNIT).then_inc(s_tg, 1)

            def hidden_hi(j, par, t):
                act.wait_ge(s_h, FT * j + t + 1)
                nc.scalar.activation(hT[HI][:, t, hidden_cols(par)], hidden[(par + t) % 2][:, :], ACT.Copy).then_inc(s_hhi, 1)

            def square(h, i, last=False):
                slot, rows = i % 2, tile_rows(i, last)
                before = tile_transfers(h, i) - len(OUT_TILES[i][1])
                act.wait_ge(s_out[slot], 16 * (before + 1))
                act.wait_ge(s_y, 5 * h + i + 1)
                nc.scalar.activation(yo[slot][0:rows, :], bank[6 + slot][0:rows, :], ACT.Square,
                                     accum_out=ssq[0:rows, slot:slot + 1]).then_inc(s_sq, 1)

            def all_gate_up(j, par):
                for t in range(FT):
                    gate_up(j, par, t)
                    if t >= 1:
                        hidden_hi(j, par, t - 1)
                hidden_hi(j, par, FT - 1)

            all_gate_up(0, 0)
            act.wait_ge(s_stored, 1)
            with act.Fori(0, PAIRS) as h:
                for par in range(2):
                    j = 2 * h + par
                    for i in TILES_OF[par]:
                        square(h, i)
                        if i == TILES_OF[par][0]:
                            for m in range(3):
                                mT_hi(j + 1, (par + 1) % 2, m)
                    all_gate_up(j + 1, (par + 1) % 2)
            for i in range(3):
                square(PAIRS, i, True)

        @block.vector
        def _(dve):
            nc.vector.memset(mv[:, :, :], 0.0).then_inc(s_setup, 1)
            nc.vector.memset(mbias[:, :, :], 0.0).then_inc(s_setup, 1)

            def weight_lo(name, k):
                dve.wait_ge(s_whole[name], k + 1)
                lo, hi = W[name][LO][:, k, :], W[name][HI][:, k, :].bitcast(F32)
                if name in ("wq", "wg"):
                    last = nc.vector.scalar_tensor_tensor(lo, raw[name][:, k, :], normw[:, k:k + 1], hi, ALU.mult, ALU.subtract)
                else:
                    last = nc.vector.tensor_tensor(lo, raw[name][:, k, :], hi, ALU.subtract)
                last.then_inc(s_split[name], 1)

            def job_lo(c, name):
                n = int(name[1])
                dve.wait_ge(s_pjhi, split_count(c, name))
                src = job_bank(c, name)
                if name[0] == "V":
                    last = nc.vector.tensor_tensor(vv[LO][0:TAIL, n, :], src[0:TAIL, :], vv[HI][0:TAIL, n, :].bitcast(F32), ALU.subtract)
                elif name[0] == "X":
                    last = nc.vector.tensor_tensor(xT[LO][:, :, L * n:L * n + L], src[:, 0:KT * L].rearrange("p (k t) -> p k t", k=KT),
                                                   xT[HI][:, :, L * n:L * n + L].bitcast(F32), ALU.subtract)
                elif name[0] == "Q":
                    last = nc.vector.scalar_tensor_tensor(qT[n % 2][LO][:, :], src[:, 0:GT], HD ** -0.5,
                                                          qT[n % 2][HI][:, :].bitcast(F32), ALU.mult, ALU.subtract)
                else:
                    for h in range(HPG):
                        p = slice(HD * h, HD * h + HD)
                        last = nc.vector.tensor_tensor(kblk[n % 2][LO][p, h, :], src[p, 0:KC],
                                                       kblk[n % 2][HI][p, h, :].bitcast(F32), ALU.subtract)
                last.then_inc(s_pjlo, 1)

            def layer_stats(g, b):
                c = 3 * (NB * g + b)
                dve.wait_ge(s_x[b], 16 * (g + 1))
                nc.vector.bn_stats(stats[0:L, b, :], xn[:, b, :]).then_inc(s_ln, 1)
                wait_apart(dve, s_ln, c + 1)
                nc.vector.bn_aggr(mv[0:L, b, :], stats[0:L, b, :]).then_inc(s_ln, 1)
                dve.wait_ge(s_ln, c + 2)
                nc.vector.tensor_scalar(var[0:L, b:b + 1], mv[0:L, b, 1:2], 1.0 + RMS_EPS, LN_EPS * RMS_EPS, ALU.mult, ALU.add)\
                  .then_inc(s_ln, 1)

            def normalise(g, b):
                dve.wait_ge(s_pow, NB * g + b + 1)
                nc.vector.tensor_scalar(xn[:, b, :], xn[:, b, :], mv[0:L, b, 0:1], rstd[0:L, b:b + 1], ALU.subtract, ALU.mult)\
                  .then_inc(s_xn, 1)

            def row_max(g, i):
                n = STEPS * g + i
                dve.wait_ge(s_sc, n + 1)
                nc.vector.tensor_reduce(nmax[:, i % 4, :], SC[i % 2][0:L, 0:KC].rearrange("t (h k) -> t h k", h=HPG),
                                        AXIS_X, ALU.max, negate=True).then_inc(s_max, 1)

            def row_inverse(g, i):
                dve.wait_ge(s_exp, STEPS * g + i + 1)
                nc.vector.reciprocal(rinv[:, i % 4, :], rsum[:, i % 4, :]).then_inc(s_inv, 1)

            def probsT_lo(g, i):
                dve.wait_ge(s_pthi, STEPS * g + i + 1)
                nc.vector.tensor_tensor(pT[i % 2][LO][0:TAIL, :, :].rearrange("k h t -> k (h t)"), PT[i % 2][0:TAIL, 0:GT],
                                        pT[i % 2][HI][0:TAIL, :, :].rearrange("k h t -> k (h t)").bitcast(F32), ALU.subtract)\
                  .then_inc(s_ptlo, 1)

            def attn_lo(g, i):
                hg, b = i // NB, i % NB
                dve.wait_ge(s_ohi, STEPS * g + i + 1)
                for h in range(HPG):
                    p = slice(HD * h, HD * h + HD)
                    last = nc.vector.tensor_tensor(oT[LO][p, hg, L * b:L * b + L], PV[i % 2][p, L * h:L * h + L],
                                                   oT[HI][p, hg, L * b:L * b + L].bitcast(F32), ALU.subtract)
                last.then_inc(s_olo, 1)

            def output(g, b):
                n = NB * g + b
                dve.wait_ge(s_gate, n + 1)
                dve.wait_ge(s_o, n + 1)
                nc.vector.scalar_tensor_tensor(gate[b][:, :], gate[b][:, :], 1.0, job_bank(g + 1, f"O{b}")[0:L, :],
                                               ALU.add, ALU.mult).then_inc(s_gated, 1)
                dve.wait_ge(s_gated, n + 1)
                dve.wait_ge(s_xa[b % 2], 32 * g + 16 * (b // 2 + 1))
                nc.vector.scalar_tensor_tensor(gate[b][:, :], gate[b][:, :], coef_a[0:L, bass.ds(n, 1)], xa[:, b % 2, :],
                                               ALU.mult, ALU.add).then_inc(s_x1, 1)

            def step(g, i, last=False):
                def dequant(stage):
                    if last and i in EARLY_AT:
                        decode(EARLY_AT[i], stage)

                probsT_lo(g, i)
                dequant(0)
                for ahead in step_ahead(g, i):
                    row_max(*ahead)
                if not last and i in NORM_AT:
                    layer_stats(g + 1, NORM_AT[i])
                dequant(1)
                if not isinstance(g, int) or g or i:
                    attn_lo(*last_step(g, i))
                if last and i == STEPS - 1:
                    ffn_stats(0)
                dequant(2)
                for ahead in step_ahead(g, i):
                    row_inverse(*ahead)
                dequant(3)
                if not last and i - 1 in NORM_AT:
                    normalise(g + 1, NORM_AT[i - 1])
                for c, name in beside(g, i):
                    if name[0] == "O":
                        output(c - 1, int(name[1]))
                    elif name[0] != "G":
                        job_lo(c, name)
                dequant(4)
                if last and i == STEPS - 1:
                    for m in range(3):
                        ffn_normalise(0, m)

            for b in range(NB):
                layer_stats(0, b)
            for b in range(NB):
                normalise(0, b)
            for k in range(KT):
                weight_lo("wq", k)
                if k >= 2:
                    job_lo(0, f"X{k - 2}")
            for b in (2, 3):
                job_lo(0, f"X{b}")
            for k in range(KT):
                weight_lo("wk", k)
            job_lo(0, "Q0")
            dve.wait_ge(s_mask, 32)
            nc.vector.tensor_reduce(flags[:, 0:1], maskall[:, :], AXIS_X, ALU.max).then_inc(s_setup, 1)
            nc.vector.tensor_reduce(flags[:, 1:2], maskall[:, 0:M - TAIL], AXIS_X, ALU.max).then_inc(s_setup, 1)
            dve.wait_ge(s_setup, 4)
            for f in range(2):
                nc.vector.tensor_scalar(flagdiag[:, f, :], ident[0:B, 0:B], flags[:, f:f + 1], None, ALU.mult).then_inc(s_setup, 1)
            nc.vector.tensor_scalar(mbias[0:1, :, :], masktail[:, :, :], 1.0, MASKED, ALU.subtract, ALU.mult).then_inc(s_setup, 1)
            job_lo(0, "K0")
            dve.wait_ge(s_flags, 1)
            nc.vector.tensor_reduce(headmax[:, :], FLAGS[0:1, B:2 * B], AXIS_X, ALU.max).then_inc(s_setup, 1)
            dve.wait_ge(s_setup, 8)
            nc.vector.tensor_copy(headkeep[:, :], headmax[:, :]).then_inc(s_setup, 1)
            dve.wait_ge(s_tanh, 1)
            nc.vector.tensor_scalar(coef_a[0:L, :], FLAGS[0:L, 0:B], tanhs[0:L, 0:1], 0.5, ALU.mult, ALU.mult).then_inc(s_setup, 1)
            for k in range(KT):
                weight_lo("wg", k)

            SIGN, MAGNITUDE = 0x80008000 - (1 << 32), 0x0E000E00

            def decode(n, stage):
                s = n % 2
                scales, word, code = scale[s], words[s], fp4[s][:, :]
                if stage == 0:
                    if n >= 2:
                        dve.wait_ge(s_wlo, n - 1)
                        dve.wait_ge(s_whi, n - 1)
                    else:
                        dve.wait_ge(s_shift, 16)
                    dve.wait_ge(s_words[s], words_loaded(n))
                    cols = 256 if n < FT else D
                    nc.vector.tensor_scalar(scale_a[s][:, 0:cols].bitcast(I16), scales[:, 0:cols].bitcast(I16), -2, None,
                                            ALU.bitwise_and).then_inc(s_scale, 1)
                    if n < FT:
                        nc.vector.tensor_scalar(word[:, 256:512], word[:, 0:256], shift[:, 1:2], None, ALU.logical_shift_left)\
                          .then_inc(s_shifted, 1)
                elif stage == 1:
                    if n < FT:
                        dve.wait_ge(s_shifted, 3 * n + 1)
                        nc.vector.tensor_scalar(word[:, 0:256], word[:, 0:256], shift[:, 0:1], None, ALU.logical_shift_left)\
                          .then_inc(s_shifted, 1)
                    elif n < PIECES - 1:
                        nc.vector.tensor_scalar(word[:, :], word[:, :], shift[:, 2:3], None, ALU.logical_shift_left)\
                          .then_inc(s_shifted, 2)
                    else:
                        nc.vector.tensor_scalar(word[:, :], word[:, :], shift[:, 3:4], shift[:, 4:5],
                                                ALU.logical_shift_right, ALU.logical_shift_left).then_inc(s_shifted, 2)
                elif stage == 2:
                    dve.wait_ge(s_shifted, 3 * n + 2)
                    nc.vector.tensor_scalar(code, word[:, :], 3, MAGNITUDE, ALU.logical_shift_right, ALU.bitwise_and)\
                      .then_inc(s_shifted, 1)
                elif stage == 3:
                    dve.wait_ge(s_shifted, 3 * n + 3)
                    nc.vector.scalar_tensor_tensor(code, word[:, :], SIGN, code, ALU.bitwise_and, ALU.bitwise_or).then_inc(s_dec, 1)
                else:
                    dve.wait_ge(s_dec, n + 1)
                    for part in range(2 if n < PIECES - 1 else 1):
                        last = nc.vector.tensor_tensor(*piece_operands(n, HI, part), ALU.mult)
                    last.then_inc(s_whi, 1)

            def decode_all(n):
                for stage in range(5):
                    decode(n, stage)

            def ffn_stats(j):
                dve.wait_ge(s_xb, 32 * (j + 1))
                for m, rows in enumerate(ROWS):
                    last = nc.vector.bn_stats(stats[0:rows, m, :], xb[0:rows, m, :])
                last.then_inc(s_bln, 1)
                wait_apart(dve, s_bln, 3 * j + 1)
                for m, rows in enumerate(ROWS):
                    last = nc.vector.bn_aggr(mv[0:rows, m, :], stats[0:rows, m, :])
                last.then_inc(s_bln, 1)
                dve.wait_ge(s_bln, 3 * j + 2)
                nc.vector.tensor_scalar(var[:, 0:3], mv[:, 0:3, 1], LN_EPS, None, ALU.add).then_inc(s_bln, 1)

            def ffn_normalise(j, m):
                rows = ROWS[m]
                if m == 0:
                    dve.wait_ge(s_bpow, j + 1)
                nc.vector.tensor_scalar(mn[m][0:rows, :].rearrange("t (e p) -> t p e", e=8),
                                        xb[0:rows, m, :].rearrange("t (p e) -> t p e", e=8), mv[0:rows, m, 0:1], rstd[0:rows, m:m + 1],
                                        ALU.subtract, ALU.mult).then_inc(s_mn, 1)

            def mT_lo(j, par, m):
                rows = ROWS[m]
                dve.wait_ge(s_mthi, 3 * j + m + 1)
                nc.vector.tensor_tensor(mT[LO][:, :, 128 * m:128 * m + rows],
                                        tile_bank(par, m)[:, 0:KT * rows].rearrange("p (k t) -> p k t", k=KT),
                                        mT[HI][:, :, 128 * m:128 * m + rows].bitcast(F32), ALU.subtract).then_inc(s_mtlo, 1)

            def full_lo(b, name):
                dve.wait_ge(f_pjhi, full_count(b, name))
                n = int(name[1:] or 0)
                if name[0] == "V":
                    last = nc.vector.tensor_tensor(vv[LO][:, n, :], FJ[:, :], vv[HI][:, n, :].bitcast(F32), ALU.subtract)
                elif name[0] == "X":
                    last = nc.vector.tensor_tensor(xT[LO][:, :, 0:L], FJ[:, 0:KT * L].rearrange("p (k t) -> p k t", k=KT),
                                                   xT[HI][:, :, 0:L].bitcast(F32), ALU.subtract)
                elif name[0] == "Q":
                    last = nc.vector.scalar_tensor_tensor(qT[0][LO][:, 0:L], FJ[:, 0:L], HD ** -0.5, qT[0][HI][:, 0:L].bitcast(F32),
                                                          ALU.mult, ALU.subtract)
                else:
                    for h in range(HPG):
                        p = slice(HD * h, HD * h + HD)
                        last = nc.vector.tensor_tensor(kblk[0][LO][p, h, :], FJ[p, 0:KC], kblk[0][HI][p, h, :].bitcast(F32),
                                                       ALU.subtract)
                last.then_inc(f_pjlo, 1)

            with dve.If(wants_full(dve)):
                job_lo(0, "V0")
                dve.wait_ge(s_pjlo, len(HEAD))
                for half in range(2):
                    nc.vector.memset(ctxT[half][:, :, M:KC].bitcast(F32), 0.0).then_inc(f_ctx, 1)
                nc.vector.memset(mbias_full[0:1, M:KC], -MASKED).then_inc(f_bias, 1)
                with dve.Fori(0, B) as b:
                    dve.wait_ge(f_load, 48 * b + 48)
                    nc.vector.tensor_scalar(mbias_full[0:1, 0:M], maskrow[:, 0:M], 1.0, MASKED, ALU.subtract, ALU.mult)\
                      .then_inc(f_bias, 1)
                    nc.vector.bn_stats(stats[0:L, 0, :], xa[:, 0, :]).then_inc(f_ln, 1)
                    wait_apart(dve, f_ln, 3 * b + 1)
                    nc.vector.bn_aggr(mv[0:L, 0, :], stats[0:L, 0, :]).then_inc(f_ln, 1)
                    dve.wait_ge(f_ln, 3 * b + 2)
                    nc.vector.tensor_scalar(var[0:L, 0:1], mv[0:L, 0, 1:2], 1.0 + RMS_EPS, LN_EPS * RMS_EPS, ALU.mult, ALU.add)\
                      .then_inc(f_ln, 1)
                    dve.wait_ge(f_pow, b + 1)
                    nc.vector.tensor_scalar(xn[:, 0, :], xa[:, 0, :], mv[0:L, 0, 0:1], rstd[0:L, 0:1], ALU.subtract, ALU.mult)\
                      .then_inc(f_xn, 1)
                    dve.wait_ge(f_ctxhi, b + 1)
                    for k in range(KT):
                        last = nc.vector.tensor_tensor(ctxT[LO][:, k, 0:M], ctx_raw[:, k, 0:M], ctxT[HI][:, k, 0:M].bitcast(F32),
                                                       ALU.subtract)
                    last.then_inc(f_ctx, 1)
                    for name in FULL_JOBS[0:CHUNKS + 1]:
                        full_lo(b, name)
                    for hg in range(HG):
                        i = HG * b + hg
                        full_lo(b, f"K{hg}")
                        full_lo(b, f"Q{hg}")
                        dve.wait_ge(f_sc, i + 1)
                        for c in range(CHUNKS):
                            nc.vector.tensor_reduce(nmax_c[:, c, :], FSC[c][0:L, :].rearrange("t (h k) -> t h k", h=HPG),
                                                    AXIS_X, ALU.max, negate=True).then_inc(f_maxc, 1)
                        dve.wait_ge(f_maxc, 4 * i + 3)
                        nc.vector.tensor_tensor(nmax[:, 0, :], nmax_c[:, 0, :], nmax_c[:, 1, :], ALU.min).then_inc(f_maxc, 1)
                        dve.wait_ge(f_maxc, 4 * i + 4)
                        nc.vector.tensor_tensor(nmax[:, 0, :], nmax[:, 0, :], nmax_c[:, 2, :], ALU.min).then_inc(f_max, 1)
                        dve.wait_ge(f_exp, i + 1)
                        nc.vector.tensor_tensor(rsum[:, 0, :], rsum_c[:, 0, :], rsum_c[:, 1, :], ALU.add).then_inc(f_sum, 1)
                        dve.wait_ge(f_sum, 2 * i + 1)
                        nc.vector.tensor_tensor(rsum[:, 0, :], rsum[:, 0, :], rsum_c[:, 2, :], ALU.add).then_inc(f_sum, 1)
                        dve.wait_ge(f_sum, 2 * i + 2)
                        nc.vector.reciprocal(rinv[:, 0, :], rsum[:, 0, :]).then_inc(f_inv, 1)
                        for c in range(CHUNKS):
                            dve.wait_ge(f_pthi, CHUNKS * i + c + 1)
                            nc.vector.tensor_tensor(pT[0][LO][:, :, :].rearrange("k h t -> k (h t)"), FPT[:, 0:GT],
                                                    pT[0][HI][:, :, :].rearrange("k h t -> k (h t)").bitcast(F32), ALU.subtract)\
                              .then_inc(f_ptlo, 1)
                        dve.wait_ge(f_ohi, i + 1)
                        for h in range(HPG):
                            p = slice(HD * h, HD * h + HD)
                            last = nc.vector.tensor_tensor(oT[LO][p, hg, 0:L], FPV[p, L * h:L * h + L],
                                                           oT[HI][p, hg, 0:L].bitcast(F32), ALU.subtract)
                        last.then_inc(f_olo, 1)
                    dve.wait_ge(f_gate, b + 1)
                    dve.wait_ge(f_o, b + 1)
                    nc.vector.scalar_tensor_tensor(gate[1][:, :], gate[0][:, :], 1.0, FO[0:L, :], ALU.add, ALU.mult)\
                      .then_inc(f_gated, 1)
                    dve.wait_ge(f_gated, b + 1)
                    nc.vector.scalar_tensor_tensor(xa[:, 0, :], gate[1][:, :], coef_a[0:L, bass.ds(b, 1)], xa[:, 0, :],
                                                   ALU.mult, ALU.add).then_inc(f_x1, 1)
                phase_barrier(dve)
                for n in range(EARLY):
                    decode_all(n)
                ffn_stats(0)
                for m in range(3):
                    ffn_normalise(0, m)
                for m in range(3):
                    mT_lo(0, 0, m)
            with dve.Else():
                for i in range(AHEAD):
                    row_max(0, i)
                    row_inverse(0, i)
                job_lo(0, "V0")
                for i in range(LOOP_FROM):
                    step(0, i)
                with dve.Fori(0, GROUPS - 1) as g:
                    for i in range(LOOP_FROM, STEPS):
                        step(g, i)
                    for i in range(LOOP_FROM):
                        step(g + 1, i)
                for i in range(LOOP_FROM, STEPS):
                    step(GROUPS - 1, i, True)
                attn_lo(GROUPS - 1, STEPS - 1)
                output(GROUPS - 1, 2)
                for m in range(2):
                    mT_lo(0, 0, m)
                output(GROUPS - 1, 3)
                mT_lo(0, 0, 2)

            dve.sem_inc(s_yo, 2)

            def hidden_tile(j, par, t):
                n = FT * j + t
                gate_bank, up_bank = (bank[2 * ((par + t) % 2) + i] for i in range(2))
                dve.wait_ge(s_tg, n + 1)
                if t >= 2:
                    dve.wait_ge(s_hlo, n - 1)
                tile = hidden[(par + t) % 2]
                nc.vector.scalar_tensor_tensor(tile[:, :], tgate[:, :], 1.0, gate_bank[:, 0:TG], ALU.add, ALU.mult)\
                  .then_inc(s_sg, 1)
                dve.wait_ge(s_sg, n + 1)
                nc.vector.scalar_tensor_tensor(tile[:, :], tile[:, :], FP4_UNIT * FP4_UNIT, up_bank[:, 0:TG], ALU.mult, ALU.mult)\
                  .then_inc(s_h, 1)

            def output_tile(h, i, last=False):
                n = 5 * h + i
                slot, rows = i % 2, tile_rows(i, last)
                dve.wait_ge(s_sq, n + 1)
                nc.vector.tensor_scalar(ms[0:rows, slot:slot + 1], ssq[0:rows, slot:slot + 1], 1.0 / D, RMS_EPS * (2 / FP4_UNIT) ** 2,
                                        ALU.mult, ALU.add).then_inc(s_ms, 1)
                dve.wait_ge(s_rr, n + 1)
                nc.vector.tensor_scalar(coef_y[0:rows, slot:slot + 1], rrms[0:rows, slot:slot + 1], tanhs[0:rows, 1:2], None,
                                        ALU.mult).then_inc(s_cy, 1)
                dve.wait_ge(s_cy, n + 1)
                dve.wait_ge(s_xr[slot], 16 * tile_transfers(h, i, last))
                nc.vector.scalar_tensor_tensor(yo[slot][0:rows, :], bank[6 + slot][0:rows, :], coef_y[0:rows, slot:slot + 1],
                                               xr[slot][0:rows, :], ALU.mult, ALU.add).then_inc(s_yo, 1)

            for t in range(FT):
                n = EARLY + t
                if n == FT:
                    dve.wait_ge(s_stored, 1)
                if n < PIECES:
                    decode(n, 0)
                    decode(n, 1)
                    decode(n, 2)
                    decode(n, 3)
                    decode(n, 4)
                hidden_tile(0, 0, t)
            with dve.Fori(0, PAIRS) as h:
                for par in range(2):
                    j = 2 * h + par
                    ffn_stats(j + 1)
                    for m in range(3):
                        ffn_normalise(j + 1, m)
                    for i in TILES_OF[par]:
                        output_tile(h, i)
                        if i == TILES_OF[par][0]:
                            for m in range(3):
                                mT_lo(j + 1, (par + 1) % 2, m)
                    for t in range(FT):
                        hidden_tile(j + 1, (par + 1) % 2, t)
            for i in range(3):
                output_tile(PAIRS, i, True)

        @block.tensor
        def _(pe):
            def open_bank(c, name):
                before = before_in_bank(c, name)
                if before is None:
                    return
                c, other = before
                if other[0] == "G":
                    pe.wait_ge(s_gate, NB * c + int(other[1]) + 1)
                elif other[0] == "O":
                    pe.wait_ge(s_gated, NB * (c - 1) + int(other[1]) + 1)
                else:
                    pe.wait_ge(s_pjlo, split_count(c, other))

            def job(c, name):
                n = int(name[1])
                dst = job_bank(c, name)
                open_bank(c, name)
                if name[0] == "V":
                    last = product(dst[0:TAIL, :], lambda a, k: ctxT[a][:, k, TAIL * n:TAIL * n + TAIL],
                                   lambda a, k: W["wv"][a][:, k, :], KT)
                elif name[0] == "K":
                    if n == 0:
                        pe.wait_ge(s_ctxlo, KT * (c + 1))
                    last = product(dst[:, 0:KC], lambda a, k: W["wk"][a][:, k, 128 * n:128 * n + 128],
                                   lambda a, k: ctxT[a][:, k, :], KT)
                elif name[0] == "X":
                    pe.wait_ge(s_xn, NB * c + n + 1)
                    for k in range(KT):
                        last = nc.tensor.transpose(dst[:, L * k:L * k + L], xn[:, n, 128 * k:128 * k + 128], ident[0:L, 0:L])
                elif name[0] == "Q":
                    if n == 0:
                        pe.wait_ge(s_pjlo, split_count(c, "X3"))
                    last = product(dst[:, 0:GT], lambda a, k: W["wq"][a][:, k, 128 * n:128 * n + 128],
                                   lambda a, k: xT[a][:, k, :], KT)
                elif name[0] == "G":
                    last = product(dst[0:L, :], lambda a, k: xT[a][:, k, L * n:L * n + L], lambda a, k: W["wg"][a][:, k, :], KT)
                    last.then_inc(s_g, 1)
                    return
                else:
                    pe.wait_ge(s_olo, STEPS * (c - 1) + NB * (HG - 1) + n + 1)
                    last = product(dst[0:L, :], lambda a, k: oT[a][:, k, L * n:L * n + L], lambda a, k: W["wo"][a][:, k, :], KT)
                    last.then_inc(s_o, 1)
                    return
                last.then_inc(s_pj, 1)

            def scores(g, i):
                n = STEPS * g + i
                hg, b = i // NB, i % NB
                dst = SC[i % 2][0:L, 0:KC].rearrange("t (h k) -> t h k", h=HPG)
                if b == 0:
                    pe.wait_ge(s_pjlo, split_count(g, max(f"K{hg}", f"Q{hg}", key=CYCLE.index)))
                if not isinstance(n, int) or n >= 2:
                    pe.wait_ge(s_exp, n - 1)
                nc.tensor.matmul(dst, ones[:, :], mbias[:, bass.ds(NB * g + b, 1), :].broadcast_to([128, HPG, TAIL]),
                                 start=True, stop=False)
                product(dst, lambda a, t: qT[hg % 2][a][:, L * b:L * b + L],
                        lambda a, t: kblk[hg % 2][a][:, :, TAIL * b:TAIL * b + TAIL], 1, first=False).then_inc(s_sc, 1)

            def transpose_probs(g, i):
                n = STEPS * g + i
                pe.wait_ge(s_norm, n + 1)
                if not isinstance(n, int) or n >= 2:
                    pe.wait_ge(s_ptlo, n - 1)
                for h in range(HPG):
                    last = nc.tensor.transpose(PT[i % 2][0:TAIL, L * h:L * h + L], probs[i % 2][:, h, :], ident[0:L, 0:L])
                last.then_inc(s_pt, 1)

            def attend(g, i):
                n = STEPS * g + i
                hg, b = i // NB, i % NB
                pe.wait_ge(s_ptlo, n + 1)
                if hg == 0:
                    pe.wait_ge(s_pjlo, split_count(g, f"V{b}"))
                if not isinstance(n, int) or n >= 2:
                    pe.wait_ge(s_olo, n - 1)
                product(PV[i % 2][:, 0:GT], lambda a, t: vv[a][0:TAIL, b, 128 * hg:128 * hg + 128],
                        lambda a, t: pT[i % 2][a][0:TAIL, :, :].rearrange("k h t -> k (h t)"), 1).then_inc(s_pv, 1)

            def step(g, i, last=False):
                transpose_probs(g, i)
                if not isinstance(g, int) or g or i:
                    attend(*last_step(g, i))
                for ahead in step_ahead(g, i):
                    scores(*ahead)
                if isinstance(g, int) and (g, i) == (0, 2):
                    pe.wait_ge(s_split["wg"], KT)
                for c, name in beside(g, i):
                    if (i, name) != (0, "V1"):
                        job(c, name)

            pe.wait_ge(s_ident, 16)
            for b in range(NB):
                job(0, f"X{b}")
            pe.wait_ge(s_split["wq"], KT)
            job(0, "Q0")
            pe.wait_ge(s_split["wk"], KT)
            job(0, "K0")
            pe.wait_ge(s_pconst, 2)
            pe.wait_ge(s_setup, 7)
            nc.tensor.matmul(FLAGS[0:L, 0:2 * B], ones[0:B, :], flagdiag[:, :, :].rearrange("p f b -> p (f b)"), start=True, stop=True)\
              .then_inc(s_flags, 1)
            pe.wait_ge(s_split["wv"], KT)
            job(0, "V0")

            def transpose_tile(j, par, m):
                rows = ROWS[m]
                wait_apart(pe, s_mn, 3 * j + m + 1)
                for k in range(KT):
                    last = nc.tensor.transpose(tile_bank(par, m)[:, rows * k:rows * k + rows],
                                               mn[m][0:rows, 128 * k:128 * k + 128], ident[0:rows, 0:rows])
                last.then_inc(s_mt, 1)

            def full_job(b, name):
                n = int(name[1:] or 0)
                if name == FULL_JOBS[0]:
                    pe.wait_ge(f_ctx, b + 3)
                else:
                    pe.wait_ge(f_pjlo, full_count(b, name) - 1)
                if name[0] == "V":
                    last = product(FJ[:, :], lambda a, k: ctxT[a][:, k, CHUNK * n:CHUNK * n + CHUNK],
                                   lambda a, k: W["wv"][a][:, k, :], KT)
                elif name[0] == "X":
                    pe.wait_ge(f_xn, b + 1)
                    for k in range(KT):
                        last = nc.tensor.transpose(FJ[:, L * k:L * k + L], xn[:, 0, 128 * k:128 * k + 128], ident[0:L, 0:L])
                elif name[0] == "Q":
                    last = product(FJ[:, 0:L], lambda a, k: W["wq"][a][:, k, 128 * n:128 * n + 128],
                                   lambda a, k: xT[a][:, k, 0:L], KT)
                else:
                    last = product(FJ[:, 0:KC], lambda a, k: W["wk"][a][:, k, 128 * n:128 * n + 128],
                                   lambda a, k: ctxT[a][:, k, :], KT)
                last.then_inc(f_pj, 1)

            with pe.If(wants_full(pe)):
                for name in ("wg", "wo"):
                    pe.wait_ge(s_split[name], KT)
                pe.wait_ge(s_pjlo, len(HEAD))
                with pe.Fori(0, B) as b:
                    for name in FULL_JOBS[0:CHUNKS + 1]:
                        full_job(b, name)
                    pe.wait_ge(f_bias, b + 2)
                    for hg in range(HG):
                        i = HG * b + hg
                        full_job(b, f"K{hg}")
                        full_job(b, f"Q{hg}")
                        pe.wait_ge(f_pjlo, full_count(b, f"Q{hg}"))
                        for c in range(CHUNKS):
                            cols = slice(CHUNK * c, CHUNK * c + CHUNK)
                            dst = FSC[c][0:L, :].rearrange("t (h k) -> t h k", h=HPG)
                            nc.tensor.matmul(dst, ones[:, :], mbias_full[:, cols].unsqueeze(1).broadcast_to([128, HPG, CHUNK]),
                                             start=True, stop=False)
                            last = product(dst, lambda a, t: qT[0][a][:, 0:L], lambda a, t: kblk[0][a][:, :, cols], 1, first=False)
                        last.then_inc(f_sc, 1)
                        pe.wait_ge(f_norm, i + 1)
                        if hg:
                            pe.wait_ge(f_olo, i)
                        for c in range(CHUNKS):
                            n = CHUNKS * i + c
                            if c:
                                pe.wait_ge(f_ptlo, n)
                            for h in range(HPG):
                                last = nc.tensor.transpose(FPT[:, L * h:L * h + L], probs_full[:, h, CHUNK * c:CHUNK * c + CHUNK],
                                                           ident[0:L, 0:L])
                            last.then_inc(f_pt, 1)
                            pe.wait_ge(f_ptlo, n + 1)
                            for p, (a, v) in enumerate(PASSES):
                                last = nc.tensor.matmul(FPV[:, 0:GT], vv[v][:, c, 128 * hg:128 * hg + 128],
                                                        pT[0][a][:, :, :].rearrange("k h t -> k (h t)"),
                                                        start=c == 0 and p == 0, stop=c == CHUNKS - 1 and p == 2)
                            last.then_inc(f_pv, 1)
                    product(FJ[0:L, :], lambda a, k: xT[a][:, k, 0:L], lambda a, k: W["wg"][a][:, k, :], KT).then_inc(f_g, 1)
                    pe.wait_ge(f_olo, HG * b + HG)
                    product(FO[0:L, :], lambda a, k: oT[a][:, k, 0:L], lambda a, k: W["wo"][a][:, k, :], KT).then_inc(f_o, 1)
                phase_barrier(pe)
                for m in range(3):
                    transpose_tile(0, 0, m)
            with pe.Else():
                for i in range(AHEAD):
                    scores(0, i)
                job(0, "V1")
                for i in range(LOOP_FROM):
                    step(0, i)
                pe.wait_ge(s_split["wo"], KT)
                with pe.Fori(0, GROUPS - 1) as g:
                    for i in range(LOOP_FROM, STEPS):
                        step(g, i)
                    for i in range(LOOP_FROM):
                        step(g + 1, i)
                for i in range(LOOP_FROM, STEPS):
                    step(GROUPS - 1, i, True)
                job(GROUPS, "O2")
                attend(GROUPS - 1, STEPS - 1)
                for m in range(2):
                    transpose_tile(0, 0, m)
                job(GROUPS, "O3")
                pe.wait_ge(s_gated, GROUPS * NB)
                transpose_tile(0, 0, 2)

            def gate_up(j, par, t, first=False):
                n = FT * j + t
                if t == 0:
                    pe.wait_ge(s_mtlo, 3 * j + 3)
                if first:
                    pe.wait_ge(s_whi, t + 1)
                    pe.wait_ge(s_wlo, t + 1)
                if not first or t >= 2:
                    pe.wait_ge(s_h, n - 1)
                for i in range(2):
                    cols = slice(128 * i, 128 * i + 128)
                    last = product(bank[2 * ((par + t) % 2) + i][:, 0:TG], lambda a, k: wgu[t][a][:, k, cols],
                                   lambda a, k: mT[a][:, k, :], KT)
                last.then_inc(s_gu, 1)

            def down(h, i, last_pair=False):
                slot, rows, col = i % 2, tile_rows(i, last_pair), OUT_TILES[i][0]
                pe.wait_ge(s_yo, 5 * h + i + 1 if i >= 2 else 5 * h + 2 - i)
                for t in range(FT):
                    if i in (0, 2) and not (last_pair and i):
                        pe.wait_ge(s_hlo, FT * (2 * h + i // 2) + t + 1)
                    for p, (a, b) in enumerate(PASSES):
                        last = nc.tensor.matmul(bank[6 + slot][0:rows, :], hT[a][:, t, col:col + rows], wdn[t // 2][b][:, t % 2, :],
                                                start=t == 0 and p == 0, stop=t == FT - 1 and p == 2)
                last.then_inc(s_y, 1)

            for t in range(FT):
                gate_up(0, 0, t, True)
            pe.wait_ge(s_wlo, PIECES)
            pe.wait_ge(s_whi, PIECES)
            with pe.Fori(0, PAIRS) as h:
                for par in range(2):
                    j = 2 * h + par
                    for i in TILES_OF[par]:
                        down(h, i)
                        if i == TILES_OF[par][0]:
                            for m in range(3):
                                transpose_tile(j + 1, (par + 1) % 2, m)
                    for t in range(FT):
                        gate_up(j + 1, (par + 1) % 2, t)
            for i in range(3):
                down(PAIRS, i, True)


INPUTS = ("x", "ctx_tail", "ctx_full", "mask", "mask_tail", "g_xattn", "g_ffn", "norm_w", "wq", "wk", "wv", "wo", "wg",
          "gu_packed", "gu_scales", "dn_packed", "dn_scales", "identity", "shifts")


def hidden_order(a, axis):
    a = np.moveaxis(a, axis, 0)
    rest = a.shape[1:]
    pairs = a[:1280].reshape(5, 32, 2, 4, *rest).transpose(0, 2, 3, 1, *range(4, 4 + len(rest))).reshape(1280, *rest)
    last = a[1280:].reshape(16, 8, *rest).transpose(1, 0, *range(2, 2 + len(rest))).reshape(128, *rest)
    return np.moveaxis(np.concatenate([pairs, last]), 0, axis)


def lay_out(inputs):
    a = {k: np.asarray(v) for k, v in inputs.items()}
    ctx = a["ctx_2048"]
    keep = a["mask_BxS2_bk0"]
    ctx_t = ctx.transpose(0, 2, 1).reshape(B, KT, 128, M)
    tail = ctx_t[..., M - TAIL:].reshape(GROUPS, NB, KT, 128, TAIL).transpose(0, 3, 2, 1, 4).reshape(GROUPS, 128, KT, KC)
    gu = a["L0_ffn_gate_up_packed"].T
    gs = a["L0_ffn_gate_up_scales"]

    def interleave(w):
        both = [hidden_order(w[:, i * FF:(i + 1) * FF], 1).reshape(w.shape[0], FT, 1, 128) for i in range(2)]
        return np.concatenate(both, 2).reshape(w.shape[0], 2 * FF)

    p = np.arange(128)
    shifts = np.stack([12 - 4 * (p // 64), 4 - 4 * (p // 64), 12 - 4 * (p // 32), 16 * (p // 64), 12 - 4 * (p // 16 % 4)], 1)
    return {
        "x": a["x"], "ctx_tail": tail, "ctx_full": ctx_t, "mask": keep, "mask_tail": keep[:, M - TAIL:],
        "g_xattn": a["g_xattn"], "g_ffn": a["g_ffn"], "norm_w": a["L0_xattn_norm_w"].reshape(KT, 128).T,
        **{n: a[f"L0_xattn_{n}"].T for n in ("wq", "wk", "wv", "wo", "wg")},
        "gu_packed": interleave(gu), "gu_scales": interleave(gs),
        "dn_packed": a["L0_ffn_down_packed"].T, "dn_scales": a["L0_ffn_down_scales"],
        "identity": np.eye(128, dtype=np.float32), "shifts": shifts.astype(np.int32),
    }


def kernel(**inputs):
    import concourse.bacc as bacc
    from concourse.bass_utils import run_bass_kernel_spmd

    nc = bacc.Bacc("TRN2", target_bir_lowering=False, num_devices=1)
    arrays, args = {}, []
    laid = lay_out(inputs)
    for name in INPUTS:
        a = np.ascontiguousarray(laid[name])
        arrays[f"in_{name}"] = a
        args.append(nc.dram_tensor(f"in_{name}", a.shape, mybir.dt.from_np(a.dtype), kind="ExternalInput").ap())
    args.append(nc.dram_tensor("x1_scratch", (B, L, D), F32, kind="Internal").ap())
    args.append(nc.dram_tensor("out_x", (B, L, D), F32, kind="ExternalOutput").ap())
    build(nc, *args)
    r = run_bass_kernel_spmd(nc, [arrays], core_ids=[0])
    return r.results[0]["out_x"]
```
